# Optimizing a Trainium2 kernel written in Bass

```python
import numpy as np
import jax
import jax.numpy as jnp

def _softmax(x, axis=-1):
    return jax.nn.softmax(x, axis=axis)

def _gelu(x):
    return jax.nn.gelu(x, approximate=True)

def _silu(x):
    return jax.nn.silu(x)

def _sigmoid(x):
    return jax.nn.sigmoid(x)

def _layernorm(x, axis=-1, eps=1e-05):
    m = jnp.mean(x, axis=axis, keepdims=True)
    v = jnp.var(x, axis=axis, keepdims=True)
    return (x - m) / jnp.sqrt(v + eps)

def _scatter_add(tgt, idx, src, axis=0):
    return tgt.at[idx].add(src)

def _segment_sum(src, seg, n):
    return jax.ops.segment_sum(src, seg, n)
kernel_name = 'mk_gnn_ffn_d2_gnn_r8_48245f'

def setup_inputs(seed: int=0):
    np.random.seed(seed)
    _w = jnp.asarray

    def _rec_inputs():
        import jax
        import jax.numpy as jnp
        _gk = jax.random.key(seed)
        x = -6.415e-05 + 1 * jax.random.normal(jax.random.fold_in(_gk, 1), (1250, 512), jnp.float32)
        src = jax.random.randint(jax.random.fold_in(_gk, 2), (20000,), 0, 1250, jnp.int32)
        dst = jax.random.randint(jax.random.fold_in(_gk, 3), (20000,), 0, 1250, jnp.int32)
        _o = jnp.argsort(dst, stable=True)
        src = src[_o]
        dst = dst[_o]
        edge_attr_4 = 0.00171547 + 0.999346 * jax.random.normal(jax.random.fold_in(_gk, 12), (20000, 4), jnp.float32)
        edge_attr_8 = 0.000126197 + 0.999763 * jax.random.normal(jax.random.fold_in(_gk, 13), (20000, 8), jnp.float32)
        return (x, src, dst, edge_attr_4, edge_attr_8)
    x, src, dst, edge_attr_4, edge_attr_8 = _rec_inputs()

    def _L0_gnn_setup():
        import jax, jax.numpy as jnp
        import numpy as np
        N, E, DM, H, DFF = (2500, 80000, 512, 8, 256)
        DK = DM // H

        def _layernorm(x, g, b, eps=1e-05):
            mu = jnp.mean(x, axis=-1, keepdims=True)
            var = jnp.mean(jnp.square(x - mu), axis=-1, keepdims=True)
            return (x - mu) * jax.lax.rsqrt(var + eps) * g + b
        key = jax.random.key(seed)
        ks = jax.random.split(key, 12)
        s = 0.02
        h = jax.random.normal(ks[0], (N, DM), dtype=jnp.float32)
        src = jax.random.randint(ks[1], (E,), 0, N, dtype=jnp.int32)
        dst = jnp.sort(jax.random.randint(ks[2], (E,), 0, N, dtype=jnp.int32))
        return {'h': h, 'src': src, 'dst': dst, 'Wq': jax.random.normal(ks[3], (DM, DM), dtype=jnp.float32) * s, 'Wk': jax.random.normal(ks[4], (DM, DM), dtype=jnp.float32) * s, 'Wv': jax.random.normal(ks[5], (DM, DM), dtype=jnp.float32) * s, 'Wo': jax.random.normal(ks[6], (DM, DM), dtype=jnp.float32) * s, 'ln1_g': jnp.ones((DM,), jnp.float32), 'ln1_b': jnp.zeros((DM,), jnp.float32), 'ln2_g': jnp.ones((DM,), jnp.float32), 'ln2_b': jnp.zeros((DM,), jnp.float32), 'W1': jax.random.normal(ks[7], (DM, DFF), dtype=jnp.float32) * s, 'b1': jnp.zeros((DFF,), jnp.float32), 'W2': jax.random.normal(ks[8], (DFF, DM), dtype=jnp.float32) * s, 'b2': jnp.zeros((DM,), jnp.float32)}
    _L0_gnn_all = _L0_gnn_setup()
    _L0_gnn_in = {k: v for k, v in _L0_gnn_all.items() if k in ('Wq', 'Wk', 'Wv', 'Wo', 'ln1_g', 'ln1_b', 'ln2_g', 'ln2_b', 'W1', 'b1', 'W2', 'b2')}
    del _L0_gnn_all

    def _L0_ffn_setup():
        import jax, jax.numpy as jnp
        import numpy as np
        DIM = 512
        NE = 8
        TOPK = 2
        CF = 1.2
        HID = 4 * DIM
        B, S = (8, 512)
        key = jax.random.key(seed)
        ks = jax.random.split(key, 4)
        s = 0.02
        return {'x': jax.random.normal(ks[0], (B, S, DIM), jnp.float32), 'gate_w': jax.random.normal(ks[1], (NE, DIM), jnp.float32) * s, 'gate_b': jnp.zeros((NE,), jnp.float32), 'w1': jax.random.normal(ks[2], (NE, DIM, HID), jnp.float32) * s, 'b1': jnp.zeros((NE, HID), jnp.float32), 'w2': jax.random.normal(ks[3], (NE, HID, DIM), jnp.float32) * s, 'b2': jnp.zeros((NE, DIM), jnp.float32)}
    _L0_ffn_all = _L0_ffn_setup()
    _L0_ffn_in = {k: v for k, v in _L0_ffn_all.items() if k in ('gate_w', 'gate_b', 'w1', 'b1', 'w2', 'b2')}
    del _L0_ffn_all

    def _L1_gnn_setup():
        import jax, jax.numpy as jnp
        import numpy as np
        MUL = 128
        N_NODES = 1250
        N_EDGES = 20000
        R_BASIS = 8
        HIDDEN = 64
        W_NUMEL = 4 * MUL
        SQRT3 = 3.0 ** 0.5
        SILU_2MOM = 1.679177
        AVG_NUM_NEIGHBORS = 10.0

        def _lin_irreps(x0, x1, W0, W1):
            y0 = x0 @ W0 / jnp.sqrt(jnp.float32(W0.shape[0]))
            y1 = jnp.einsum('num,uv->nvm', x1, W1) / jnp.sqrt(jnp.float32(W1.shape[0]))
            return (y0, y1)

        def _forward(node_feats, edge_attrs, edge_feats, edge_index, W_up0, W_up1, W_mlp1, W_mlp2, W_mlp3, W_mlp4, W_out0, W_out1):
            num_nodes = node_feats.shape[0]
            sender, receiver = (edge_index[0], edge_index[1])
            x0 = node_feats[:, :MUL]
            x1 = node_feats[:, MUL:].reshape(num_nodes, MUL, 3)
            x0, x1 = _lin_irreps(x0, x1, W_up0, W_up1)
            h = edge_feats
            for W in (W_mlp1, W_mlp2, W_mlp3):
                h = SILU_2MOM * jax.nn.silu(h @ W / jnp.sqrt(jnp.float32(W.shape[0])))
            tpw = h @ W_mlp4 / jnp.sqrt(jnp.float32(W_mlp4.shape[0]))
            w1, w2, w3, w4 = jnp.split(tpw, 4, axis=-1)
            s0 = x0[sender]
            s1 = x1[sender]
            y0 = edge_attrs[:, 0:1]
            y1 = edge_attrs[:, 1:4]
            p1 = w1 * s0 * y0
            p2 = (w2 * s0)[:, :, None] * y1[:, None, :]
            p3 = w3[:, :, None] * s1 * y0[:, None, :]
            p4 = w4 * jnp.einsum('eum,em->eu', s1, y1) / SQRT3
            m0 = jnp.concatenate([p1, p4], axis=-1)
            m1 = jnp.concatenate([p2, p3], axis=1)
            msg0 = jax.ops.segment_sum(m0, receiver, num_segments=num_nodes)
            msg1 = jax.ops.segment_sum(m1, receiver, num_segments=num_nodes)
            o0, o1 = _lin_irreps(msg0, msg1, W_out0, W_out1)
            out = jnp.concatenate([o0, o1.reshape(num_nodes, 3 * MUL)], axis=-1)
            return out / AVG_NUM_NEIGHBORS
        key = jax.random.key(seed)
        ks = jax.random.split(key, 12)
        rn = lambda k, s: jax.random.normal(k, s, dtype=jnp.float32)
        return {'node_feats': rn(ks[0], (N_NODES, 4 * MUL)), 'edge_attrs': rn(ks[1], (N_EDGES, 4)), 'edge_feats': rn(ks[2], (N_EDGES, R_BASIS)), 'edge_index': jax.random.randint(ks[3], (2, N_EDGES), 0, N_NODES), 'W_up0': rn(ks[4], (MUL, MUL)), 'W_up1': rn(ks[5], (MUL, MUL)), 'W_mlp1': rn(ks[6], (R_BASIS, HIDDEN)), 'W_mlp2': rn(ks[7], (HIDDEN, HIDDEN)), 'W_mlp3': rn(ks[8], (HIDDEN, HIDDEN)), 'W_mlp4': rn(ks[9], (HIDDEN, W_NUMEL)), 'W_out0': rn(ks[10], (2 * MUL, MUL)), 'W_out1': rn(ks[11], (2 * MUL, MUL))}
    _L1_gnn_all = _L1_gnn_setup()
    _L1_gnn_in = {k: v for k, v in _L1_gnn_all.items() if k in ('W_up0', 'W_up1', 'W_mlp1', 'W_mlp2', 'W_mlp3', 'W_mlp4', 'W_out0', 'W_out1')}
    del _L1_gnn_all

    def _L1_ffn_setup():
        import math
        import jax, jax.numpy as jnp
        import numpy as np
        B, T, D, FF, E = (32, 1024, 512, 256, 8)
        CAPACITY_FACTOR = 1.25
        CAP = int(math.ceil(CAPACITY_FACTOR * B * T / E))

        def _bank_residual(x2, Wr, br, W1, b1, W2, b2):
            N, d = x2.shape
            e = Wr.shape[1]
            logits = x2 @ Wr + br
            probs = jax.nn.softmax(logits, axis=-1)
            expert = jnp.argmax(probs, axis=-1)
            gate = jnp.take_along_axis(probs, expert[:, None], axis=-1)[:, 0]
            oneh = jax.nn.one_hot(expert, e, dtype=x2.dtype)
            pos = (jnp.cumsum(oneh, axis=0) * oneh).sum(-1).astype(jnp.int32) - 1
            keep = pos < CAP
            slot = expert.astype(jnp.int32) * CAP + jnp.minimum(pos, CAP - 1)
            xd = jnp.where(keep[:, None], x2, 0.0)
            buf = jnp.zeros((e * CAP, d), x2.dtype).at[slot].add(xd)
            buf = buf.reshape(e, CAP, d)
            h = jax.nn.gelu(jnp.einsum('ecd,edf->ecf', buf, W1) + b1[:, None, :], approximate=False)
            out = jnp.einsum('ecf,efd->ecd', h, W2) + b2[:, None, :]
            y = out.reshape(e * CAP, d)[slot]
            return y * (gate * keep.astype(x2.dtype))[:, None]
        key = jax.random.key(seed)
        ks = jax.random.split(key, 18)
        s = 0.02
        inp = {'x': jax.random.normal(ks[0], (B, T, D), dtype=jnp.float32), 'Wr_sp': jax.random.normal(ks[1], (D, E)) * s, 'br_sp': jnp.zeros((E,), jnp.float32), 'Wr_fq': jax.random.normal(ks[2], (D, E)) * s, 'br_fq': jnp.zeros((E,), jnp.float32), 'Ws1': jax.random.normal(ks[3], (D, FF)) * s, 'bs1': jnp.zeros((FF,), jnp.float32), 'Ws2': jax.random.normal(ks[4], (FF, D)) * s, 'bs2': jnp.zeros((D,), jnp.float32), 'W1_sp': jax.random.normal(ks[5], (E, D, FF)) * s, 'b1_sp': jnp.zeros((E, FF), jnp.float32), 'W2_sp': jax.random.normal(ks[6], (E, FF, D)) * s, 'b2_sp': jnp.zeros((E, D), jnp.float32), 'W1_fq': jax.random.normal(ks[7], (E, D, FF)) * s, 'b1_fq': jnp.zeros((E, FF), jnp.float32), 'W2_fq': jax.random.normal(ks[8], (E, FF, D)) * s, 'b2_fq': jnp.zeros((E, D), jnp.float32)}
        return inp
    _L1_ffn_all = _L1_ffn_setup()
    _L1_ffn_in = {k: v for k, v in _L1_ffn_all.items() if k in ('Wr_sp', 'br_sp', 'Wr_fq', 'br_fq', 'Ws1', 'bs1', 'Ws2', 'bs2', 'W1_sp', 'b1_sp', 'W2_sp', 'b2_sp', 'W1_fq', 'b1_fq', 'W2_fq', 'b2_fq')}
    del _L1_ffn_all
    return {'x': x, 'src': src, 'dst': dst, 'edge_attr_4': edge_attr_4, 'edge_attr_8': edge_attr_8, 'L0_gnn_Wq': _L0_gnn_in['Wq'], 'L0_gnn_Wk': _L0_gnn_in['Wk'], 'L0_gnn_Wv': _L0_gnn_in['Wv'], 'L0_gnn_Wo': _L0_gnn_in['Wo'], 'L0_gnn_ln1_g': _L0_gnn_in['ln1_g'], 'L0_gnn_ln1_b': _L0_gnn_in['ln1_b'], 'L0_gnn_ln2_g': _L0_gnn_in['ln2_g'], 'L0_gnn_ln2_b': _L0_gnn_in['ln2_b'], 'L0_gnn_W1': _L0_gnn_in['W1'], 'L0_gnn_b1': _L0_gnn_in['b1'], 'L0_gnn_W2': _L0_gnn_in['W2'], 'L0_gnn_b2': _L0_gnn_in['b2'], 'L0_ffn_gate_w': _L0_ffn_in['gate_w'], 'L0_ffn_gate_b': _L0_ffn_in['gate_b'], 'L0_ffn_w1': _L0_ffn_in['w1'], 'L0_ffn_b1': _L0_ffn_in['b1'], 'L0_ffn_w2': _L0_ffn_in['w2'], 'L0_ffn_b2': _L0_ffn_in['b2'], 'L1_gnn_W_up0': _L1_gnn_in['W_up0'], 'L1_gnn_W_up1': _L1_gnn_in['W_up1'], 'L1_gnn_W_mlp1': _L1_gnn_in['W_mlp1'], 'L1_gnn_W_mlp2': _L1_gnn_in['W_mlp2'], 'L1_gnn_W_mlp3': _L1_gnn_in['W_mlp3'], 'L1_gnn_W_mlp4': _L1_gnn_in['W_mlp4'], 'L1_gnn_W_out0': _L1_gnn_in['W_out0'], 'L1_gnn_W_out1': _L1_gnn_in['W_out1'], 'L1_ffn_Wr_sp': _L1_ffn_in['Wr_sp'], 'L1_ffn_br_sp': _L1_ffn_in['br_sp'], 'L1_ffn_Wr_fq': _L1_ffn_in['Wr_fq'], 'L1_ffn_br_fq': _L1_ffn_in['br_fq'], 'L1_ffn_Ws1': _L1_ffn_in['Ws1'], 'L1_ffn_bs1': _L1_ffn_in['bs1'], 'L1_ffn_Ws2': _L1_ffn_in['Ws2'], 'L1_ffn_bs2': _L1_ffn_in['bs2'], 'L1_ffn_W1_sp': _L1_ffn_in['W1_sp'], 'L1_ffn_b1_sp': _L1_ffn_in['b1_sp'], 'L1_ffn_W2_sp': _L1_ffn_in['W2_sp'], 'L1_ffn_b2_sp': _L1_ffn_in['b2_sp'], 'L1_ffn_W1_fq': _L1_ffn_in['W1_fq'], 'L1_ffn_b1_fq': _L1_ffn_in['b1_fq'], 'L1_ffn_W2_fq': _L1_ffn_in['W2_fq'], 'L1_ffn_b2_fq': _L1_ffn_in['b2_fq']}

def reference(x, src, dst, edge_attr_4, edge_attr_8, L0_gnn_Wq, L0_gnn_Wk, L0_gnn_Wv, L0_gnn_Wo, L0_gnn_ln1_g, L0_gnn_ln1_b, L0_gnn_ln2_g, L0_gnn_ln2_b, L0_gnn_W1, L0_gnn_b1, L0_gnn_W2, L0_gnn_b2, L0_ffn_gate_w, L0_ffn_gate_b, L0_ffn_w1, L0_ffn_b1, L0_ffn_w2, L0_ffn_b2, L1_gnn_W_up0, L1_gnn_W_up1, L1_gnn_W_mlp1, L1_gnn_W_mlp2, L1_gnn_W_mlp3, L1_gnn_W_mlp4, L1_gnn_W_out0, L1_gnn_W_out1, L1_ffn_Wr_sp, L1_ffn_br_sp, L1_ffn_Wr_fq, L1_ffn_br_fq, L1_ffn_Ws1, L1_ffn_bs1, L1_ffn_Ws2, L1_ffn_bs2, L1_ffn_W1_sp, L1_ffn_b1_sp, L1_ffn_W2_sp, L1_ffn_b2_sp, L1_ffn_W1_fq, L1_ffn_b1_fq, L1_ffn_W2_fq, L1_ffn_b2_fq):
    import jax
    import jax.numpy as jnp

    def _L0_gnn_ref(h, src, dst, Wq, Wk, Wv, Wo, ln1_g, ln1_b, ln2_g, ln2_b, W1, b1, W2, b2):
        import jax, jax.numpy as jnp
        import numpy as np
        N, E, DM, H, DFF = (2500, 80000, 512, 8, 256)
        DK = DM // H

        def _layernorm(x, g, b, eps=1e-05):
            mu = jnp.mean(x, axis=-1, keepdims=True)
            var = jnp.mean(jnp.square(x - mu), axis=-1, keepdims=True)
            return (x - mu) * jax.lax.rsqrt(var + eps) * g + b
        n = h.shape[0]
        q = (h @ Wq).reshape(n, H, DK)
        k = (h @ Wk).reshape(n, H, DK)
        v = (h @ Wv).reshape(n, H, DK)
        e = jnp.einsum('ehd,ehd->eh', k[src], q[dst]) / np.sqrt(DK).astype(np.float32)
        m = jax.ops.segment_max(e, dst, num_segments=n)
        ex = jnp.exp(e - m[dst])
        z = jax.ops.segment_sum(ex, dst, num_segments=n)
        attn = ex / z[dst]
        a = jax.ops.segment_sum(attn[:, :, None] * v[src], dst, num_segments=n)
        a = a.reshape(n, DM)
        o = a @ Wo
        x = _layernorm(h + o, ln1_g, ln1_b)
        f = jax.nn.relu(x @ W1 + b1) @ W2 + b2
        return _layernorm(x + f, ln2_g, ln2_b)

    def _L0_ffn_ref(x, gate_w, gate_b, w1, b1, w2, b2):
        import jax, jax.numpy as jnp
        import numpy as np
        DIM = 512
        NE = 8
        TOPK = 2
        CF = 1.2
        HID = 4 * DIM
        B, S = (8, 512)
        Bq, Sq, D = x.shape
        T = Bq * Sq
        cap = int(CF * T / NE)
        xf = x.reshape(T, D)
        probs = jax.nn.softmax(xf @ gate_w.T + gate_b, axis=-1)
        topw, topi = jax.lax.top_k(probs, TOPK)
        onehot = jax.nn.one_hot(topi, NE, dtype=topw.dtype)
        w_te = jnp.einsum('tk,tke->te', topw, onehot)
        routed = onehot.sum(axis=1) > 0
        wm = jnp.where(routed, w_te, -1.0)
        sel_w, sel_idx = jax.lax.top_k(wm.T, cap)
        sel_w = jnp.maximum(sel_w, 0.0)
        xg = xf[sel_idx]
        h = jax.nn.gelu(jnp.einsum('ecd,edh->ech', xg, w1) + b1[:, None, :], approximate=False)
        out = jnp.einsum('ech,ehd->ecd', h, w2) + b2[:, None, :]
        weighted = out * sel_w[..., None]
        of = jnp.zeros((T, D), x.dtype).at[sel_idx.reshape(-1)].add(weighted.reshape(-1, D))
        return of.reshape(Bq, Sq, D)

    def _L1_gnn_ref(node_feats, edge_attrs, edge_feats, edge_index, W_up0, W_up1, W_mlp1, W_mlp2, W_mlp3, W_mlp4, W_out0, W_out1):
        import jax, jax.numpy as jnp
        import numpy as np
        MUL = 128
        N_NODES = 1250
        N_EDGES = 20000
        R_BASIS = 8
        HIDDEN = 64
        W_NUMEL = 4 * MUL
        SQRT3 = 3.0 ** 0.5
        SILU_2MOM = 1.679177
        AVG_NUM_NEIGHBORS = 10.0

        def _lin_irreps(x0, x1, W0, W1):
            y0 = x0 @ W0 / jnp.sqrt(jnp.float32(W0.shape[0]))
            y1 = jnp.einsum('num,uv->nvm', x1, W1) / jnp.sqrt(jnp.float32(W1.shape[0]))
            return (y0, y1)

        def _forward(node_feats, edge_attrs, edge_feats, edge_index, W_up0, W_up1, W_mlp1, W_mlp2, W_mlp3, W_mlp4, W_out0, W_out1):
            num_nodes = node_feats.shape[0]
            sender, receiver = (edge_index[0], edge_index[1])
            x0 = node_feats[:, :MUL]
            x1 = node_feats[:, MUL:].reshape(num_nodes, MUL, 3)
            x0, x1 = _lin_irreps(x0, x1, W_up0, W_up1)
            h = edge_feats
            for W in (W_mlp1, W_mlp2, W_mlp3):
                h = SILU_2MOM * jax.nn.silu(h @ W / jnp.sqrt(jnp.float32(W.shape[0])))
            tpw = h @ W_mlp4 / jnp.sqrt(jnp.float32(W_mlp4.shape[0]))
            w1, w2, w3, w4 = jnp.split(tpw, 4, axis=-1)
            s0 = x0[sender]
            s1 = x1[sender]
            y0 = edge_attrs[:, 0:1]
            y1 = edge_attrs[:, 1:4]
            p1 = w1 * s0 * y0
            p2 = (w2 * s0)[:, :, None] * y1[:, None, :]
            p3 = w3[:, :, None] * s1 * y0[:, None, :]
            p4 = w4 * jnp.einsum('eum,em->eu', s1, y1) / SQRT3
            m0 = jnp.concatenate([p1, p4], axis=-1)
            m1 = jnp.concatenate([p2, p3], axis=1)
            msg0 = jax.ops.segment_sum(m0, receiver, num_segments=num_nodes)
            msg1 = jax.ops.segment_sum(m1, receiver, num_segments=num_nodes)
            o0, o1 = _lin_irreps(msg0, msg1, W_out0, W_out1)
            out = jnp.concatenate([o0, o1.reshape(num_nodes, 3 * MUL)], axis=-1)
            return out / AVG_NUM_NEIGHBORS
        return _forward(node_feats, edge_attrs, edge_feats, edge_index, W_up0, W_up1, W_mlp1, W_mlp2, W_mlp3, W_mlp4, W_out0, W_out1)

    def _L1_ffn_ref(x, Wr_sp, br_sp, Wr_fq, br_fq, Ws1, bs1, Ws2, bs2, W1_sp, b1_sp, W2_sp, b2_sp, W1_fq, b1_fq, W2_fq, b2_fq):
        import math
        import jax, jax.numpy as jnp
        import numpy as np
        B, T, D, FF, E = (32, 1024, 512, 256, 8)
        CAPACITY_FACTOR = 1.25
        CAP = int(math.ceil(CAPACITY_FACTOR * B * T / E))

        def _bank_residual(x2, Wr, br, W1, b1, W2, b2):
            N, d = x2.shape
            e = Wr.shape[1]
            logits = x2 @ Wr + br
            probs = jax.nn.softmax(logits, axis=-1)
            expert = jnp.argmax(probs, axis=-1)
            gate = jnp.take_along_axis(probs, expert[:, None], axis=-1)[:, 0]
            oneh = jax.nn.one_hot(expert, e, dtype=x2.dtype)
            pos = (jnp.cumsum(oneh, axis=0) * oneh).sum(-1).astype(jnp.int32) - 1
            keep = pos < CAP
            slot = expert.astype(jnp.int32) * CAP + jnp.minimum(pos, CAP - 1)
            xd = jnp.where(keep[:, None], x2, 0.0)
            buf = jnp.zeros((e * CAP, d), x2.dtype).at[slot].add(xd)
            buf = buf.reshape(e, CAP, d)
            h = jax.nn.gelu(jnp.einsum('ecd,edf->ecf', buf, W1) + b1[:, None, :], approximate=False)
            out = jnp.einsum('ecf,efd->ecd', h, W2) + b2[:, None, :]
            y = out.reshape(e * CAP, d)[slot]
            return y * (gate * keep.astype(x2.dtype))[:, None]
        b, t, d = x.shape
        x2 = x.reshape(b * t, d)
        shared = jax.nn.gelu(x2 @ Ws1 + bs1, approximate=False) @ Ws2 + bs2
        y = shared
        y = y + _bank_residual(x2, Wr_sp, br_sp, W1_sp, b1_sp, W2_sp, b2_sp)
        y = y + _bank_residual(x2, Wr_fq, br_fq, W1_fq, b1_fq, W2_fq, b2_fq)
        return y.reshape(b, t, d)
    edge_index = jnp.stack([src, dst])
    x = x + _L0_gnn_ref(_layernorm(x, axis=-1), src, dst, L0_gnn_Wq, L0_gnn_Wk, L0_gnn_Wv, L0_gnn_Wo, L0_gnn_ln1_g, L0_gnn_ln1_b, L0_gnn_ln2_g, L0_gnn_ln2_b, L0_gnn_W1, L0_gnn_b1, L0_gnn_W2, L0_gnn_b2)
    x = x + _L0_ffn_ref(_layernorm(x, axis=-1)[None], L0_ffn_gate_w, L0_ffn_gate_b, L0_ffn_w1, L0_ffn_b1, L0_ffn_w2, L0_ffn_b2)[0]
    x = x + _L1_gnn_ref(_layernorm(x, axis=-1), edge_attr_4, edge_attr_8, edge_index, L1_gnn_W_up0, L1_gnn_W_up1, L1_gnn_W_mlp1, L1_gnn_W_mlp2, L1_gnn_W_mlp3, L1_gnn_W_mlp4, L1_gnn_W_out0, L1_gnn_W_out1)
    x = x + _L1_ffn_ref(_layernorm(x, axis=-1)[None], L1_ffn_Wr_sp, L1_ffn_br_sp, L1_ffn_Wr_fq, L1_ffn_br_fq, L1_ffn_Ws1, L1_ffn_bs1, L1_ffn_Ws2, L1_ffn_bs2, L1_ffn_W1_sp, L1_ffn_b1_sp, L1_ffn_W2_sp, L1_ffn_b2_sp, L1_ffn_W1_fq, L1_ffn_b1_fq, L1_ffn_W2_fq, L1_ffn_b2_fq)[0]
    return x

_drawn_inputs = setup_inputs


def setup_inputs(seed=0):
    import zlib

    import numpy as np

    out = dict(_drawn_inputs(seed))
    spreads = {'L0_gnn_ln1_g': (1.0, 0.2),
     'L0_gnn_ln1_b': (0.0, 0.1),
     'L0_gnn_ln2_g': (1.0, 0.2),
     'L0_gnn_ln2_b': (0.0, 0.1),
     'L0_gnn_b1': (0.0, 0.725),
     'L0_gnn_b2': (0.0, 0.1),
     'L0_ffn_gate_b': (0.0, 0.8),
     'L0_ffn_b1': (0.0, 0.8),
     'L0_ffn_b2': (0.0, 0.603),
     'L1_ffn_br_sp': (0.0, 0.8),
     'L1_ffn_br_fq': (0.0, 0.8),
     'L1_ffn_bs1': (0.0, 0.8),
     'L1_ffn_bs2': (0.0, 0.34),
     'L1_ffn_b1_sp': (0.0, 0.8),
     'L1_ffn_b2_sp': (0.0, 0.708),
     'L1_ffn_b1_fq': (0.0, 0.8),
     'L1_ffn_b2_fq': (0.0, 0.681)}
    factors = {'L0_gnn_Wq': 8.0,
     'L0_gnn_Wk': 8.0,
     'L1_ffn_Wr_sp': 4.087,
     'L1_ffn_Wr_fq': 4.097,
     'L1_ffn_W1_sp': 6.384,
     'L1_ffn_W2_sp': 5.94,
     'L1_ffn_W1_fq': 6.252,
     'L1_ffn_W2_fq': 5.881}
    for name, (base, spread) in spreads.items():
        noise = np.random.default_rng([zlib.crc32(name.encode()), seed]).standard_normal(out[name].shape)
        drawn = base * np.exp(spread * noise) if base else spread * noise
        out[name] = jnp.asarray(drawn.astype(out[name].dtype))
    for name, factor in factors.items():
        out[name] = (out[name] * factor).astype(out[name].dtype)
    return out
```

```python
import math
from contextlib import ExitStack

import concourse.bass as bass
from concourse import mybir

F32 = mybir.dt.float32
F16 = mybir.dt.float16
I32 = mybir.dt.int32
U32 = mybir.dt.uint32
ALU = mybir.AluOpType
ACT = mybir.ActivationFunctionType
X_AXIS = mybir.AxisListType.X

NODES, DIM, EDGES = 1250, 512, 20000
P = 125
TILES = NODES // P
KC = DIM // 128
HEADS, DK = 8, 64
ECOLS = EDGES // P
LANES, EPP = 128, 4
GROUP = LANES * EPP
GROUPS = (EDGES + TILES * (GROUP - 1)) // GROUP
GROUPS += GROUPS % 2
SLOTS = GROUPS * GROUP
REC = 16
NEG = -1e30
EPS = 1e-5
CHUNKS = [(0, 512), (512, 512), (1024, NODES - 1024)]
EXPERTS = 8
CAP0 = int(1.2 * NODES / EXPERTS)
ROWS0 = CAP0 + 1
HALF0 = ROWS0 // 2
HID0 = 2048
MC0 = HID0 // 128
FF1 = 256
TT1 = (NODES + EXPERTS * (LANES - 1)) // LANES
TT1 += TT1 % 2
ROWS1 = TT1 * LANES
BANKS = ("sp", "fq")
SILU_2MOM = 1.679177
MUL = 128


class Chain:

    def __init__(self, engine, done):
        self.engine, self.done, self.n = engine, done, 0

    def __call__(self, instruction):
        instruction.then_inc(self.done, 1)
        self.n += 1
        self.engine.wait_ge(self.done, self.n)


def gnn_moe_gnn_moe(nc, I, out):
    top = ExitStack()

    used = {}

    def fresh(name):
        used[name] = used.get(name, 0) + 1
        return name if used[name] == 1 else f"{name}_{used[name]}"

    def tile_in(stack):
        return lambda name, shape, dt=F32: stack.enter_context(nc.sbuf_tensor(fresh(name), shape, dt))

    def bank_in(stack):
        return lambda name, shape, dt=F32: stack.enter_context(nc.psum_tensor(fresh(name), shape, dt))

    finished = []

    def sems_in(stack):
        def allocate(*names):
            handles = [nc.alloc_semaphore(name=fresh(n)) for n in names]
            stack.callback(finished.extend, handles)
            return handles
        return allocate

    def recycle():
        nc.clear_and_free_semaphores(finished)
        finished.clear()
        nc.all_engine_barrier()

    def row(ap):
        return ap.rearrange("(a n) -> a n", a=1)

    def dram(name, shape, dt=F32):
        return nc.dram_tensor(name, shape, dt, kind="Internal").ap()

    rec_dram = dram("rec_dram", (SLOTS, REC))
    up_dram = dram("up_dram", (NODES, DIM))
    xin0 = dram("xin0", (EXPERTS * ROWS0 + 2 * NODES, DIM))
    yout0 = dram("yout0", (EXPERTS * ROWS0, DIM))
    xin1 = {b: dram("xin1_" + b, (ROWS1, DIM)) for b in BANKS}
    yout1 = {b: dram("yout1_" + b, (ROWS1, DIM)) for b in BANKS}

    with top:
        sb = tile_in(top)
        X = sb("X", [P, TILES, DIM])
        ident = sb("ident", [128, 128])
        ones = sb("ones", [128, 128])
        before = sb("before", [128, 128])
        earlier = sb("earlier", [128, 128])
        zeros = sb("zeros", [128, DIM])
        count = sb("count", [128, 64])
        tiny = sb("tiny", [128, 1])
        blockI = sb("blockI", [P, GROUPS], I32)

        def order_edges(pos, recs):
            with ExitStack() as st:
                sb, pb = tile_in(st), bank_in(st)
                loaded, consts, routed, rows_ready, totals, filled, fill_ready = sems_in(st)(
                    "edges_loaded", "consts_ready", "routed", "rows_ready", "totals_ready", "rec_filled", "fill_ready")
                srcI, dstI = sb("srcI", [P, ECOLS], I32), sb("dstI", [P, ECOLS], I32)
                a4, a8 = sb("a4", [P, ECOLS, 4]), sb("a8", [P, ECOLS, 8])
                dstF = sb("dstF", [P, ECOLS])
                ge = sb("ge", [P, TILES + 1, ECOLS])
                oh = sb("oh", [P, TILES, ECOLS])
                cum = sb("cum", [P, TILES, ECOLS])
                blk = sb("blk", [P, ECOLS])
                onesE = sb("onesE", [P, ECOLS])
                base, grp, gI, start = (sb("base", [P, TILES]), sb("grp", [P, TILES]),
                                        sb("gI", [P, TILES], I32), sb("start", [P, TILES]))
                rows = sb("rows", [P, TILES])
                posF = sb("posF", [P, ECOLS])
                bf = sb("bf", [P, GROUPS])
                fill = sb("fill", [128, SLOTS // 128, REC])
                ps = pb("ps", [128, 2, 512])
                with nc.Block() as block:
                    @block.sync
                    def _(sp):
                        sp.dma_start(srcI[:], I["src"].rearrange("(p c) -> p c", p=P)).then_inc(loaded, 16)
                        sp.dma_start(dstI[:], I["dst"].rearrange("(p c) -> p c", p=P)).then_inc(loaded, 16)
                        sp.dma_start(a4[:], I["edge_attr_4"].rearrange("(p c) f -> p c f", p=P)).then_inc(loaded, 16)
                        sp.dma_start(a8[:], I["edge_attr_8"].rearrange("(p c) f -> p c f", p=P)).then_inc(loaded, 16)
                        sp.dma_start(X[:], I["x"].rearrange("(t p) d -> p t d", p=P)).then_inc(loaded, 16)
                        sp.wait_ge(fill_ready, 1)
                        sp.dma_start(rec_dram.rearrange("(p c) w -> p c w", p=128), fill[:]).then_inc(filled, 16)
                        sp.wait_ge(loaded, 80)
                        sp.wait_ge(filled, 16)

                    @block.gpsimd
                    def _(pool):
                        nc.gpsimd.memset(ident[:], 0.0)
                        nc.gpsimd.memset(before[:], 0.0)
                        nc.gpsimd.memset(earlier[:], 0.0)
                        nc.gpsimd.memset(ones[:], 1.0)
                        nc.gpsimd.memset(zeros[:], 0.0)
                        nc.gpsimd.memset(tiny[:], EPS)
                        nc.gpsimd.memset(onesE[:], 1.0)
                        nc.gpsimd.iota(count[:], pattern=[[1, 64]], base=0, channel_multiplier=0,
                                       allow_small_or_imprecise_dtypes=True).then_inc(consts, 1)
                        pool.wait_ge(consts, 1)
                        nc.gpsimd.affine_select(out=ident[:], in_=ident[:], compare_op=ALU.not_equal, fill=1.0,
                                                base=0, pattern=[[-1, 128]], channel_multiplier=1)
                        nc.gpsimd.affine_select(out=before[:], in_=before[:], compare_op=ALU.is_ge, fill=1.0,
                                                base=0, pattern=[[-1, 128]], channel_multiplier=1)
                        nc.gpsimd.affine_select(out=earlier[:], in_=earlier[:], compare_op=ALU.is_ge, fill=1.0,
                                                base=0, pattern=[[1, 128]], channel_multiplier=-1).then_inc(consts, 1)

                    @block.vector
                    def _(dve):
                        step = Chain(dve, routed)
                        step(nc.vector.memset(fill[:], 0.0))
                        nc.vector.memset(fill[:, :, 1:2], -1.0).then_inc(fill_ready, 1)
                        dve.wait_ge(loaded, 80)
                        step(nc.vector.tensor_copy(dstF[:], dstI[:]))
                        step(nc.vector.tensor_copy(recs[:, :, 0], srcI[:]))
                        for b in range(TILES):
                            nc.vector.tensor_scalar(ge[:, b, :], dstF[:], float(P * b), None, ALU.is_ge)
                        nc.vector.tensor_copy(recs[:, :, 4:8], a4[:])
                        nc.vector.tensor_copy(recs[:, :, 8:16], a8[:])
                        nc.vector.memset(recs[:, :, 2:4], 0.0)
                        step(nc.vector.memset(ge[:, TILES, :], 0.0))
                        step(nc.vector.tensor_tensor(oh[:], ge[:, 0:TILES, :], ge[:, 1:TILES + 1, :], ALU.subtract))
                        step(nc.vector.tensor_reduce(blk[:], ge[:, 1:TILES, :].rearrange("p b c -> p c b"), X_AXIS, ALU.add))
                        step(nc.vector.scalar_tensor_tensor(out=recs[:, :, 1], in0=blk[:], scalar=-float(P), in1=dstF[:],
                                                            op0=ALU.mult, op1=ALU.add))
                        dve.wait_ge(consts, 2)
                        for b in range(TILES):
                            scan = nc.vector.tensor_tensor_scan(cum[:, b, :], onesE[:], oh[:, b, :], 0.0, ALU.mult, ALU.add)
                        step(scan)
                        nc.vector.tensor_copy(rows[:], cum[:, :, ECOLS - 1]).then_inc(rows_ready, 1)
                        dve.wait_ge(totals, 1)
                        step(nc.vector.tensor_scalar(gI[:], ps[:P, 1, 0:TILES], float(GROUP - 1), None, ALU.add))
                        step(nc.vector.tensor_scalar(gI[:], gI[:], int(math.log2(GROUP)), None, ALU.arith_shift_right))
                        step(nc.vector.tensor_copy(grp[:], gI[:]))
                        step(nc.vector.tensor_tensor_scan(start[:], onesE[:, 0:TILES], grp[:], 0.0, ALU.mult, ALU.add))
                        step(nc.vector.tensor_tensor(start[:], start[:], grp[:], ALU.subtract))
                        step(nc.vector.scalar_tensor_tensor(out=base[:], in0=start[:], scalar=float(GROUP),
                                                            in1=ps[:P, 0, 0:TILES], op0=ALU.mult, op1=ALU.add))
                        for b in range(TILES):
                            nc.vector.scalar_tensor_tensor(out=ge[:, b, :], in0=cum[:, b, :], scalar=base[:, b:b + 1],
                                                           in1=oh[:, b, :], op0=ALU.add, op1=ALU.mult)
                        step(nc.vector.tensor_scalar(bf[:], count[:P, 0:GROUPS], start[:, 1:2], None, ALU.is_ge))
                        step(nc.vector.tensor_reduce(posF[:], ge[:, 0:TILES, :].rearrange("p b c -> p c b"), X_AXIS, ALU.add))
                        step(nc.vector.tensor_scalar(pos[:], posF[:], -1.0, None, ALU.add))
                        for b in range(2, TILES):
                            step(nc.vector.scalar_tensor_tensor(out=bf[:], in0=count[:P, 0:GROUPS], scalar=start[:, b:b + 1],
                                                                in1=bf[:], op0=ALU.is_ge, op1=ALU.add))
                        step(nc.vector.tensor_copy(blockI[:], bf[:]))

                    @block.tensor
                    def _(pe):
                        pe.wait_ge(consts, 2)
                        pe.wait_ge(rows_ready, 1)
                        nc.tensor.matmul(ps[:P, 0, 0:TILES], before[:P, :P], rows[:], start=True, stop=True)
                        nc.tensor.matmul(ps[:P, 1, 0:TILES], ones[:P, :P], rows[:], start=True, stop=True).then_inc(totals, 1)

        def layer_norm(src, dst, gain=None, shift=None, add_to=None):
            with ExitStack() as st:
                sb = tile_in(st)
                stats_done, root_done, steps, params = sems_in(st)("ln_stats", "ln_root", "ln_steps", "ln_params")
                stats = sb("stats", [P, TILES, 6])
                mv = sb("mv", [P, TILES, 2])
                root, rstd = sb("root", [P, TILES]), sb("rstd", [P, TILES])
                if gain is not None:
                    gainB, shiftB = sb("gainB", [P, DIM]), sb("shiftB", [P, DIM])
                with nc.Block() as block:
                    if gain is not None:
                        @block.sync
                        def _(sp):
                            sp.dma_start(gainB[:], row(gain).broadcast_to([P, DIM])).then_inc(params, 16)
                            sp.dma_start(shiftB[:], row(shift).broadcast_to([P, DIM])).then_inc(params, 16)

                    @block.vector
                    def _(dve):
                        step = Chain(dve, steps)
                        for t in range(TILES):
                            stat = nc.vector.bn_stats(stats[:, t, :], src[:, t, :])
                        step(stat)
                        for t in range(TILES):
                            aggr = nc.vector.bn_aggr(mv[:, t, :], stats[:, t, :])
                        aggr.then_inc(stats_done, 1)
                        dve.wait_ge(root_done, 1)
                        step(nc.vector.reciprocal(rstd[:], root[:]))
                        if gain is not None:
                            dve.wait_ge(params, 32)
                        for t in range(TILES):
                            last = nc.vector.tensor_scalar(dst[:, t, :], src[:, t, :], mv[:, t, 0:1], rstd[:, t:t + 1],
                                                           ALU.subtract, ALU.mult)
                        step(last)
                        if gain is not None:
                            for t in range(TILES):
                                last = nc.vector.tensor_tensor(dst[:, t, :], dst[:, t, :], gainB[:], ALU.mult)
                            step(last)
                            for t in range(TILES):
                                last = nc.vector.tensor_tensor(dst[:, t, :], dst[:, t, :], shiftB[:], ALU.add)
                            step(last)
                        if add_to is not None:
                            for t in range(TILES):
                                last = nc.vector.tensor_tensor(add_to[:, t, :], dst[:, t, :], add_to[:, t, :], ALU.add)
                            step(last)

                    @block.scalar
                    def _(act):
                        act.wait_ge(stats_done, 1)
                        nc.scalar.activation(root[:], mv[:, :, 1], ACT.Sqrt, bias=tiny[:P, :]).then_inc(root_done, 1)

        def transpose_all(src, dst, chunks=None):
            chunks = chunks or [lambda t, k=k: src[:, t, 128 * k:128 * (k + 1)] for k in range(KC)]
            with ExitStack() as st:
                ps = bank_in(st)("ps", [128, 4, 512])
                turned, moved = sems_in(st)("turned", "moved")
                n = len(chunks)
                with nc.Block() as block:
                    @block.tensor
                    def _(pe):
                        for t in range(TILES):
                            if t >= 4:
                                pe.wait_ge(moved, t - 3)
                            for k in range(n):
                                last = nc.tensor.transpose(ps[:, t % 4, P * k:P * (k + 1)], chunks[k](t), ident[:P, :P])
                            last.then_inc(turned, 1)

                    @block.scalar
                    def _(act):
                        for t in range(TILES):
                            act.wait_ge(turned, t + 1)
                            nc.scalar.activation(dst[:, :, P * t:P * (t + 1)],
                                                 ps[:, t % 4, 0:n * P].rearrange("p (k c) -> p k c", k=n),
                                                 ACT.Copy).then_inc(moved, 1)

        def qkv_and_scatter(HT, QT, KT, V, pos, recs):
            with ExitStack() as st:
                sb, pb = tile_in(st), bank_in(st)
                wload, done, moved, staged, scattered, tick = sems_in(st)(
                    "w_loaded", "product_done", "product_moved", "rec_staged", "rec_scattered", "tick")
                W = [sb(f"Wqkv{i}", [128, KC, DIM]) for i in range(3)]
                pos8, rec8 = sb("pos8", [P, 8], I32), sb("rec8", [P, 8, REC])
                ps = pb("ps", [128, 8, 512])
                jobs = []
                for which in range(2):
                    for j in range(KC):
                        for c0, cn in CHUNKS:
                            jobs.append((which, j, c0, cn))
                for t in range(TILES):
                    jobs.append((2, t, 0, DIM))

                def target(job):
                    which, j, c0, cn = job
                    return V[:, j, :] if which == 2 else (QT, KT)[which][:, j, c0:c0 + cn]

                with nc.Block() as block:
                    @block.sync
                    def _(sp):
                        for i, name in enumerate(("L0_gnn_Wq", "L0_gnn_Wk", "L0_gnn_Wv")):
                            sp.dma_start(W[i][:], I[name].rearrange("(k p) n -> p k n", p=128)).then_inc(wload, 16)

                    @block.gpsimd
                    def _(pool):
                        with pool.Fori(0, ECOLS // 8) as c:
                            nc.gpsimd.tensor_copy(pos8[:], pos[:, bass.ds(c * 8, 8)]).then_inc(staged, 1)
                            nc.gpsimd.tensor_copy(rec8[:], recs[:, bass.ds(c * 8, 8), :]).then_inc(staged, 1)
                            pool.wait_ge(staged, 2 * (c + 1))
                            pool.sem_inc(tick, 1)
                            for k in range(8):
                                pool.indirect_dma_start(
                                    out=rec_dram, out_offset=bass.IndirectOffsetOnAxis(ap=pos8[:, k:k + 1], axis=0),
                                    in_=rec8[:, k, :], in_offset=None).then_inc(scattered, 16)
                            pool.wait_ge(scattered, 128 * (c + 1))
                            pool.sem_inc(tick, 1)

                    @block.tensor
                    def _(pe):
                        pe.wait_ge(wload, 48)
                        for n, (which, j, c0, cn) in enumerate(jobs):
                            if n >= 8:
                                pe.wait_ge(moved, n - 7)
                            for k in range(KC):
                                if which < 2:
                                    last = nc.tensor.matmul(ps[:, n % 8, 0:cn], W[which][:, k, 128 * j:128 * (j + 1)],
                                                            HT[:, k, c0:c0 + cn], start=k == 0, stop=k == KC - 1)
                                else:
                                    last = nc.tensor.matmul(ps[:P, n % 8, :], HT[:, k, P * j:P * (j + 1)],
                                                            W[2][:, k, :], start=k == 0, stop=k == KC - 1)
                            last.then_inc(done, 1)

                    @block.scalar
                    def _(act):
                        for n, job in enumerate(jobs):
                            act.wait_ge(done, n + 1)
                            parts = 128 if job[0] < 2 else P
                            scale = 1.0 / math.sqrt(DK) if job[0] == 0 else 1.0
                            nc.scalar.activation(target(job), ps[:parts, n % 8, 0:job[3]], ACT.Copy,
                                                 scale=scale).then_inc(moved, 1)

        def count_edges(LA, has, RECS):
            with ExitStack() as st:
                sb, pb = tile_in(st), bank_in(st)
                loaded, cols, hot, counted, added, cleared = sems_in(st)(
                    "recs_loaded", "cols_ready", "one_hots_ready", "counted", "counts_added", "cleared")
                nodes16 = sb("nodes16", [128, NODES], F16)
                ohS, ohD = sb("ohS", [128, 2, NODES], F16), sb("ohD", [128, 2, P], F16)
                ps = pb("ps", [128, 2, 2048])
                with nc.Block() as block:
                    @block.sync
                    def _(sp):
                        sp.dma_start(RECS[:, 0:GROUPS], rec_dram.rearrange("(g p t) w -> p g t w", p=128, t=EPP)).then_inc(loaded, 16)

                    @block.gpsimd
                    def _(pool):
                        nc.gpsimd.iota(nodes16[:], pattern=[[1, NODES]], base=0, channel_multiplier=0,
                                       allow_small_or_imprecise_dtypes=True).then_inc(cols, 1)
                        nc.gpsimd.memset(RECS[:, GROUPS, :, :], 0.0)
                        nc.gpsimd.memset(LA[:], 0.0).then_inc(cleared, 1)

                    @block.vector
                    def _(dve):
                        dve.wait_ge(cols, 1)
                        dve.wait_ge(loaded, 16)
                        dve.wait_ge(cleared, 1)
                        with dve.Fori(0, GROUPS) as g:
                            block_of = dve.value_load(blockI[0:1, bass.ds(g, 1)], min_val=0, max_val=TILES - 1)
                            for t in range(EPP):
                                dve.wait_ge(counted, EPP * g + t + 1)
                                nc.vector.tensor_scalar(ohS[:, t % 2, :], nodes16[:], RECS[:, bass.ds(g, 1), t, 0:1].rearrange("p a b -> p (a b)"),
                                                        None, ALU.is_equal)
                                nc.vector.tensor_scalar(ohD[:, t % 2, :], nodes16[:, 0:P], RECS[:, bass.ds(g, 1), t, 1:2].rearrange("p a b -> p (a b)"),
                                                        None, ALU.is_equal).then_inc(hot, 1)
                            dve.wait_ge(counted, EPP * (g + 1) + 2)
                            dve.wait_ge(added, g + 1)
                            acc = LA[:, bass.ds(block_of, 1), :].rearrange("p a n -> p (a n)")
                            nc.vector.tensor_tensor(acc, acc, ps[:P, 0, 0:NODES], ALU.add).then_inc(added, 1)

                    @block.tensor
                    def _(pe):
                        pe.sem_inc(counted, 2)
                        pe.sem_inc(added, 1)
                        with pe.Fori(0, GROUPS) as g:
                            for t in range(EPP):
                                pe.wait_ge(hot, EPP * g + t + 1)
                                if t == 0:
                                    pe.wait_ge(added, g + 1)
                                for c0, cn in CHUNKS:
                                    last = nc.tensor.matmul(ps[:P, 0, c0:c0 + cn], ohD[:, t % 2, :], ohS[:, t % 2, c0:c0 + cn],
                                                            start=t == 0, stop=t == EPP - 1)
                                last.then_inc(counted, 1)

            with ExitStack() as st:
                sb = tile_in(st)
                least, logs, done = sems_in(st)("counts_floored", "logs_ready", "log_steps")
                low, lg = sb("low", [P, 2, NODES]), sb("lg", [P, 2, NODES])
                with nc.Block() as block:
                    @block.vector
                    def _(dve):
                        step = Chain(dve, done)
                        for t in range(TILES):
                            step(nc.vector.tensor_reduce(has[:, t:t + 1], LA[:, t, :], X_AXIS, ALU.max))
                        step(nc.vector.tensor_scalar(has[:], has[:], 0.5, None, ALU.is_ge))
                        nc.vector.tensor_scalar(low[:, 0, :], LA[:, 0, :], 2.0 ** -60, None, ALU.max).then_inc(least, 1)
                        for t in range(TILES):
                            if t + 1 < TILES:
                                nc.vector.tensor_scalar(low[:, (t + 1) % 2, :], LA[:, t + 1, :], 2.0 ** -60, None,
                                                        ALU.max).then_inc(least, 1)
                            dve.wait_ge(logs, t + 1)
                            step(nc.vector.tensor_scalar(LA[:, t, :], lg[:, t % 2, :], 1.0, 2.5e28, ALU.add, ALU.mult))
                            step(nc.vector.tensor_tensor(LA[:, t, :], LA[:, t, :], lg[:, t % 2, :], ALU.min))

                    @block.scalar
                    def _(act):
                        for t in range(TILES):
                            act.wait_ge(least, t + 1)
                            if t >= 2:
                                act.wait_ge(done, TILES + 1 + 2 * (t - 1))
                            nc.scalar.activation(lg[:, t % 2, :], low[:, t % 2, :], ACT.Ln).then_inc(logs, 1)

        def attend(QT, KT, V, LA, has, A):
            with ExitStack() as st:
                sb, pb = tile_in(st), bank_in(st)
                (q_staged, scored, masked, shifted, probs_ready, turned, copied, valued, inverse, normed, logs_staged, tick) = sems_in(st)(
                    "q_staged", "scored", "masked", "shifted", "probs_ready", "probs_turned", "turned_copied",
                    "head_valued", "inverse_steps", "tile_normed", "logs_staged", "tick")
                QS = sb("QS", [128, KC, P])
                logs = sb("logs", [P, NODES])
                S = sb("S", [P, 2, NODES])
                PT = sb("PT", [P, 2, TILES, P])
                mx, z, rz = sb("mx", [P, HEADS]), sb("z", [P, HEADS]), sb("rz", [P, HEADS])
                score_ps, turn_ps, out_ps = pb("score_ps", [128, 1536]), pb("turn_ps", [128, 1536]), pb("out_ps", [128, 512])
                HALF = 4
                with nc.Block() as block:
                    @block.gpsimd
                    def _(pool):
                        pool.sem_inc(masked, 1)
                        with pool.Fori(0, TILES) as i:
                            pool.wait_ge(masked, HEADS * i + 1)
                            pool.sem_inc(tick, 1)
                            nc.gpsimd.tensor_copy(logs[:], LA[:, bass.ds(i, 1), :].rearrange("p a n -> p (a n)")
                                                  ).then_inc(logs_staged, 1)

                    @block.tensor
                    def _(pe):
                        pe.sem_inc(normed, 1)
                        with pe.Fori(0, TILES) as i:
                            for h in range(HEADS + 2):
                                if h < HEADS:
                                    lo = DK * (h % 2)
                                    if h == 0:
                                        pe.wait_ge(q_staged, i + 1)
                                    else:
                                        pe.wait_ge(masked, HEADS * i + h + 1)
                                    for c0, cn in CHUNKS:
                                        last = nc.tensor.matmul(score_ps[:P, c0:c0 + cn], QS[lo:lo + DK, h // 2, :],
                                                                KT[lo:lo + DK, h // 2, c0:c0 + cn], start=True, stop=True)
                                    last.then_inc(scored, 1)
                                if 1 <= h <= HEADS:
                                    pe.wait_ge(probs_ready, HEADS * i + h)
                                    if h > 1:
                                        pe.wait_ge(copied, 2 * (HEADS * i + h - 1))
                                    for s in range(TILES):
                                        last = nc.tensor.transpose(turn_ps[:P, 128 * s:128 * s + P],
                                                                   S[:, (h - 1) % 2, P * s:P * (s + 1)], ident[:P, :P])
                                        if s in (HALF - 1, TILES - 1):
                                            last.then_inc(turned, 1)
                                if h >= 2:
                                    v = h - 2
                                    if v == 0:
                                        pe.wait_ge(normed, i + 1)
                                    pe.wait_ge(copied, 2 * (HEADS * i + v + 1))
                                    for s in range(TILES):
                                        last = nc.tensor.matmul(out_ps[:P, DK * v:DK * (v + 1)], PT[:, v % 2, s, :],
                                                                V[:, s, DK * v:DK * (v + 1)], start=s == 0, stop=s == TILES - 1)
                                    last.then_inc(valued, 1)

                    @block.vector
                    def _(dve):
                        with dve.Fori(0, TILES) as i:
                            nc.vector.tensor_copy(QS[:], QT[:, :, bass.ds(i * P, P)]).then_inc(q_staged, 1)
                            for h in range(HEADS + 1):
                                if h < HEADS:
                                    dve.wait_ge(scored, HEADS * i + h + 1)
                                    if h >= 2:
                                        dve.wait_ge(turned, 2 * (HEADS * i + h - 1))
                                    if h == 0:
                                        dve.wait_ge(logs_staged, i + 1)
                                    dve.sem_inc(tick, 1)
                                    nc.vector.tensor_tensor_reduce(
                                        out=S[:, h % 2, :], in0=score_ps[:P, 0:NODES], in1=logs[:],
                                        scale=1.0, scalar=-3e38, op0=ALU.add, op1=ALU.max,
                                        accum_out=mx[:, h:h + 1]).then_inc(masked, 1)
                                    dve.wait_ge(masked, HEADS * i + h + 2)
                                    nc.vector.tensor_scalar(mx[:, h:h + 1], mx[:, h:h + 1], -1.0, None,
                                                            ALU.mult).then_inc(shifted, 1)
                                if h >= 1:
                                    t = h - 1
                                    dve.wait_ge(turned, 2 * (HEADS * i + t) + 1)
                                    if t >= 2:
                                        dve.wait_ge(valued, HEADS * i + t - 1)
                                    nc.vector.tensor_copy(PT[:, t % 2, 0:HALF, :],
                                                          turn_ps[:P, 0:HALF * 128].rearrange("p (s c) -> p s c", c=128)[:, :, 0:P]
                                                          ).then_inc(copied, 1)
                            dve.wait_ge(probs_ready, HEADS * (i + 1))
                            nc.vector.reciprocal(rz[:], z[:]).then_inc(inverse, 1)
                            dve.wait_ge(inverse, 2 * i + 2)
                            nc.vector.tensor_scalar(rz[:], rz[:], has[:, bass.ds(i, 1)], None, ALU.mult).then_inc(inverse, 1)
                            dve.wait_ge(inverse, 2 * i + 3)
                            dve.wait_ge(valued, HEADS * (i + 1))
                            nc.vector.tensor_tensor(
                                A[:, bass.ds(i, 1), :].rearrange("p a (h c) -> p (a h) c", c=DK),
                                out_ps[:P, :].rearrange("p (h c) -> p h c", c=DK),
                                rz[:].unsqueeze(2).to_broadcast([P, HEADS, DK]), ALU.mult).then_inc(normed, 1)

                    @block.scalar
                    def _(act):
                        act.sem_inc(inverse, 1)
                        with act.Fori(0, TILES) as i:
                            for h in range(HEADS + 1):
                                if h < HEADS:
                                    act.wait_ge(shifted, HEADS * i + h + 1)
                                    if h == 0:
                                        act.wait_ge(inverse, 2 * i + 1)
                                    nc.scalar.activation(S[:, h % 2, :], S[:, h % 2, :], ACT.Exp, bias=mx[:, h:h + 1],
                                                         accum_out=z[:, h:h + 1]).then_inc(probs_ready, 1)
                                if h >= 1:
                                    t = h - 1
                                    act.wait_ge(turned, 2 * (HEADS * i + t) + 2)
                                    if t == 0:
                                        act.wait_ge(normed, i + 1)
                                    if t >= 2:
                                        act.wait_ge(valued, HEADS * i + t - 1)
                                    nc.scalar.activation(PT[:, t % 2, HALF:TILES, :],
                                                         turn_ps[:P, HALF * 128:TILES * 128].rearrange("p (s c) -> p s c", c=128)[:, :, 0:P],
                                                         ACT.Copy).then_inc(copied, 1)

        def node_major_product(srcT, weights, k_chunks, dst, bias=None, add=None):
            with ExitStack() as st:
                sb, pb = tile_in(st), bank_in(st)
                loaded, done, moved = sems_in(st)("w_loaded", "product_done", "product_moved")
                W = sb("Wnm", [128, k_chunks, DIM])
                ps = pb("ps", [128, 4, 512])
                biasB = sb("biasB", [P, DIM]) if bias is not None else None
                with nc.Block() as block:
                    @block.sync
                    def _(sp):
                        sp.dma_start(W[:], weights.rearrange("(k p) n -> p k n", p=128)).then_inc(loaded, 16)
                        if bias is not None:
                            sp.dma_start(biasB[:], row(bias).broadcast_to([P, DIM])).then_inc(loaded, 16)

                    @block.tensor
                    def _(pe):
                        pe.wait_ge(loaded, 16 if bias is None else 32)
                        for t in range(TILES):
                            if t >= 4:
                                pe.wait_ge(moved, (t - 3) * (1 if bias is None else 2))
                            for k in range(k_chunks):
                                last = nc.tensor.matmul(ps[:P, t % 4, :], srcT[:, k, P * t:P * (t + 1)], W[:, k, :],
                                                        start=k == 0, stop=k == k_chunks - 1)
                            last.then_inc(done, 1)

                    @block.vector
                    def _(dve):
                        if bias is not None:
                            dve.wait_ge(loaded, 32)
                        n = 0
                        for t in range(TILES):
                            dve.wait_ge(done, t + 1)
                            nc.vector.tensor_tensor(dst[:, t, :], ps[:P, t % 4, :], add[:, t, :], ALU.add).then_inc(moved, 1)
                            n += 1
                            if bias is not None:
                                dve.wait_ge(moved, n)
                                nc.vector.tensor_tensor(dst[:, t, :], dst[:, t, :], biasB[:], ALU.add).then_inc(moved, 1)
                                n += 1

        def feature_major_layer(srcT, weights, bias, dstT, m_chunks, function):
            with ExitStack() as st:
                sb, pb = tile_in(st), bank_in(st)
                loaded, turned, bias_ready, done, moved = sems_in(st)(
                    "w_loaded", "bias_turned", "bias_ready", "product_done", "product_moved")
                W = sb("Wfm", [128, KC, m_chunks * 128])
                braw, bT = sb("braw", [m_chunks, 128]), sb("bT", [128, m_chunks])
                ps = pb("ps", [128, 4, 512])
                jobs = [(m, c0, cn) for m in range(m_chunks) for c0, cn in CHUNKS]
                with nc.Block() as block:
                    @block.sync
                    def _(sp):
                        sp.dma_start(W[:], weights.rearrange("(k p) n -> p k n", p=128)).then_inc(loaded, 16)
                        sp.dma_start(braw[:], bias.rearrange("(m p) -> m p", p=128)).then_inc(loaded, 16)

                    @block.tensor
                    def _(pe):
                        pe.wait_ge(loaded, 32)
                        nc.tensor.transpose(ps[:, 3, 0:m_chunks], braw[:], ident[:m_chunks, :m_chunks]).then_inc(turned, 1)
                        for n, (m, c0, cn) in enumerate(jobs):
                            if n == 3:
                                pe.wait_ge(bias_ready, 1)
                            if n >= 4:
                                pe.wait_ge(moved, n - 3)
                            for k in range(KC):
                                last = nc.tensor.matmul(ps[:, n % 4, 0:cn], W[:, k, 128 * m:128 * (m + 1)],
                                                        srcT[:, k, c0:c0 + cn], start=k == 0, stop=k == KC - 1)
                            last.then_inc(done, 1)

                    @block.scalar
                    def _(act):
                        act.wait_ge(turned, 1)
                        nc.scalar.activation(bT[:], ps[:, 3, 0:m_chunks], ACT.Copy).then_inc(bias_ready, 1)
                        act.wait_ge(bias_ready, 1)
                        for n, (m, c0, cn) in enumerate(jobs):
                            act.wait_ge(done, n + 1)
                            nc.scalar.activation(dstT[:, m, c0:c0 + cn], ps[:, n % 4, 0:cn], function,
                                                 bias=bT[:, m:m + 1]).then_inc(moved, 1)

        def gate(srcT, weights, weights_are_rows, bias, probs, best, bestI):
            with ExitStack() as st:
                sb, pb = tile_in(st), bank_in(st)
                loaded, turned, w_ready, done, logits_in, exped, steps = sems_in(st)(
                    "w_loaded", "w_turned", "w_ready", "logits_done", "logits_in", "exped", "gate_steps")
                W = sb("Wg", [128, KC, EXPERTS])
                Wraw = sb("Wraw", [EXPERTS, DIM]) if weights_are_rows else None
                biasB = sb("biasB", [P, EXPERTS])
                mx, zs = sb("mx", [P, TILES]), sb("zs", [P, TILES])
                lg = sb("lg", [P, TILES, EXPERTS])
                ps = pb("ps", [128, 2, 512])
                with nc.Block() as block:
                    @block.sync
                    def _(sp):
                        if weights_are_rows:
                            sp.dma_start(Wraw[:], weights).then_inc(loaded, 16)
                        else:
                            sp.dma_start(W[:], weights.rearrange("(k p) n -> p k n", p=128)).then_inc(loaded, 16)
                        sp.dma_start(biasB[:], row(bias).broadcast_to([P, EXPERTS])).then_inc(loaded, 16)

                    @block.tensor
                    def _(pe):
                        pe.wait_ge(loaded, 32)
                        if weights_are_rows:
                            for k in range(KC):
                                last = nc.tensor.transpose(ps[:, 1, EXPERTS * k:EXPERTS * (k + 1)],
                                                           Wraw[:, 128 * k:128 * (k + 1)], ident[:EXPERTS, :EXPERTS])
                            last.then_inc(turned, 1)
                            pe.wait_ge(w_ready, 1)
                        for t in range(TILES):
                            for k in range(KC):
                                last = nc.tensor.matmul(ps[:P, 0, EXPERTS * t:EXPERTS * (t + 1)], srcT[:, k, P * t:P * (t + 1)],
                                                        W[:, k, :], start=k == 0, stop=k == KC - 1)
                        last.then_inc(done, 1)

                    @block.scalar
                    def _(act):
                        if weights_are_rows:
                            act.wait_ge(turned, 1)
                            nc.scalar.activation(W[:], ps[:, 1, 0:KC * EXPERTS].rearrange("p (k e) -> p k e", k=KC),
                                                 ACT.Copy).then_inc(w_ready, 1)
                        act.wait_ge(logits_in, 1)
                        nc.scalar.activation(probs[:], lg[:], ACT.Exp).then_inc(exped, 1)

                    @block.vector
                    def _(dve):
                        step = Chain(dve, steps)
                        dve.wait_ge(loaded, 32)
                        dve.wait_ge(done, 1)
                        step(nc.vector.tensor_tensor(lg[:], ps[:P, 0, 0:TILES * EXPERTS].rearrange("p (t e) -> p t e", t=TILES),
                                                     biasB[:].unsqueeze(1).to_broadcast([P, TILES, EXPERTS]), ALU.add))
                        step(nc.vector.tensor_reduce(mx[:], lg[:], X_AXIS, ALU.max))
                        nc.vector.tensor_tensor(lg[:], lg[:], mx[:].unsqueeze(2).to_broadcast([P, TILES, EXPERTS]),
                                                ALU.subtract).then_inc(logits_in, 1)
                        dve.wait_ge(exped, 1)
                        step(nc.vector.tensor_reduce(zs[:], probs[:], X_AXIS, ALU.add))
                        step(nc.vector.reciprocal(zs[:], zs[:]))
                        step(nc.vector.tensor_tensor(probs[:], probs[:], zs[:].unsqueeze(2).to_broadcast([P, TILES, EXPERTS]), ALU.mult))
                        for t in range(TILES):
                            step(nc.vector.max(best[:, t, :], probs[:, t, :]))
                            step(nc.vector.max_index(bestI[:, t, :], best[:, t, :], probs[:, t, :]))

        def place_choices(best, bestI, weight, slot_in, slot_out):
            with ExitStack() as st:
                sb, pb = tile_in(st), bank_in(st)
                steps, numbered, w8_ready, turned, first_out, rows_in, compared, ranked = sems_in(st)(
                    "place_steps", "nodes_numbered", "w8_ready", "turned", "first_out", "rows_in", "compared", "ranked")
                idxF = sb("idxF", [P, TILES, 2])
                oh = sb("oh", [P, 2, TILES, EXPERTS])
                w8, tmp, routed = (sb("w8", [P, TILES, EXPERTS]), sb("tmp", [P, TILES, EXPERTS]),
                                   sb("routed", [P, TILES, EXPERTS]))
                w8T = sb("w8T", [EXPERTS, NODES])
                ohT = sb("ohT", [EXPERTS, 2, NODES])
                junk, same = sb("junk", [P, NODES]), sb("same", [P, P])
                own = sb("own", [P, TILES, 2])
                parts = sb("parts", [P, TILES, 2, 3])
                rank, keep = sb("rank", [P, TILES, 2]), sb("keep", [P, TILES, 2])
                slotF, node, nodeF = (sb("slotF", [P, TILES, 2]), sb("node", [P, TILES, 2], I32),
                                      sb("nodeF", [P, TILES, 2]))
                ps = pb("ps", [128, 2, 2048])
                wide = [P, TILES, EXPERTS]
                with nc.Block() as block:
                    @block.gpsimd
                    def _(pool):
                        nc.gpsimd.iota(node[:], pattern=[[P, TILES], [NODES, 2]], base=EXPERTS * ROWS0,
                                       channel_multiplier=1).then_inc(numbered, 1)

                    @block.vector
                    def _(dve):
                        step = Chain(dve, steps)
                        step(nc.vector.memset(parts[:], 0.0))
                        step(nc.vector.tensor_copy(idxF[:], bestI[:, :, 0:2]))
                        e8 = count[:P, 0:EXPERTS].unsqueeze(1).to_broadcast(wide)
                        for c in range(2):
                            step(nc.vector.tensor_tensor(oh[:, c], e8, idxF[:, :, c:c + 1].to_broadcast(wide), ALU.is_equal))
                        step(nc.vector.tensor_tensor(routed[:], oh[:, 0], oh[:, 1], ALU.add))
                        step(nc.vector.tensor_scalar(routed[:], routed[:], -1.0, None, ALU.add))
                        step(nc.vector.tensor_tensor(w8[:], oh[:, 0], best[:, :, 0:1].to_broadcast(wide), ALU.mult))
                        step(nc.vector.tensor_tensor(tmp[:], oh[:, 1], best[:, :, 1:2].to_broadcast(wide), ALU.mult))
                        step(nc.vector.tensor_tensor(w8[:], w8[:], tmp[:], ALU.add))
                        step(nc.vector.tensor_tensor(w8[:], w8[:], routed[:], ALU.add))
                        dve.sem_inc(w8_ready, 1)
                        dve.wait_ge(numbered, 1)
                        step(nc.vector.tensor_copy(nodeF[:], node[:]))
                        for n in range(2 * TILES):
                            t, c = n // 2, n % 2
                            mine = own[:, t, c:c + 1]
                            dve.wait_ge(ranked, n + 1)
                            full = ps[:P, n % 2, 0:NODES]
                            step(nc.vector.tensor_tensor(same[:], full[:, P * t:P * (t + 1)], ident[:P, :P], ALU.mult))
                            step(nc.vector.tensor_reduce(mine, same[:], X_AXIS, ALU.add))
                            if t > 0:
                                step(nc.vector.tensor_scalar(junk[:, 0:P * t], full[:, 0:P * t], mine, None, ALU.is_ge, ALU.add,
                                                             accum_out=parts[:, t, c, 0:1]))
                            step(nc.vector.tensor_scalar(junk[:, 0:NODES - P * t], full[:, P * t:NODES], mine, None,
                                                         ALU.is_gt, ALU.add, accum_out=parts[:, t, c, 1:2]))
                            step(nc.vector.scalar_tensor_tensor(out=same[:], in0=full[:, P * t:P * (t + 1)], scalar=mine,
                                                                in1=earlier[:P, :P], op0=ALU.is_equal, op1=ALU.mult))
                            dve.sem_inc(compared, 1)
                            step(nc.vector.tensor_reduce(parts[:, t, c, 2:3], same[:], X_AXIS, ALU.add))
                        step(nc.vector.tensor_reduce(rank[:], parts[:], X_AXIS, ALU.add))
                        step(nc.vector.tensor_scalar(keep[:], rank[:], CAP0 - 0.5, None, ALU.is_lt))
                        step(nc.vector.scalar_tensor_tensor(out=slotF[:], in0=idxF[:], scalar=float(ROWS0), in1=rank[:],
                                                            op0=ALU.mult, op1=ALU.add))
                        step(nc.vector.tensor_tensor(slotF[:], slotF[:], keep[:], ALU.mult))
                        step(nc.vector.tensor_copy(slot_out[:], slotF[:]))
                        step(nc.vector.tensor_tensor(weight[:], best[:, :, 0:2], keep[:], ALU.mult))
                        step(nc.vector.tensor_scalar(keep[:], keep[:], -1.0, 1.0, ALU.mult, ALU.add))
                        step(nc.vector.tensor_tensor(keep[:], keep[:], nodeF[:], ALU.mult))
                        step(nc.vector.tensor_tensor(slot_in[:], slotF[:], keep[:], ALU.add))

                    @block.tensor
                    def _(pe):
                        pe.wait_ge(w8_ready, 1)
                        for t in range(TILES):
                            nc.tensor.transpose(ps[:EXPERTS, 0, 128 * t:128 * t + P], w8[:, t, :], ident[:P, :P])
                        for c in range(2):
                            if c == 1:
                                pe.wait_ge(first_out, 1)
                            for t in range(TILES):
                                last = nc.tensor.transpose(ps[:EXPERTS, 1, 128 * t:128 * t + P], oh[:, c, t, :], ident[:P, :P])
                            last.then_inc(turned, 1)
                        pe.wait_ge(rows_in, 1)
                        for n in range(2 * TILES):
                            t, c = n // 2, n % 2
                            if n >= 2:
                                pe.wait_ge(compared, n - 1)
                            for c0, cn in CHUNKS:
                                last = nc.tensor.matmul(ps[:P, n % 2, c0:c0 + cn], ohT[:, c, P * t:P * (t + 1)],
                                                        w8T[:, c0:c0 + cn], start=True, stop=True)
                            last.then_inc(ranked, 1)

                    @block.scalar
                    def _(act):
                        act.wait_ge(turned, 1)

                        def row_of_tiles(bank):
                            return ps[:EXPERTS, bank, 0:128 * TILES].rearrange("e (t n) -> e t n", n=128)[:, :, 0:P]

                        def by_tile(rows):
                            return rows.rearrange("e (t n) -> e t n", n=P)

                        nc.scalar.activation(by_tile(w8T[:]), row_of_tiles(0), ACT.Copy)
                        nc.scalar.activation(by_tile(ohT[:, 0, :]), row_of_tiles(1), ACT.Copy).then_inc(first_out, 1)
                        act.wait_ge(turned, 2)
                        nc.scalar.activation(by_tile(ohT[:, 1, :]), row_of_tiles(1), ACT.Copy).then_inc(rows_in, 1)

        def scatter_rows(src, slots, choices, target):
            n_rows = target.shape[0]
            with ExitStack() as st:
                zeroed, sent = sems_in(st)("zeroed", "rows_sent")
                with nc.Block() as block:
                    @block.sync
                    def _(sp):
                        n = 0
                        for r in range(0, n_rows, 128):
                            m = min(128, n_rows - r)
                            sp.dma_start(target[r:r + m, :], zeros[:m, :]).then_inc(zeroed, 16)
                            n += 16
                        sp.wait_ge(zeroed, n)

                    @block.gpsimd
                    def _(pool):
                        pool.wait_ge(zeroed, 16 * ((n_rows + 127) // 128))
                        for t in range(TILES):
                            for c in range(choices):
                                pool.indirect_dma_start(
                                    out=target, out_offset=bass.IndirectOffsetOnAxis(ap=slots[:, t, c:c + 1], axis=0),
                                    in_=src[:, t, :], in_offset=None).then_inc(sent, 16)
                        pool.wait_ge(sent, 16 * TILES * choices)

        def experts0():
            with ExitStack() as st:
                sb, pb = tile_in(st), bank_in(st)
                x_loaded = sems_in(st)("x_loaded0", "x_loaded1")
                w1_loaded = sems_in(st)("w1_loaded0", "w1_loaded1")
                w2_loaded = sems_in(st)("w2_loaded0", "w2_loaded1")
                stored = sems_in(st)("stored0", "stored1")
                (b_loaded, b_turned, b_ready, x_turned, x_moved, hid_done, hid_moved, y_done, y_moved, back_done,
                 back_moved, y_free, tick) = sems_in(st)(
                    "b_loaded", "b_turned", "b_ready", "x_turned", "x_moved", "hid_done", "hid_moved", "y_done",
                    "y_moved", "back_done", "back_moved", "y_free", "tick")
                W1 = [sb(f"W1_{i}", [128, KC, HID0]) for i in range(2)]
                W2 = [sb(f"W2_{i}", [128, MC0, DIM]) for i in range(2)]
                b1raw, b2raw = sb("b1raw", [EXPERTS * MC0, 128]), sb("b2raw", [EXPERTS * KC, 128])
                b1T, b2T = sb("b1T", [128, EXPERTS * MC0]), sb("b2T", [128, EXPERTS * KC])
                xe = [sb(f"xe{i}", [HALF0, 2, DIM]) for i in range(2)]
                ye = [sb(f"ye{i}", [HALF0, 2, DIM]) for i in range(2)]
                xT, yT = sb("xT", [128, KC, ROWS0]), sb("yT", [128, KC, ROWS0])
                hid = sb("hid", [128, MC0, ROWS0])
                hid_ps, y_ps, turn_ps = pb("hid_ps", [128, 4, 512]), pb("y_ps", [128, 2, 512]), pb("turn_ps", [128, 2, 512])
                with nc.Block() as block:
                    def load_first(sp, e, b):
                        rows = xin0[bass.ds(e * ROWS0, ROWS0), :].rearrange("(c p) d -> p c d", p=HALF0)
                        sp.dma_start(xe[b][:], rows).then_inc(x_loaded[b], 16)
                        sp.dma_start(W1[b][:], I["L0_ffn_w1"][bass.ds(e, 1)].rearrange("a (k p) n -> p (a k) n", p=128)
                                     ).then_inc(w1_loaded[b], 16)

                    def load_second(sp, e, b):
                        sp.dma_start(W2[b][:], I["L0_ffn_w2"][bass.ds(e, 1)].rearrange("a (m p) n -> p (a m) n", p=128)
                                     ).then_inc(w2_loaded[b], 16)

                    @block.sync
                    def _(sp):
                        sp.dma_start(b1raw[:], I["L0_ffn_b1"].rearrange("e (m p) -> (e m) p", p=128)).then_inc(b_loaded, 16)
                        sp.dma_start(b2raw[:], I["L0_ffn_b2"].rearrange("e (m p) -> (e m) p", p=128)).then_inc(b_loaded, 16)
                        for b in range(2):
                            load_first(sp, b, b)
                            load_second(sp, b, b)
                        with sp.Fori(0, EXPERTS // 2 - 1) as r:
                            for b in range(2):
                                sp.wait_ge(hid_done, MC0 * (2 * r + b + 1))
                                sp.sem_inc(tick, 1)
                                load_first(sp, 2 * r + 2 + b, b)
                                sp.wait_ge(y_done, KC * (2 * r + b + 1))
                                sp.sem_inc(tick, 1)
                                load_second(sp, 2 * r + 2 + b, b)

                    @block.gpsimd
                    def _(pool):
                        with pool.Fori(0, EXPERTS // 2) as r:
                            for b in range(2):
                                pool.wait_ge(back_moved, 2 * (2 * r + b + 1) + 2)
                                pool.sem_inc(tick, 1)
                                rows = yout0[bass.ds((2 * r + b) * ROWS0, ROWS0), :].rearrange("(c p) d -> p c d", p=HALF0)
                                pool.dma_start(rows, ye[b][:]).then_inc(stored[b], 16)
                                pool.wait_ge(stored[b], 16 * (r + 1))
                                pool.sem_inc(y_free, 1)

                    @block.tensor
                    def _(pe):
                        pe.wait_ge(b_loaded, 32)
                        nc.tensor.transpose(y_ps[:, 0, 0:EXPERTS * MC0], b1raw[:], ident[:])
                        nc.tensor.transpose(y_ps[:, 1, 0:EXPERTS * KC], b2raw[:], ident[:EXPERTS * KC, :EXPERTS * KC]
                                            ).then_inc(b_turned, 1)
                        pe.wait_ge(b_ready, 2)
                        pe.sem_inc(back_moved, 2)
                        with pe.Fori(0, EXPERTS // 2) as r:
                            for b in range(2):
                                e = 2 * r + b
                                pe.wait_ge(x_loaded[b], 16 * (r + 1))
                                for c in range(2):
                                    pe.wait_ge(back_moved, 2 * e + c + 1)
                                    for k in range(KC):
                                        last = nc.tensor.transpose(turn_ps[:, c, HALF0 * k:HALF0 * (k + 1)],
                                                                   xe[b][:, c, 128 * k:128 * (k + 1)], ident[:HALF0, :HALF0])
                                    last.then_inc(x_turned, 1)
                                pe.wait_ge(w1_loaded[b], 16 * (r + 1))
                                pe.wait_ge(x_moved, 2 * (e + 1))
                                for m in range(MC0):
                                    if m >= 4:
                                        pe.wait_ge(hid_moved, MC0 * e + m - 3)
                                    for k in range(KC):
                                        last = nc.tensor.matmul(hid_ps[:, m % 4, 0:ROWS0], W1[b][:, k, 128 * m:128 * (m + 1)],
                                                                xT[:, k, :], start=k == 0, stop=k == KC - 1)
                                    last.then_inc(hid_done, 1)
                                pe.wait_ge(w2_loaded[b], 16 * (r + 1))
                                for d in range(KC):
                                    if d >= 2:
                                        pe.wait_ge(y_moved, KC * e + d - 1)
                                    for m in range(MC0):
                                        if d == 0:
                                            pe.wait_ge(hid_moved, MC0 * e + m + 1)
                                        last = nc.tensor.matmul(y_ps[:, d % 2, 0:ROWS0], W2[b][:, m, 128 * d:128 * (d + 1)],
                                                                hid[:, m, :], start=m == 0, stop=m == MC0 - 1)
                                    last.then_inc(y_done, 1)
                                pe.wait_ge(y_moved, KC * (e + 1))
                                for c in range(2):
                                    for k in range(KC):
                                        last = nc.tensor.transpose(turn_ps[:HALF0, c, 128 * k:128 * (k + 1)],
                                                                   yT[:, k, HALF0 * c:HALF0 * (c + 1)], ident[:])
                                    last.then_inc(back_done, 1)

                    @block.scalar
                    def _(act):
                        act.wait_ge(b_turned, 1)
                        nc.scalar.activation(b1T[:], y_ps[:, 0, 0:EXPERTS * MC0], ACT.Copy).then_inc(b_ready, 1)
                        nc.scalar.activation(b2T[:], y_ps[:, 1, 0:EXPERTS * KC], ACT.Copy).then_inc(b_ready, 1)
                        act.wait_ge(b_ready, 2)
                        with act.Fori(0, EXPERTS) as e:
                            for c in range(2):
                                act.wait_ge(x_turned, 2 * e + c + 1)
                                nc.scalar.activation(xT[:, :, HALF0 * c:HALF0 * (c + 1)],
                                                     turn_ps[:, c, 0:KC * HALF0].rearrange("p (k n) -> p k n", k=KC),
                                                     ACT.Copy).then_inc(x_moved, 1)
                            for m in range(MC0):
                                act.wait_ge(hid_done, MC0 * e + m + 1)
                                nc.scalar.activation(hid[:, m, :], hid_ps[:, m % 4, 0:ROWS0], ACT.Gelu,
                                                     bias=b1T[:, bass.ds(e * MC0 + m, 1)]).then_inc(hid_moved, 1)

                    @block.vector
                    def _(dve):
                        dve.sem_inc(y_free, 2)
                        dve.wait_ge(b_ready, 2)
                        with dve.Fori(0, EXPERTS // 2) as r:
                            for b in range(2):
                                e = 2 * r + b
                                for d in range(KC):
                                    dve.wait_ge(y_done, KC * e + d + 1)
                                    nc.vector.tensor_scalar(yT[:, d, :], y_ps[:, d % 2, 0:ROWS0], b2T[:, bass.ds(e * KC + d, 1)],
                                                            None, ALU.add).then_inc(y_moved, 1)
                                dve.wait_ge(y_free, e + 1)
                                for c in range(2):
                                    dve.wait_ge(back_done, 2 * e + c + 1)
                                    nc.vector.tensor_copy(ye[b][:, c, :], turn_ps[:HALF0, c, :]).then_inc(back_moved, 1)

        def combine(picks):
            with ExitStack() as st:
                sb = tile_in(st)
                RING = 4
                arrived = sems_in(st)(*[f"arrived{i}" for i in range(RING)])
                (added,) = sems_in(st)("added")
                got = sb("got", [P, RING, DIM])
                jobs = [(t, *pick) for t in range(TILES) for pick in picks]
                with nc.Block() as block:
                    @block.gpsimd
                    def _(pool):
                        for n, (t, source, slots, _) in enumerate(jobs):
                            if n >= RING:
                                pool.wait_ge(added, n - RING + 1)
                            pool.indirect_dma_start(
                                out=got[:, n % RING, :], out_offset=None, in_=source,
                                in_offset=bass.IndirectOffsetOnAxis(ap=slots(t), axis=0)).then_inc(arrived[n % RING], 16)

                    @block.vector
                    def _(dve):
                        for n, (t, _, _, weight) in enumerate(jobs):
                            dve.wait_ge(arrived[n % RING], 16 * (n // RING + 1))
                            if n >= 1:
                                dve.wait_ge(added, n)
                            nc.vector.scalar_tensor_tensor(out=X[:, t, :], in0=got[:, n % RING, :], scalar=weight(t),
                                                           in1=X[:, t, :], op0=ALU.mult, op1=ALU.add).then_inc(added, 1)

        def mix_up(xT):
            with ExitStack() as st:
                sb, pb = tile_in(st), bank_in(st)
                loaded, done, moved, stored = sems_in(st)("w_loaded", "mixed", "mixed_moved", "mixed_stored")
                W = sb("Wup", [128, 2, MUL])
                rows = sb("rows", [P, TILES, DIM])
                ps = pb("ps", [128, 4, 512])
                with nc.Block() as block:
                    @block.sync
                    def _(sp):
                        sp.dma_start(W[:, 0, :], I["L1_gnn_W_up0"]).then_inc(loaded, 16)
                        sp.dma_start(W[:, 1, :], I["L1_gnn_W_up1"]).then_inc(loaded, 16)
                        for t in range(TILES):
                            sp.wait_ge(moved, t + 1)
                            sp.dma_start(up_dram[P * t:P * (t + 1), :], rows[:, t, :]).then_inc(stored, 16)
                        sp.wait_ge(stored, 16 * TILES)

                    @block.tensor
                    def _(pe):
                        pe.wait_ge(loaded, 32)
                        for t in range(TILES):
                            if t >= 4:
                                pe.wait_ge(moved, t - 3)
                            for q in range(4):
                                last = nc.tensor.matmul(ps[:P, t % 4, MUL * q:MUL * (q + 1)], xT[:, q, P * t:P * (t + 1)],
                                                        W[:, min(q, 1), :], start=True, stop=True)
                            last.then_inc(done, 1)

                    @block.scalar
                    def _(act):
                        for t in range(TILES):
                            act.wait_ge(done, t + 1)
                            nc.scalar.activation(rows[:, t, :], ps[:P, t % 4, :], ACT.Copy,
                                                 scale=1.0 / math.sqrt(MUL)).then_inc(moved, 1)

        def messages(RECS, MSG):
            HID = 64
            with ExitStack() as st:
                sb, pb = tile_in(st), bank_in(st)
                arrived = sems_in(st)(*[f"rows_arrived{t}" for t in range(EPP)])
                (zeroed, w_loaded, w_scaled, consts, feats, feats_turned, feats_in, layer_done, layer_out, weighed, products,
                 one_hots, summed, taken, idx_ready, staged, tick) = sems_in(st)(
                    "zeroed", "mlp_loaded", "mlp_scaled", "consts_ready", "feats_staged", "feats_turned", "feats_in",
                    "layer_done", "layer_out", "edge_weights_done", "products_ready", "one_hots_ready", "group_summed",
                    "sums_taken", "indices_ready", "recs_staged", "tick")
                W1b, W2b, W3b = sb("W1b", [16, 128]), sb("W2b", [128, 128]), sb("W3b", [128, 128])
                W4 = sb("W4", [128, DIM])
                srcI = sb("srcI", [128, GROUPS, EPP], I32)
                idx = sb("idx", [128, 2, EPP], I32)
                rows = sb("rows", [128, EPP, DIM])
                lane = sb("lane", [128, P])
                rg = sb("rg", [128, EPP, 8])
                fs = sb("fs", [128, 2, 16])
                fT, h1, h2, h3 = sb("fT", [16, 256]), sb("h1", [128, 256]), sb("h2", [128, 256]), sb("h3", [128, 256])
                prod = sb("prod", [128, 2, 2 * DIM])
                oh = sb("oh", [128, 2, 4, P])
                acc, w_ps, mlp_ps = pb("acc", [128, 2, 2, 512]), pb("w_ps", [128, 2, 512]), pb("mlp_ps", [128, 2, 512])

                with nc.Block() as block:
                    @block.sync
                    def _(sp):
                        sp.wait_ge(zeroed, 1)
                        for w, name, k in ((W1b, "L1_gnn_W_mlp1", 8), (W2b, "L1_gnn_W_mlp2", HID), (W3b, "L1_gnn_W_mlp3", HID)):
                            for half in range(2):
                                sp.dma_start(w[k * half:k * (half + 1), HID * half:HID * (half + 1)], I[name]).then_inc(w_loaded, 16)
                        for half in range(2):
                            sp.dma_start(W4[HID * half:HID * (half + 1), :], I["L1_gnn_W_mlp4"]).then_inc(w_loaded, 16)

                    @block.gpsimd
                    def _(pool):
                        nc.gpsimd.memset(W1b[:], 0.0)
                        nc.gpsimd.memset(W2b[:], 0.0)
                        nc.gpsimd.memset(W3b[:], 0.0)
                        nc.gpsimd.iota(lane[:], pattern=[[1, P]], base=0, channel_multiplier=0,
                                       allow_small_or_imprecise_dtypes=True).then_inc(zeroed, 1)
                        nc.gpsimd.memset(MSG[:], 0.0).then_inc(consts, 1)
                        pool.sem_inc(products, EPP)
                        pool.wait_ge(idx_ready, 1)
                        with pool.Fori(0, GROUPS // 2) as r:
                            for par in range(2):
                                g = 2 * r + par
                                nc.gpsimd.tensor_copy(idx[:, par, :], srcI[:, bass.ds(g, 1), :].rearrange("p a t -> p (a t)")
                                                      ).then_inc(idx_ready, 1)
                                pool.wait_ge(idx_ready, g + 2)
                                pool.sem_inc(tick, 1)
                                for t in range(EPP):
                                    pool.wait_ge(products, EPP * g + t + 1)
                                    pool.sem_inc(tick, 1)
                                    pool.indirect_dma_start(
                                        out=rows[:, t, :], out_offset=None, in_=up_dram,
                                        in_offset=bass.IndirectOffsetOnAxis(ap=idx[:, par, t:t + 1], axis=0)
                                    ).then_inc(arrived[t], 16)

                    @block.tensor
                    def _(pe):
                        def turn_features(n):
                            pe.wait_ge(feats, n)
                            for tt in range(2):
                                last = nc.tensor.transpose(mlp_ps[:16, 0, 128 * tt:128 * (tt + 1)], fs[:, tt, :], ident[:])
                            last.then_inc(feats_turned, 1)

                        def weigh(t, layers):
                            if layers is not None:
                                pe.wait_ge(layer_out, layers)
                            half, col = t // 2, 128 * (t % 2)
                            nc.tensor.matmul(w_ps[:, t % 2, :], h3[HID * half:HID * (half + 1), col:col + 128],
                                             W4[HID * half:HID * (half + 1), :], start=True, stop=True).then_inc(weighed, 1)

                        def layer1(n):
                            pe.wait_ge(feats_in, n)
                            nc.tensor.matmul(mlp_ps[:, 1, 0:256], W1b[:], fT[:], start=True, stop=True).then_inc(layer_done, 1)

                        def layer2(done):
                            pe.wait_ge(layer_out, done)
                            nc.tensor.matmul(mlp_ps[:, 0, 0:256], W2b[:], h1[:], start=True, stop=True).then_inc(layer_done, 1)

                        def layer3(done):
                            pe.wait_ge(layer_out, done)
                            nc.tensor.matmul(mlp_ps[:, 1, 0:256], W3b[:], h2[:], start=True, stop=True).then_inc(layer_done, 1)

                        pe.wait_ge(w_loaded, 128)
                        pe.wait_ge(w_scaled, 2)
                        turn_features(1)
                        layer1(1)
                        layer2(1)
                        layer3(2)
                        weigh(0, 3)
                        pe.sem_inc(taken, 2)
                        with pe.Fori(0, GROUPS // 2) as r:
                            for par in range(2):
                                g = 2 * r + par
                                for t in range(EPP):
                                    pe.wait_ge(products, EPP * g + t + EPP)
                                    weigh((t + 1) % EPP, 3 * (g + 2) if t == EPP - 1 else None)
                                    if t == 0:
                                        turn_features(g + 2)
                                    pe.wait_ge(one_hots, EPP * g + t + 1)
                                    pe.wait_ge(products, EPP * g + t + 1 + EPP)
                                    if t == 0:
                                        pe.wait_ge(taken, g + 1)
                                    nc.tensor.matmul(acc[:P, par, 0, :], oh[:, t % 2, 0, :], prod[:, t % 2, 0:DIM],
                                                     start=t == 0, stop=t == EPP - 1)
                                    if t == 0:
                                        layer1(g + 2)
                                    if t == 1:
                                        layer2(3 * (g + 1) + 1)
                                    if t == 2:
                                        layer3(3 * (g + 1) + 2)
                                    outs = acc[:P, par, 1, :].rearrange("p (b c) -> p b c", c=128)
                                    prods = prod[:, t % 2, DIM:2 * DIM].rearrange("p (b c) -> p b c", c=128)
                                    for i in range(3):
                                        last = nc.tensor.matmul(outs[:, i::3 - i, :], oh[:, t % 2, 1 + i, :],
                                                                prods[:, 0:2 + i:1 + i, :], start=t == 0 and i == 0,
                                                                stop=t == EPP - 1 and i == 2, skip_group_check=True)
                                    last.then_inc(summed, 1)

                    @block.scalar
                    def _(act):
                        def features_in(n):
                            act.wait_ge(feats_turned, n)
                            nc.scalar.activation(fT[:], mlp_ps[:16, 0, 0:256], ACT.Copy).then_inc(feats_in, 1)

                        def layer(n, which):
                            act.wait_ge(layer_done, n)
                            nc.scalar.activation((h1, h2, h3)[which][:], mlp_ps[:, (which + 1) % 2, 0:256], ACT.Silu,
                                                 scale=(1 / math.sqrt(8), SILU_2MOM / math.sqrt(HID), SILU_2MOM / math.sqrt(HID))[which]
                                                 ).then_inc(layer_out, 1)

                        features_in(1)
                        for which in range(3):
                            layer(which + 1, which)
                        with act.Fori(0, GROUPS) as g:
                            features_in(g + 2)
                            for which in range(3):
                                layer(3 * (g + 1) + which + 1, which)

                    @block.vector
                    def _(dve):
                        def stage_features(g):
                            nc.vector.tensor_copy(fs[:].rearrange("p t (b f) -> p b t f", b=2),
                                                  RECS[:, bass.ds(g, 1), :, 8:16].rearrange("p a (b t) f -> p (a b) t f", b=2)
                                                  ).then_inc(feats, 1)

                        nc.vector.tensor_copy(srcI[:], RECS[:, 0:GROUPS, :, 0]).then_inc(idx_ready, 1)
                        dve.wait_ge(w_loaded, 128)
                        nc.vector.tensor_scalar(W4[:], W4[:], SILU_2MOM / math.sqrt(HID), None, ALU.mult).then_inc(w_scaled, 1)
                        dve.wait_ge(w_scaled, 1)
                        nc.vector.tensor_scalar(W4[:, 384:512], W4[:, 384:512], 1 / math.sqrt(3), None, ALU.mult).then_inc(w_scaled, 1)
                        stage_features(0)
                        dve.wait_ge(consts, 1)
                        dve.sem_inc(summed, 2)
                        with dve.Fori(0, GROUPS // 2) as r:
                            for par in range(2):
                                g = 2 * r + par
                                block_of = dve.value_load(blockI[0:1, bass.ds(g, 1)], min_val=0, max_val=TILES - 1)
                                nc.vector.tensor_copy(rg[:], RECS[:, bass.ds(g, 1), :, 0:8].rearrange("p a t w -> p (a t) w")
                                                      ).then_inc(staged, 1)
                                dve.wait_ge(feats_turned, g + 1)
                                stage_features(g + 1)
                                dve.wait_ge(staged, g + 1)
                                for t in range(EPP):
                                    dve.wait_ge(summed, EPP * g + t + 1)
                                    for q in range(4):
                                        last = nc.vector.tensor_scalar(oh[:, t % 2, q, :], lane[:], rg[:, t, 1:2],
                                                                       rg[:, t, 4 + q:5 + q], ALU.is_equal, ALU.mult)
                                    last.then_inc(one_hots, 1)
                                    dve.wait_ge(weighed, EPP * g + t + 1)
                                    dve.wait_ge(arrived[t], 16 * (g + 1))
                                    pr = prod[:, t % 2, :].rearrange("p (b c) -> p b c", c=128)
                                    w = w_ps[:, t % 2, :].rearrange("p (b c) -> p b c", c=128)
                                    s = rows[:, t, :].rearrange("p (b c) -> p b c", c=128)
                                    nc.vector.tensor_tensor(pr[:, 0:5:4, :], w[:, 0:2, :], s[:, 0:1, :].to_broadcast([128, 2, 128]), ALU.mult)
                                    nc.vector.tensor_tensor(pr[:, 1:4, :], w[:, 2:3, :].to_broadcast([128, 3, 128]), s[:, 1:4, :], ALU.mult)
                                    nc.vector.tensor_tensor(pr[:, 5:8, :], w[:, 3:4, :].to_broadcast([128, 3, 128]), s[:, 1:4, :], ALU.mult
                                                            ).then_inc(products, 1)
                                dve.wait_ge(summed, EPP * (g + 1) + 2)
                                dve.wait_ge(taken, g + 2)
                                sums = MSG[:, bass.ds(block_of, 1), :].rearrange("p a n -> p (a n)")
                                nc.vector.tensor_tensor(sums, sums, acc[:P, par, :, :].rearrange("p a n -> p (a n)"), ALU.add).then_inc(taken, 1)

        def mix_out(MSG):
            with ExitStack() as st:
                sb, pb = tile_in(st), bank_in(st)
                loaded, turned, moved, done, added = sems_in(st)("w_loaded", "turned", "turned_moved", "mixed", "added")
                W = sb("Wout", [128, 4, MUL])
                mT = sb("mT", [128, 2, 8, P])
                turn_ps, ps = pb("turn_ps", [128, 4, 512]), pb("ps", [128, 2, 512])
                with nc.Block() as block:
                    @block.sync
                    def _(sp):
                        sp.dma_start(W[:, 0:2, :], I["L1_gnn_W_out0"].rearrange("(k p) n -> p k n", p=128)).then_inc(loaded, 16)
                        sp.dma_start(W[:, 2:4, :], I["L1_gnn_W_out1"].rearrange("(k p) n -> p k n", p=128)).then_inc(loaded, 16)

                    pairs = [((0, 7), 0)] + [((4 + i, 1 + i), 2) for i in range(3)]

                    @block.tensor
                    def _(pe):
                        pe.wait_ge(loaded, 32)

                        def mix(t):
                            pe.wait_ge(moved, 2 * (t + 1))
                            if t >= 2:
                                pe.wait_ge(added, 2 * (t - 1))
                            for q, (chunks, w) in enumerate(pairs):
                                for n, c in enumerate(chunks):
                                    last = nc.tensor.matmul(ps[:P, t % 2, MUL * q:MUL * (q + 1)], mT[:, t % 2, c, :],
                                                            W[:, w + n, :], start=n == 0, stop=n == 1)
                            last.then_inc(done, 1)

                        for t in range(TILES):
                            if t >= 2:
                                pe.wait_ge(moved, 2 * (t - 1))
                            for half in range(2):
                                for c in range(4):
                                    last = nc.tensor.transpose(turn_ps[:, 2 * (t % 2) + half, P * c:P * (c + 1)],
                                                               MSG[:, t, 128 * (4 * half + c):128 * (4 * half + c + 1)], ident[:P, :P])
                                last.then_inc(turned, 1)
                            if t >= 1:
                                mix(t - 1)
                        mix(TILES - 1)

                    @block.scalar
                    def _(act):
                        for t in range(TILES):
                            if t >= 2:
                                act.wait_ge(done, t - 1)
                            for half in range(2):
                                act.wait_ge(turned, 2 * t + half + 1)
                                nc.scalar.activation(mT[:, t % 2, 4 * half:4 * half + 4, :],
                                                     turn_ps[:, 2 * (t % 2) + half, 0:4 * P].rearrange("p (c n) -> p c n", c=4),
                                                     ACT.Copy).then_inc(moved, 1)

                    @block.vector
                    def _(dve):
                        scale = 1 / (math.sqrt(2 * MUL) * 10.0)
                        for t in range(TILES):
                            dve.wait_ge(done, t + 1)
                            xs, xv = X[:, t, 0:MUL], X[:, t, MUL:DIM].rearrange("p (v m) -> p m v", m=3)
                            nc.vector.scalar_tensor_tensor(out=xs, in0=ps[:P, t % 2, 0:MUL], scalar=scale, in1=xs,
                                                           op0=ALU.mult, op1=ALU.add).then_inc(added, 1)
                            nc.vector.scalar_tensor_tensor(out=xv, in0=ps[:P, t % 2, MUL:DIM].rearrange("p (m v) -> p m v", m=3),
                                                           scalar=scale, in1=xv, op0=ALU.mult, op1=ALU.add).then_inc(added, 1)

        def place_nodes(bestI, slots, expertI):
            with ExitStack() as st:
                sb, pb = tile_in(st), bank_in(st)
                steps, oh_ready, totals = sems_in(st)("place_steps", "one_hots_ready", "totals_ready")
                wide = [P, TILES, EXPERTS]
                idxF = sb("idxF", [P, TILES])
                oh, before_me = sb("oh", wide), sb("before_me", wide)
                n, grp, gI, start = (sb("n", [P, EXPERTS]), sb("grp", [P, EXPERTS]), sb("gI", [P, EXPERTS], I32),
                                     sb("start", [P, EXPERTS]))
                slotF, ef = sb("slotF", [P, TILES]), sb("ef", [P, TT1])
                ps = pb("ps", [128, 2, 512])
                with nc.Block() as block:
                    @block.vector
                    def _(dve):
                        step = Chain(dve, steps)
                        step(nc.vector.tensor_copy(idxF[:], bestI[:, :, 0]))
                        nc.vector.tensor_tensor(oh[:], count[:P, 0:EXPERTS].unsqueeze(1).to_broadcast(wide),
                                                idxF[:].unsqueeze(2).to_broadcast(wide), ALU.is_equal).then_inc(oh_ready, 1)
                        dve.wait_ge(totals, 1)
                        step(nc.vector.tensor_copy(before_me[:], ps[:P, 0, 0:TILES * EXPERTS].rearrange("p (t e) -> p t e", t=TILES)))
                        step(nc.vector.memset(n[:], 0.0))
                        for t in range(TILES):
                            step(nc.vector.tensor_tensor(before_me[:, t, :], before_me[:, t, :], n[:], ALU.add))
                            step(nc.vector.tensor_tensor(n[:], n[:], ps[:P, 1, EXPERTS * t:EXPERTS * (t + 1)], ALU.add))
                        step(nc.vector.tensor_scalar(gI[:], n[:], float(LANES - 1), None, ALU.add))
                        step(nc.vector.tensor_scalar(gI[:], gI[:], int(math.log2(LANES)), None, ALU.arith_shift_right))
                        step(nc.vector.tensor_copy(grp[:], gI[:]))
                        step(nc.vector.tensor_tensor_scan(start[:], ones[:P, 0:EXPERTS], grp[:], 0.0, ALU.mult, ALU.add))
                        step(nc.vector.tensor_tensor(start[:], start[:], grp[:], ALU.subtract))
                        step(nc.vector.tensor_scalar(ef[:], count[:P, 0:TT1], start[:, 1:2], None, ALU.is_ge))
                        for e in range(2, EXPERTS):
                            step(nc.vector.scalar_tensor_tensor(out=ef[:], in0=count[:P, 0:TT1], scalar=start[:, e:e + 1], in1=ef[:],
                                                                op0=ALU.is_ge, op1=ALU.add))
                        step(nc.vector.tensor_copy(expertI[:], ef[:]))
                        step(nc.vector.tensor_scalar(start[:], start[:], float(LANES), None, ALU.mult))
                        step(nc.vector.tensor_tensor(before_me[:], before_me[:], start[:].unsqueeze(1).to_broadcast(wide), ALU.add))
                        step(nc.vector.tensor_tensor(before_me[:], before_me[:], oh[:], ALU.mult))
                        step(nc.vector.tensor_reduce(slotF[:], before_me[:], X_AXIS, ALU.add))
                        step(nc.vector.tensor_copy(slots[:, :, 0], slotF[:]))

                    @block.tensor
                    def _(pe):
                        pe.wait_ge(oh_ready, 1)
                        flat = oh[:].rearrange("p t e -> p (t e)")
                        nc.tensor.matmul(ps[:P, 0, 0:TILES * EXPERTS], before[:P, :P], flat, start=True, stop=True)
                        nc.tensor.matmul(ps[:P, 1, 0:TILES * EXPERTS], ones[:P, :P], flat, start=True, stop=True).then_inc(totals, 1)

        def experts1(expertI):
            UNITS = 4
            ITERS = TT1 // 2
            FC = FF1 // 128
            with ExitStack() as st:
                sb, pb = tile_in(st), bank_in(st)
                loaded = sems_in(st)(*[f"unit_loaded{u}" for u in range(UNITS)])
                stored = sems_in(st)(*[f"unit_stored{u}" for u in range(UNITS)])
                b_loaded, b_turned, b_ready, x_turned, x_moved, hid_done, hid_moved, y_done, y_moved, y_free, tick = sems_in(st)(
                    "b_loaded", "b_turned", "b_ready", "x_turned", "x_moved", "hid_done", "hid_moved", "y_done", "y_moved",
                    "y_free", "tick")
                xe = [sb(f"xe{u}", [128, DIM]) for u in range(UNITS)]
                W1 = [sb(f"W1_{u}", [128, KC, FF1]) for u in range(UNITS)]
                W2 = [sb(f"W2_{u}", [128, FC, DIM]) for u in range(UNITS)]
                b2B = [sb(f"b2B{u}", [128, DIM]) for u in range(UNITS)]
                ye = [sb(f"ye{u}", [128, DIM]) for u in range(UNITS)]
                b1raw, b1T = sb("b1raw", [2 * EXPERTS * FC, 128]), sb("b1T", [128, 2 * EXPERTS, FC])
                xT, hid = sb("xT", [128, 2, KC, 128]), sb("hid", [128, 2, FC, 128])
                turn_ps, hid_ps, y_ps = pb("turn_ps", [128, 2, 512]), pb("hid_ps", [128, 2, 512]), pb("y_ps", [128, 2, 512])
                with nc.Block() as block:
                    def expert_of(engine, r, u):
                        b = u % 2
                        return engine.value_load(expertI[b][0:1, bass.ds(2 * r + u // 2, 1)], min_val=0, max_val=EXPERTS - 1)

                    @block.sync
                    def _(sp):
                        for b, bank in enumerate(BANKS):
                            n = EXPERTS * FC
                            sp.dma_start(b1raw[n * b:n * (b + 1), :], I[f"L1_ffn_b1_{bank}"].rearrange("e (m p) -> (e m) p", p=128)
                                         ).then_inc(b_loaded, 16)
                        sp.sem_inc(y_moved, UNITS)
                        with sp.Fori(0, ITERS) as r:
                            for u in range(UNITS):
                                bank = BANKS[u % 2]
                                e = expert_of(sp, r, u)
                                sp.wait_ge(y_moved, UNITS * r + u + 1)
                                sp.sem_inc(tick, 1)
                                sp.dma_start(xe[u][:], xin1[bank][bass.ds((2 * r + u // 2) * LANES, LANES), :]).then_inc(loaded[u], 16)
                                sp.dma_start(W1[u][:], I[f"L1_ffn_W1_{bank}"][bass.ds(e, 1)].rearrange("a (k p) n -> p (a k) n", p=128)
                                             ).then_inc(loaded[u], 16)
                                sp.dma_start(W2[u][:], I[f"L1_ffn_W2_{bank}"][bass.ds(e, 1)].rearrange("a (k p) n -> p (a k) n", p=128)
                                             ).then_inc(loaded[u], 16)
                                sp.dma_start(b2B[u][:], I[f"L1_ffn_b2_{bank}"][bass.ds(e, 1), :].broadcast_to([128, DIM])
                                             ).then_inc(loaded[u], 16)

                    @block.gpsimd
                    def _(pool):
                        with pool.Fori(0, ITERS) as r:
                            for u in range(UNITS):
                                pool.wait_ge(y_moved, UNITS * (r + 1) + u + 1)
                                pool.sem_inc(tick, 1)
                                pool.dma_start(yout1[BANKS[u % 2]][bass.ds((2 * r + u // 2) * LANES, LANES), :], ye[u][:]
                                               ).then_inc(stored[u], 16)
                                pool.wait_ge(stored[u], 16 * (r + 1))
                                pool.sem_inc(y_free, 1)

                    @block.tensor
                    def _(pe):
                        pe.wait_ge(b_loaded, 32)
                        nb = 2 * EXPERTS * FC
                        nc.tensor.transpose(y_ps[:, 0, 0:nb], b1raw[:], ident[:nb, :nb]).then_inc(b_turned, 1)
                        pe.wait_ge(b_ready, 1)

                        def turn(r, u):
                            n = UNITS * r + u
                            pe.wait_ge(loaded[u], 64 * (r + 1))
                            if u >= 2:
                                pe.wait_ge(x_moved, n - 1)
                            for k in range(KC):
                                last = nc.tensor.transpose(turn_ps[:, u % 2, 128 * k:128 * (k + 1)],
                                                           xe[u][:, 128 * k:128 * (k + 1)], ident[:])
                            last.then_inc(x_turned, 1)

                        def up(r, u):
                            n = UNITS * r + u
                            pe.wait_ge(x_moved, n + 1)
                            for m in range(FC):
                                for k in range(KC):
                                    last = nc.tensor.matmul(hid_ps[:, u % 2, 128 * m:128 * (m + 1)], W1[u][:, k, 128 * m:128 * (m + 1)],
                                                            xT[:, u % 2, k, :], start=k == 0, stop=k == KC - 1)
                            last.then_inc(hid_done, 1)

                        def down(r, u):
                            n = UNITS * r + u
                            pe.wait_ge(hid_moved, FC * (n + 1))
                            pe.wait_ge(y_moved, n - 2 + UNITS + 1)
                            for m in range(FC):
                                last = nc.tensor.matmul(y_ps[:, u % 2, :], hid[:, u % 2, m, :], W2[u][:, m, :],
                                                        start=m == 0, stop=m == FC - 1)
                            last.then_inc(y_done, 1)

                        with pe.Fori(0, ITERS) as r:
                            for s in range(UNITS + 2):
                                if s < UNITS:
                                    turn(r, s)
                                if 1 <= s <= UNITS:
                                    up(r, s - 1)
                                if s >= 2:
                                    down(r, s - 2)

                    @block.scalar
                    def _(act):
                        act.wait_ge(b_turned, 1)
                        nc.scalar.activation(b1T[:], y_ps[:, 0, 0:2 * EXPERTS * FC].rearrange("p (e m) -> p e m", m=FC),
                                             ACT.Copy).then_inc(b_ready, 1)
                        act.wait_ge(b_ready, 1)
                        with act.Fori(0, ITERS) as r:
                            for s in range(UNITS + 1):
                                if s < UNITS:
                                    n = UNITS * r + s
                                    act.wait_ge(x_turned, n + 1)
                                    if s >= 2:
                                        act.wait_ge(hid_done, n - 1)
                                    nc.scalar.activation(xT[:, s % 2, :, :], turn_ps[:, s % 2, :].rearrange("p (k n) -> p k n", k=KC),
                                                         ACT.Copy).then_inc(x_moved, 1)
                                if s >= 1:
                                    u = s - 1
                                    n = UNITS * r + u
                                    e = expert_of(act, r, u)
                                    act.wait_ge(hid_done, n + 1)
                                    if u >= 2:
                                        act.wait_ge(y_done, n - 1)
                                    for m in range(FC):
                                        nc.scalar.activation(hid[:, u % 2, m, :], hid_ps[:, u % 2, 128 * m:128 * (m + 1)], ACT.Gelu,
                                                             bias=b1T[:, bass.ds(e + EXPERTS * (u % 2), 1), m:m + 1].rearrange("p a b -> p (a b)")
                                                             ).then_inc(hid_moved, 1)

                    @block.vector
                    def _(dve):
                        dve.sem_inc(y_free, UNITS)
                        with dve.Fori(0, ITERS) as r:
                            for u in range(UNITS):
                                dve.wait_ge(y_done, UNITS * r + u + 1)
                                dve.wait_ge(y_free, UNITS * r + u + 1)
                                nc.vector.tensor_tensor(ye[u][:], y_ps[:, u % 2, :], b2B[u][:], ALU.add).then_inc(y_moved, 1)

        def move(target, source):
            with ExitStack() as st:
                (moved,) = sems_in(st)("array_moved")
                with nc.Block() as block:
                    @block.sync
                    def _(sp):
                        sp.dma_start(target, source).then_inc(moved, 16)
                        sp.wait_ge(moved, 16)

        RECS = sb("RECS", [128, GROUPS + 1, EPP, REC])
        whole_x = I["x"].rearrange("(t p) d -> p t d", p=P)

        with ExitStack() as outer:
            A = tile_in(outer)("A", [P, TILES, DIM])
            with ExitStack() as attention:
                sb1 = tile_in(attention)
                QT, KT, V = sb1("QT", [128, KC, NODES]), sb1("KT", [128, KC, NODES]), sb1("V", [P, TILES, DIM])
                with ExitStack() as early:
                    sb2 = tile_in(early)
                    pos, recs = sb2("pos", [P, ECOLS], I32), sb2("recs", [P, ECOLS, REC])
                    order_edges(pos, recs)
                    layer_norm(X, X)
                    HT = sb2("HT", [128, KC, NODES])
                    transpose_all(X, HT)
                    qkv_and_scatter(HT, QT, KT, V, pos, recs)
                LA, has = sb1("LA", [P, TILES, NODES]), sb1("has", [P, TILES])
                count_edges(LA, has, RECS)
                attend(QT, KT, V, LA, has, A)
            with ExitStack() as post:
                sb1 = tile_in(post)
                T, R, hT = sb1("T", [128, KC, NODES]), sb1("R", [P, TILES, DIM]), sb1("hT", [128, 2, NODES])
                transpose_all(A, T)
                node_major_product(T, I["L0_gnn_Wo"], KC, R, add=X)
                layer_norm(R, R, I["L0_gnn_ln1_g"], I["L0_gnn_ln1_b"])
                transpose_all(R, T)
                feature_major_layer(T, I["L0_gnn_W1"], I["L0_gnn_b1"], hT, 2, ACT.Relu)
                node_major_product(hT, I["L0_gnn_W2"], 2, R, bias=I["L0_gnn_b2"], add=R)
                move(X[:], whole_x)
                layer_norm(R, R, I["L0_gnn_ln2_g"], I["L0_gnn_ln2_b"], add_to=X)
        recycle()
        with ExitStack() as moe:
            sb1 = tile_in(moe)
            best, bestI = sb1("best", [P, TILES, 8]), sb1("bestI", [P, TILES, 8], U32)
            weight = sb1("weight", [P, TILES, 2])
            slot_in, slot_out = sb1("slot_in", [P, TILES, 2], I32), sb1("slot_out", [P, TILES, 2], I32)
            with ExitStack() as routing:
                sb2 = tile_in(routing)
                N, NT, probs = sb2("N", [P, TILES, DIM]), sb2("NT", [128, KC, NODES]), sb2("probs", [P, TILES, EXPERTS])
                layer_norm(X, N)
                transpose_all(N, NT)
                gate(NT, I["L0_ffn_gate_w"], True, I["L0_ffn_gate_b"], probs, best, bestI)
                place_choices(best, bestI, weight, slot_in, slot_out)
                scatter_rows(N, slot_in, 2, xin0)
            experts0()
            combine([(yout0, lambda t, c=c: slot_out[:, t, c:c + 1], lambda t, c=c: weight[:, t, c:c + 1]) for c in range(2)])
        recycle()
        with ExitStack() as graph:
            sb1 = tile_in(graph)
            with ExitStack() as up:
                sb2 = tile_in(up)
                N, NT = sb2("N", [P, TILES, DIM]), sb2("NT", [128, KC, NODES])
                layer_norm(X, N)
                transpose_all(N, NT, [lambda t: N[:, t, 0:MUL]] + [lambda t, m=m: N[:, t, MUL + m:DIM:3] for m in range(3)])
                mix_up(NT)
            MSG = sb1("MSG", [P, TILES, 2 * DIM])
            messages(RECS, MSG)
            mix_out(MSG)
        with ExitStack() as ffn:
            sb1 = tile_in(ffn)
            gates, slots, experts = [], [], []
            for b in range(2):
                gates.append(sb1(f"best{b}", [P, TILES, 8]))
                slots.append(sb1(f"slots{b}", [P, TILES, 1], I32))
                experts.append(sb1(f"expertI{b}", [P, TT1], I32))
            with ExitStack() as routing:
                sb2 = tile_in(routing)
                N, NT, hT = sb2("N", [P, TILES, DIM]), sb2("NT", [128, KC, NODES]), sb2("hT", [128, 2, NODES])
                probs, bestI = sb2("probs", [P, TILES, EXPERTS]), sb2("bestI", [P, TILES, 8], U32)
                layer_norm(X, N)
                transpose_all(N, NT)
                for b, bank in enumerate(BANKS):
                    gate(NT, I[f"L1_ffn_Wr_{bank}"], False, I[f"L1_ffn_br_{bank}"], probs, gates[b], bestI)
                    place_nodes(bestI, slots[b], experts[b])
                    scatter_rows(N, slots[b], 1, xin1[bank])
                feature_major_layer(NT, I["L1_ffn_Ws1"], I["L1_ffn_bs1"], hT, 2, ACT.Gelu)
                node_major_product(hT, I["L1_ffn_Ws2"], 2, X, bias=I["L1_ffn_bs2"], add=X)
            experts1(experts)
            combine([(yout1[bank], lambda t, b=b: slots[b][:, t, 0:1], lambda t, b=b: gates[b][:, t, 0:1])
                     for b, bank in enumerate(BANKS)])
        move(out.rearrange("(t p) d -> p t d", p=P), X[:])


_INS = ['x', 'src', 'dst', 'edge_attr_4', 'edge_attr_8', 'L0_gnn_Wq', 'L0_gnn_Wk', 'L0_gnn_Wv', 'L0_gnn_Wo',
        'L0_gnn_ln1_g', 'L0_gnn_ln1_b', 'L0_gnn_ln2_g', 'L0_gnn_ln2_b', 'L0_gnn_W1', 'L0_gnn_b1', 'L0_gnn_W2',
        'L0_gnn_b2', 'L0_ffn_gate_w', 'L0_ffn_gate_b', 'L0_ffn_w1', 'L0_ffn_b1', 'L0_ffn_w2', 'L0_ffn_b2',
        'L1_gnn_W_up0', 'L1_gnn_W_up1', 'L1_gnn_W_mlp1', 'L1_gnn_W_mlp2', 'L1_gnn_W_mlp3', 'L1_gnn_W_mlp4',
        'L1_gnn_W_out0', 'L1_gnn_W_out1', 'L1_ffn_Wr_sp', 'L1_ffn_br_sp', 'L1_ffn_Wr_fq', 'L1_ffn_br_fq',
        'L1_ffn_Ws1', 'L1_ffn_bs1', 'L1_ffn_Ws2', 'L1_ffn_bs2', 'L1_ffn_W1_sp', 'L1_ffn_b1_sp', 'L1_ffn_W2_sp',
        'L1_ffn_b2_sp', 'L1_ffn_W1_fq', 'L1_ffn_b1_fq', 'L1_ffn_W2_fq', 'L1_ffn_b2_fq']


def kernel(**inputs):
    import numpy as _np
    import concourse.bacc as _bacc
    from concourse import mybir as _mybir
    from concourse.bass_utils import run_bass_kernel_spmd as _run

    nc = _bacc.Bacc("TRN2", target_bir_lowering=False, num_devices=1)
    arrays, args = {}, {}
    for name in _INS:
        a = _np.ascontiguousarray(inputs[name])
        arrays[f"in_{name}"] = a
        args[name] = nc.dram_tensor(f"in_{name}", a.shape, _mybir.dt.from_np(a.dtype), kind="ExternalInput").ap()
    out = nc.dram_tensor("out_0", (NODES, DIM), F32, kind="ExternalOutput").ap()
    gnn_moe_gnn_moe(nc, args, out)
    return _run(nc, [arrays], core_ids=[0]).results[0]["out_0"]
```

```python
import math
from contextlib import ExitStack

import concourse.bass as bass
from concourse import mybir

F32 = mybir.dt.float32
F16 = mybir.dt.float16
F32R = mybir.dt.float32r
I32 = mybir.dt.int32
U32 = mybir.dt.uint32
ALU = mybir.AluOpType
ACT = mybir.ActivationFunctionType
X_AXIS = mybir.AxisListType.X

NODES, DIM, EDGES = 1250, 512, 20000
P = 125
TILES = NODES // P
KC = DIM // 128
HEADS, DK = 8, 64
ECOLS = EDGES // P
LANES, EPP = 128, 4
GROUP = LANES * EPP
GROUPS = (EDGES + TILES * (GROUP - 1)) // GROUP
GROUPS += GROUPS % 2
SLOTS = GROUPS * GROUP
REC = 16
NEG = -1e30
EPS = 1e-5
CHUNKS = [(0, 512), (512, 512), (1024, NODES - 1024)]
EXPERTS = 8
CAP0 = int(1.2 * NODES / EXPERTS)
ROWS0 = CAP0 + 1
HALF0 = ROWS0 // 2
HID0 = 2048
MC0 = HID0 // 128
FF1 = 256
TT1 = (NODES + EXPERTS * (LANES - 1)) // LANES
TT1 += TT1 % 2
ROWS1 = TT1 * LANES
BANKS = ("sp", "fq")
SILU_2MOM = 1.679177
MUL = 128


class Chain:

    def __init__(self, engine, done):
        self.engine, self.done, self.n = engine, done, 0

    def __call__(self, instruction):
        instruction.then_inc(self.done, 1)
        self.n += 1
        self.engine.wait_ge(self.done, self.n)


def gnn_moe_gnn_moe(nc, I, out):
    top = ExitStack()

    used = {}

    def fresh(name):
        used[name] = used.get(name, 0) + 1
        return name if used[name] == 1 else f"{name}_{used[name]}"

    def tile_in(stack):
        return lambda name, shape, dt=F32: stack.enter_context(nc.sbuf_tensor(fresh(name), shape, dt))

    def bank_in(stack):
        return lambda name, shape, dt=F32: stack.enter_context(nc.psum_tensor(fresh(name), shape, dt))

    finished = []

    def sems_in(stack):
        def allocate(*names):
            handles = [nc.alloc_semaphore(name=fresh(n)) for n in names]
            stack.callback(finished.extend, handles)
            return handles
        return allocate

    def recycle():
        nc.clear_and_free_semaphores(finished)
        finished.clear()
        nc.all_engine_barrier()

    def row(ap):
        return ap.rearrange("(a n) -> a n", a=1)

    def dram(name, shape, dt=F32):
        return nc.dram_tensor(name, shape, dt, kind="Internal").ap()

    rec_dram = dram("rec_dram", (SLOTS, REC))
    up_dram = dram("up_dram", (NODES, DIM))
    xin0 = dram("xin0", (EXPERTS * ROWS0 + 2 * NODES, DIM))
    yout0 = dram("yout0", (EXPERTS * ROWS0, DIM))
    xin1 = {b: dram("xin1_" + b, (ROWS1, DIM)) for b in BANKS}
    yout1 = {b: dram("yout1_" + b, (ROWS1, DIM)) for b in BANKS}

    with top:
        sb = tile_in(top)
        X = sb("X", [P, TILES, DIM])
        ident = sb("ident", [128, 128])
        ones = sb("ones", [128, 128])
        before = sb("before", [128, 128])
        earlier = sb("earlier", [128, 128])
        zeros = sb("zeros", [128, DIM])
        count = sb("count", [128, 64])
        tiny = sb("tiny", [128, 1])
        blockI = sb("blockI", [P, GROUPS + 1], I32)

        def order_edges(pos, recs):
            with ExitStack() as st:
                sb, pb = tile_in(st), bank_in(st)
                loaded, consts, routed, rows_ready, totals, filled, fill_ready = sems_in(st)(
                    "edges_loaded", "consts_ready", "routed", "rows_ready", "totals_ready", "rec_filled", "fill_ready")
                srcI, dstI = sb("srcI", [P, ECOLS], I32), sb("dstI", [P, ECOLS], I32)
                a4, a8 = sb("a4", [P, ECOLS, 4]), sb("a8", [P, ECOLS, 8])
                dstF = sb("dstF", [P, ECOLS])
                ge = sb("ge", [P, TILES + 1, ECOLS])
                oh = sb("oh", [P, TILES, ECOLS])
                cum = sb("cum", [P, TILES, ECOLS])
                blk = sb("blk", [P, ECOLS])
                onesE = sb("onesE", [P, ECOLS])
                base, grp, gI, start = (sb("base", [P, TILES]), sb("grp", [P, TILES]),
                                        sb("gI", [P, TILES], I32), sb("start", [P, TILES]))
                rows = sb("rows", [P, TILES])
                posF = sb("posF", [P, ECOLS])
                bf = sb("bf", [P, GROUPS])
                fill = sb("fill", [128, SLOTS // 128, REC])
                ps = pb("ps", [128, 2, 512])
                with nc.Block() as block:
                    @block.sync
                    def _(sp):
                        sp.dma_start(srcI[:], I["src"].rearrange("(p c) -> p c", p=P)).then_inc(loaded, 16)
                        sp.dma_start(dstI[:], I["dst"].rearrange("(p c) -> p c", p=P)).then_inc(loaded, 16)
                        sp.dma_start(a4[:], I["edge_attr_4"].rearrange("(p c) f -> p c f", p=P)).then_inc(loaded, 16)
                        sp.dma_start(a8[:], I["edge_attr_8"].rearrange("(p c) f -> p c f", p=P)).then_inc(loaded, 16)
                        sp.dma_start(X[:], I["x"].rearrange("(t p) d -> p t d", p=P)).then_inc(loaded, 16)
                        sp.wait_ge(fill_ready, 1)
                        sp.dma_start(rec_dram.rearrange("(p c) w -> p c w", p=128), fill[:]).then_inc(filled, 16)
                        sp.wait_ge(loaded, 80)
                        sp.wait_ge(filled, 16)

                    @block.gpsimd
                    def _(pool):
                        nc.gpsimd.memset(ident[:], 0.0)
                        nc.gpsimd.memset(before[:], 0.0)
                        nc.gpsimd.memset(earlier[:], 0.0)
                        nc.gpsimd.memset(ones[:], 1.0)
                        nc.gpsimd.memset(zeros[:], 0.0)
                        nc.gpsimd.memset(tiny[:], EPS)
                        nc.gpsimd.memset(onesE[:], 1.0)
                        nc.gpsimd.iota(count[:], pattern=[[1, 64]], base=0, channel_multiplier=0,
                                       allow_small_or_imprecise_dtypes=True).then_inc(consts, 1)
                        pool.wait_ge(consts, 1)
                        nc.gpsimd.affine_select(out=ident[:], in_=ident[:], compare_op=ALU.not_equal, fill=1.0,
                                                base=0, pattern=[[-1, 128]], channel_multiplier=1)
                        nc.gpsimd.affine_select(out=before[:], in_=before[:], compare_op=ALU.is_ge, fill=1.0,
                                                base=0, pattern=[[-1, 128]], channel_multiplier=1)
                        nc.gpsimd.affine_select(out=earlier[:], in_=earlier[:], compare_op=ALU.is_ge, fill=1.0,
                                                base=0, pattern=[[1, 128]], channel_multiplier=-1).then_inc(consts, 1)

                    @block.vector
                    def _(dve):
                        step = Chain(dve, routed)
                        step(nc.vector.memset(fill[:], 0.0))
                        nc.vector.memset(fill[:, :, 1:2], -1.0).then_inc(fill_ready, 1)
                        dve.wait_ge(loaded, 80)
                        step(nc.vector.tensor_copy(dstF[:], dstI[:]))
                        step(nc.vector.tensor_copy(recs[:, :, 0], srcI[:]))
                        for b in range(TILES):
                            nc.vector.tensor_scalar(ge[:, b, :], dstF[:], float(P * b), None, ALU.is_ge)
                        nc.vector.tensor_copy(recs[:, :, 4:8], a4[:])
                        nc.vector.tensor_copy(recs[:, :, 8:16], a8[:])
                        nc.vector.memset(recs[:, :, 2:4], 0.0)
                        step(nc.vector.memset(ge[:, TILES, :], 0.0))
                        step(nc.vector.tensor_tensor(oh[:], ge[:, 0:TILES, :], ge[:, 1:TILES + 1, :], ALU.subtract))
                        step(nc.vector.tensor_reduce(blk[:], ge[:, 1:TILES, :].rearrange("p b c -> p c b"), X_AXIS, ALU.add))
                        step(nc.vector.scalar_tensor_tensor(out=recs[:, :, 1], in0=blk[:], scalar=-float(P), in1=dstF[:],
                                                            op0=ALU.mult, op1=ALU.add))
                        dve.wait_ge(consts, 2)
                        for b in range(TILES):
                            scan = nc.vector.tensor_tensor_scan(cum[:, b, :], onesE[:], oh[:, b, :], 0.0, ALU.mult, ALU.add)
                        step(scan)
                        nc.vector.tensor_copy(rows[:], cum[:, :, ECOLS - 1]).then_inc(rows_ready, 1)
                        dve.wait_ge(totals, 1)
                        step(nc.vector.tensor_scalar(gI[:], ps[:P, 1, 0:TILES], float(GROUP - 1), None, ALU.add))
                        step(nc.vector.tensor_scalar(gI[:], gI[:], int(math.log2(GROUP)), None, ALU.arith_shift_right))
                        step(nc.vector.tensor_copy(grp[:], gI[:]))
                        step(nc.vector.tensor_tensor_scan(start[:], onesE[:, 0:TILES], grp[:], 0.0, ALU.mult, ALU.add))
                        step(nc.vector.tensor_tensor(start[:], start[:], grp[:], ALU.subtract))
                        step(nc.vector.scalar_tensor_tensor(out=base[:], in0=start[:], scalar=float(GROUP),
                                                            in1=ps[:P, 0, 0:TILES], op0=ALU.mult, op1=ALU.add))
                        for b in range(TILES):
                            nc.vector.scalar_tensor_tensor(out=ge[:, b, :], in0=cum[:, b, :], scalar=base[:, b:b + 1],
                                                           in1=oh[:, b, :], op0=ALU.add, op1=ALU.mult)
                        step(nc.vector.tensor_scalar(bf[:], count[:P, 0:GROUPS], start[:, 1:2], None, ALU.is_ge))
                        step(nc.vector.tensor_reduce(posF[:], ge[:, 0:TILES, :].rearrange("p b c -> p c b"), X_AXIS, ALU.add))
                        step(nc.vector.tensor_scalar(pos[:], posF[:], -1.0, None, ALU.add))
                        for b in range(2, TILES):
                            step(nc.vector.scalar_tensor_tensor(out=bf[:], in0=count[:P, 0:GROUPS], scalar=start[:, b:b + 1],
                                                                in1=bf[:], op0=ALU.is_ge, op1=ALU.add))
                        nc.vector.memset(blockI[:, 0:1], 0)
                        step(nc.vector.tensor_copy(blockI[:, 1:GROUPS + 1], bf[:]))

                    @block.tensor
                    def _(pe):
                        pe.wait_ge(consts, 2)
                        pe.wait_ge(rows_ready, 1)
                        nc.tensor.matmul(ps[:P, 0, 0:TILES], before[:P, :P], rows[:], start=True, stop=True)
                        nc.tensor.matmul(ps[:P, 1, 0:TILES], ones[:P, :P], rows[:], start=True, stop=True).then_inc(totals, 1)

        def layer_norm(src, dst, gain=None, shift=None, add_to=None, pool_work=None):
            with ExitStack() as st:
                sb = tile_in(st)
                stats_done, root_done, steps, params = sems_in(st)("ln_stats", "ln_root", "ln_steps", "ln_params")
                stats = sb("stats", [P, TILES, 6])
                mv = sb("mv", [P, TILES, 2])
                root, rstd = sb("root", [P, TILES]), sb("rstd", [P, TILES])
                if gain is not None:
                    gainB, shiftB = sb("gainB", [P, DIM]), sb("shiftB", [P, DIM])
                with nc.Block() as block:
                    if pool_work is not None:
                        block.gpsimd(pool_work)

                    if gain is not None:
                        @block.sync
                        def _(sp):
                            sp.dma_start(gainB[:], row(gain).broadcast_to([P, DIM])).then_inc(params, 16)
                            sp.dma_start(shiftB[:], row(shift).broadcast_to([P, DIM])).then_inc(params, 16)

                    @block.vector
                    def _(dve):
                        step = Chain(dve, steps)
                        for t in range(TILES):
                            stat = nc.vector.bn_stats(stats[:, t, :], src[:, t, :])
                        step(stat)
                        for t in range(TILES):
                            aggr = nc.vector.bn_aggr(mv[:, t, :], stats[:, t, :])
                        aggr.then_inc(stats_done, 1)
                        dve.wait_ge(root_done, 1)
                        step(nc.vector.reciprocal(rstd[:], root[:]))
                        if gain is not None:
                            dve.wait_ge(params, 32)
                        for t in range(TILES):
                            last = nc.vector.tensor_scalar(dst[:, t, :], src[:, t, :], mv[:, t, 0:1], rstd[:, t:t + 1],
                                                           ALU.subtract, ALU.mult)
                        step(last)
                        if gain is not None:
                            for t in range(TILES):
                                last = nc.vector.tensor_tensor(dst[:, t, :], dst[:, t, :], gainB[:], ALU.mult)
                            step(last)
                            for t in range(TILES):
                                last = nc.vector.tensor_tensor(dst[:, t, :], dst[:, t, :], shiftB[:], ALU.add)
                            step(last)
                        if add_to is not None:
                            for t in range(TILES):
                                last = nc.vector.tensor_tensor(add_to[:, t, :], dst[:, t, :], add_to[:, t, :], ALU.add)
                            step(last)

                    @block.scalar
                    def _(act):
                        act.wait_ge(stats_done, 1)
                        nc.scalar.activation(root[:], mv[:, :, 1], ACT.Sqrt, bias=tiny[:P, :]).then_inc(root_done, 1)

        def transpose_all(src, dst, chunks=None, pool_work=None):
            chunks = chunks or [lambda t, k=k: src[:, t, 128 * k:128 * (k + 1)] for k in range(KC)]
            with ExitStack() as st:
                ps = bank_in(st)("ps", [128, 4, 512])
                turned, moved = sems_in(st)("turned", "moved")
                n = len(chunks)
                with nc.Block() as block:
                    if pool_work is not None:
                        block.gpsimd(pool_work)

                    @block.tensor
                    def _(pe):
                        for t in range(TILES):
                            if t >= 4:
                                pe.wait_ge(moved, t - 3)
                            for k in range(n):
                                last = nc.tensor.transpose(ps[:, t % 4, P * k:P * (k + 1)], chunks[k](t), ident[:P, :P])
                            last.then_inc(turned, 1)

                    @block.scalar
                    def _(act):
                        for t in range(TILES):
                            act.wait_ge(turned, t + 1)
                            nc.scalar.activation(dst[:, :, P * t:P * (t + 1)],
                                                 ps[:, t % 4, 0:n * P].rearrange("p (k c) -> p k c", k=n),
                                                 ACT.Copy).then_inc(moved, 1)

        def record_scatter(stack, pos, recs):
            COLS = 4
            staged, tick = sems_in(stack)("rec_staged", "tick")
            scattered = sems_in(stack)("rec_scattered0", "rec_scattered1")
            pos_st = [tile_in(stack)(f"pos_st{b}", [P, COLS], I32) for b in range(2)]
            rec_st = [tile_in(stack)(f"rec_st{b}", [P, COLS, REC]) for b in range(2)]

            def columns(pool, c, b, first):
                m = 2 * c + b
                if not first:
                    pool.wait_ge(scattered[b], 16 * COLS * c)
                    pool.sem_inc(tick, 1)
                nc.gpsimd.tensor_copy(pos_st[b][:], pos[:, bass.ds(m * COLS, COLS)]).then_inc(staged, 1)
                nc.gpsimd.tensor_copy(rec_st[b][:], recs[:, bass.ds(m * COLS, COLS), :]).then_inc(staged, 1)
                pool.wait_ge(staged, 2 * (m + 1))
                pool.sem_inc(tick, 1)
                for k in range(COLS):
                    pool.indirect_dma_start(
                        out=rec_dram, out_offset=bass.IndirectOffsetOnAxis(ap=pos_st[b][:, k:k + 1], axis=0),
                        in_=rec_st[b][:, k, :], in_offset=None).then_inc(scattered[b], 16)

            def part(first, end):
                def program(pool):
                    start = first
                    if start == 0:
                        for b in range(2):
                            columns(pool, 0, b, True)
                        start = 1
                    with pool.Fori(start, end) as c:
                        for b in range(2):
                            columns(pool, c, b, False)
                    if end * 2 * COLS == ECOLS:
                        for b in range(2):
                            pool.wait_ge(scattered[b], 8 * ECOLS)
                return program

            return part

        def qkv(HT, QT, KT, V, pool_work):
            with ExitStack() as st:
                sb, pb = tile_in(st), bank_in(st)
                wload, done, moved = sems_in(st)("w_loaded", "product_done", "product_moved")
                W = [sb(f"Wqkv{i}", [128, KC, DIM]) for i in range(3)]
                ps = pb("ps", [128, 8, 512])
                jobs = []
                for which in range(2):
                    for j in range(KC):
                        for c0, cn in CHUNKS:
                            jobs.append((which, j, c0, cn))
                for t in range(TILES):
                    jobs.append((2, t, 0, DIM))

                def target(job):
                    which, j, c0, cn = job
                    return V[:, j, :] if which == 2 else (QT, KT)[which][:, j, c0:c0 + cn]

                with nc.Block() as block:
                    @block.sync
                    def _(sp):
                        for i, name in enumerate(("L0_gnn_Wq", "L0_gnn_Wk", "L0_gnn_Wv")):
                            sp.dma_start(W[i][:], I[name].rearrange("(k p) n -> p k n", p=128)).then_inc(wload, 16)

                    block.gpsimd(pool_work)

                    @block.tensor
                    def _(pe):
                        pe.wait_ge(wload, 48)
                        for n, (which, j, c0, cn) in enumerate(jobs):
                            if n >= 8:
                                pe.wait_ge(moved, n - 7)
                            for k in range(KC):
                                if which < 2:
                                    last = nc.tensor.matmul(ps[:, n % 8, 0:cn], W[which][:, k, 128 * j:128 * (j + 1)],
                                                            HT[:, k, c0:c0 + cn], start=k == 0, stop=k == KC - 1)
                                else:
                                    last = nc.tensor.matmul(ps[:P, n % 8, :], HT[:, k, P * j:P * (j + 1)],
                                                            W[2][:, k, :], start=k == 0, stop=k == KC - 1)
                            last.then_inc(done, 1)

                    @block.scalar
                    def _(act):
                        for n, job in enumerate(jobs):
                            act.wait_ge(done, n + 1)
                            parts = 128 if job[0] < 2 else P
                            scale = 1.0 / math.sqrt(DK) if job[0] == 0 else 1.0
                            nc.scalar.activation(target(job), ps[:parts, n % 8, 0:job[3]], ACT.Copy,
                                                 scale=scale).then_inc(moved, 1)

        def count_edges(LA, has, RECS):
            with ExitStack() as st:
                sb, pb = tile_in(st), bank_in(st)
                loaded, cols, hot, counted, added, cleared, zeroed = sems_in(st)(
                    "recs_loaded", "cols_ready", "one_hots_ready", "counted", "counts_added", "cleared", "zeroed")
                RING = 4
                nodes16 = sb("nodes16", [128, NODES], F16)
                ohS, ohD = sb("ohS", [128, RING, NODES], F16), sb("ohD", [128, RING, P], F16)
                ps = pb("ps", [128, 2, 2048])
                with nc.Block() as block:
                    @block.sync
                    def _(sp):
                        sp.dma_start(RECS[:, 0:GROUPS], rec_dram.rearrange("(g p t) w -> p g t w", p=128, t=EPP)).then_inc(loaded, 16)
                        zeros_in = fill_zeros(sp, xin0, zeroed)
                        for bank in BANKS:
                            zeros_in += fill_zeros(sp, xin1[bank], zeroed)
                        sp.wait_ge(zeroed, zeros_in)

                    @block.gpsimd
                    def _(pool):
                        nc.gpsimd.iota(nodes16[:], pattern=[[1, NODES]], base=0, channel_multiplier=0,
                                       allow_small_or_imprecise_dtypes=True).then_inc(cols, 1)
                        nc.gpsimd.memset(RECS[:, GROUPS, :, :], 0.0)

                    @block.vector
                    def _(dve):
                        def add_counts(block, g, par):
                            dve.wait_ge(counted, EPP * g + RING)
                            dve.wait_ge(added, g + 1)
                            acc = LA[:, bass.ds(block, 1), :].rearrange("p a n -> p (a n)")
                            nc.vector.tensor_tensor(acc, acc, ps[:P, par, 0:NODES], ALU.add).then_inc(added, 1)

                        nc.vector.memset(ps[:, 1, 0:NODES], 0.0).then_inc(added, 1)
                        nc.vector.memset(LA[:], 0.0).then_inc(cleared, 1)
                        dve.wait_ge(cols, 1)
                        dve.wait_ge(loaded, 16)
                        dve.wait_ge(cleared, 1)
                        with dve.Fori(0, GROUPS // 2) as r:
                            for par in range(2):
                                g = 2 * r + par
                                block_before = dve.value_load(blockI[0:1, bass.ds(g, 1)], min_val=0, max_val=TILES - 1)
                                for t in range(EPP):
                                    dve.wait_ge(counted, EPP * g + t + 1)
                                    nc.vector.tensor_scalar(ohS[:, t, :], nodes16[:], RECS[:, bass.ds(g, 1), t, 0:1].rearrange("p a b -> p (a b)"),
                                                            None, ALU.is_equal)
                                    nc.vector.tensor_scalar(ohD[:, t, :], nodes16[:, 0:P], RECS[:, bass.ds(g, 1), t, 1:2].rearrange("p a b -> p (a b)"),
                                                            None, ALU.is_equal).then_inc(hot, 1)
                                    if t == 1:
                                        add_counts(block_before, g, 1 - par)
                        add_counts(dve.value_load(blockI[0:1, GROUPS:GROUPS + 1], min_val=0, max_val=TILES - 1), GROUPS, 1)

                    @block.tensor
                    def _(pe):
                        pe.sem_inc(counted, RING)
                        with pe.Fori(0, GROUPS // 2) as r:
                            for par in range(2):
                                g = 2 * r + par
                                for t in range(EPP):
                                    pe.wait_ge(hot, EPP * g + t + 1)
                                    if t == 0:
                                        pe.wait_ge(added, g + 1)
                                    for c0, cn in CHUNKS:
                                        last = nc.tensor.matmul(ps[:P, par, c0:c0 + cn], ohD[:, t, :], ohS[:, t, c0:c0 + cn],
                                                                start=t == 0, stop=t == EPP - 1)
                                    last.then_inc(counted, 1)

            with ExitStack() as st:
                sb = tile_in(st)
                least, logs, done = sems_in(st)("counts_floored", "logs_ready", "log_steps")
                low, lg = sb("low", [P, 2, NODES]), sb("lg", [P, 2, NODES])
                with nc.Block() as block:
                    @block.vector
                    def _(dve):
                        step = Chain(dve, done)
                        for t in range(TILES):
                            step(nc.vector.tensor_reduce(has[:, t:t + 1], LA[:, t, :], X_AXIS, ALU.max))
                        step(nc.vector.tensor_scalar(has[:], has[:], 0.5, None, ALU.is_ge))
                        nc.vector.tensor_scalar(low[:, 0, :], LA[:, 0, :], 2.0 ** -60, None, ALU.max).then_inc(least, 1)
                        for t in range(TILES):
                            if t + 1 < TILES:
                                nc.vector.tensor_scalar(low[:, (t + 1) % 2, :], LA[:, t + 1, :], 2.0 ** -60, None,
                                                        ALU.max).then_inc(least, 1)
                            dve.wait_ge(logs, t + 1)
                            step(nc.vector.tensor_scalar(LA[:, t, :], lg[:, t % 2, :], 1.0, 2.5e28, ALU.add, ALU.mult))
                            step(nc.vector.tensor_tensor(LA[:, t, :], LA[:, t, :], lg[:, t % 2, :], ALU.min))

                    @block.scalar
                    def _(act):
                        for t in range(TILES):
                            act.wait_ge(least, t + 1)
                            if t >= 2:
                                act.wait_ge(done, TILES + 1 + 2 * (t - 1))
                            nc.scalar.activation(lg[:, t % 2, :], low[:, t % 2, :], ACT.Ln).then_inc(logs, 1)

        def attend(QT, KT, V, LA, has, A):
            with ExitStack() as st:
                sb, pb = tile_in(st), bank_in(st)
                staged = sems_in(st)("tile_staged0", "tile_staged1")
                scored, masked, shifted, probs_ready, turned, copied, valued, inverse, normed, tick = sems_in(st)(
                    "scored", "masked", "shifted", "probs_ready", "probs_turned", "turned_copied",
                    "head_valued", "inverse_steps", "tile_normed", "tick")
                QS = [sb(f"QS{par}", [128, KC, P]) for par in range(2)]
                logs = [sb(f"logs{par}", [P, NODES]) for par in range(2)]
                S = sb("S", [P, 2, NODES])
                PT = sb("PT", [P, 2, TILES, P])
                mx, z, rz = sb("mx", [P, 2, HEADS]), sb("z", [P, 2, HEADS]), sb("rz", [P, HEADS])
                score_ps, turn_ps, out_ps = pb("score_ps", [128, 1536]), pb("turn_ps", [128, 1536]), pb("out_ps", [128, 2, 512])
                HALF = 4

                def pair(r, step, last):
                    for par in range(2):
                        for h in range(HEADS):
                            after = 2 * HEADS - 1 - (HEADS * par + h) if last else 2
                            step(r, par, h, after)

                with nc.Block() as block:
                    @block.sync
                    def _(sp):
                        def stage(i, par):
                            sp.dma_start(QS[par][:], QT[:, :, bass.ds(i * P, P)]).then_inc(staged[par], 16)
                            sp.dma_start(logs[par][:], LA[:, bass.ds(i, 1), :].rearrange("p a n -> p (a n)")
                                         ).then_inc(staged[par], 16)

                        for par in range(2):
                            stage(par, par)
                        with sp.Fori(0, TILES // 2 - 1) as r:
                            for par in range(2):
                                sp.wait_ge(masked, HEADS * (2 * r + par + 1))
                                sp.sem_inc(tick, 1)
                                stage(2 * r + 2 + par, par)

                    @block.tensor
                    def _(pe):
                        def scores(par, h, pairs):
                            if h == 0:
                                pe.wait_ge(staged[par], 32 * pairs)
                            lo = DK * (h % 2)
                            for c0, cn in CHUNKS:
                                last = nc.tensor.matmul(score_ps[:P, c0:c0 + cn], QS[par][lo:lo + DK, h // 2, :],
                                                        KT[lo:lo + DK, h // 2, c0:c0 + cn], start=True, stop=True)
                            last.then_inc(scored, 1)

                        def turn(h):
                            for s in range(TILES):
                                last = nc.tensor.transpose(turn_ps[:P, 128 * s:128 * s + P],
                                                           S[:, h % 2, P * s:P * (s + 1)], ident[:P, :P])
                                if s in (HALF - 1, TILES - 1):
                                    last.then_inc(turned, 1)

                        def step(r, par, h, after):
                            n = 2 * HEADS * r + HEADS * par + h
                            if after >= 2:
                                pe.wait_ge(masked, n + 2)
                                ahead = (HEADS * par + h + 2) // HEADS
                                scores(ahead % 2, (h + 2) % HEADS, r + 1 + ahead // 2)
                            pe.wait_ge(copied, 2 * (n + 1))
                            if after >= 1:
                                pe.wait_ge(probs_ready, n + 2)
                                turn((h + 1) % HEADS)
                            if h == 0:
                                pe.wait_ge(normed, 2 * r + par + 1)
                            for s in range(TILES):
                                last = nc.tensor.matmul(out_ps[:P, par, DK * h:DK * (h + 1)], PT[:, h % 2, s, :],
                                                        V[:, s, DK * h:DK * (h + 1)], start=s == 0, stop=s == TILES - 1)
                            last.then_inc(valued, 1)

                        pe.sem_inc(normed, 2)
                        pe.sem_inc(valued, 1)
                        scores(0, 0, 1)
                        pe.wait_ge(masked, 1)
                        scores(0, 1, 1)
                        pe.wait_ge(probs_ready, 1)
                        turn(0)
                        with pe.Fori(0, TILES // 2 - 1) as r:
                            pair(r, step, False)
                        pair(TILES // 2 - 1, step, True)

                    @block.vector
                    def _(dve):
                        def mask(n, par, h, pairs):
                            if h == 0:
                                dve.wait_ge(staged[par], 32 * pairs)
                            dve.wait_ge(scored, n + 1)
                            dve.sem_inc(tick, 1)
                            nc.vector.tensor_tensor_reduce(
                                out=S[:, h % 2, :], in0=score_ps[:P, 0:NODES], in1=logs[par][:],
                                scale=1.0, scalar=-3e38, op0=ALU.add, op1=ALU.max,
                                accum_out=mx[:, par, h:h + 1]).then_inc(masked, 1)
                            dve.wait_ge(masked, n + 1)
                            nc.vector.tensor_scalar(mx[:, par, h:h + 1], mx[:, par, h:h + 1], -1.0, None,
                                                    ALU.mult).then_inc(shifted, 1)

                        def copy(n, h):
                            dve.wait_ge(turned, 2 * n + 1)
                            nc.vector.tensor_copy(PT[:, h % 2, 0:HALF, :],
                                                  turn_ps[:P, 0:HALF * 128].rearrange("p (s c) -> p s c", c=128)[:, :, 0:P]
                                                  ).then_inc(copied, 1)

                        def step(r, par, h, after):
                            i = 2 * r + par
                            n = HEADS * i + h
                            if after >= 2:
                                dve.wait_ge(turned, 2 * (n + 1))
                                ahead = (HEADS * par + h + 2) // HEADS
                                mask(n + 2, ahead % 2, (h + 2) % HEADS, r + 1 + ahead // 2)
                            if after >= 1:
                                dve.wait_ge(valued, n + 1)
                                copy(n + 1, h + 1)
                            if h == HEADS - 1:
                                dve.wait_ge(probs_ready, n + 1)
                                nc.vector.reciprocal(rz[:], z[:, par, :]).then_inc(inverse, 1)
                                dve.wait_ge(inverse, 2 * i + 1)
                                nc.vector.tensor_scalar(rz[:], rz[:], has[:, bass.ds(i, 1)], None, ALU.mult).then_inc(inverse, 1)
                                dve.wait_ge(inverse, 2 * i + 2)
                                dve.wait_ge(valued, n + 2)
                                nc.vector.tensor_tensor(
                                    A[:, bass.ds(i, 1), :].rearrange("p a (h c) -> p (a h) c", c=DK),
                                    out_ps[:P, par, :].rearrange("p (h c) -> p h c", c=DK),
                                    rz[:].unsqueeze(2).to_broadcast([P, HEADS, DK]), ALU.mult).then_inc(normed, 1)

                        mask(0, 0, 0, 1)
                        mask(1, 0, 1, 1)
                        copy(0, 0)
                        with dve.Fori(0, TILES // 2 - 1) as r:
                            pair(r, step, False)
                        pair(TILES // 2 - 1, step, True)

                    @block.scalar
                    def _(act):
                        def exp(n, par, h):
                            act.wait_ge(shifted, n + 1)
                            nc.scalar.activation(S[:, h % 2, :], S[:, h % 2, :], ACT.Exp, bias=mx[:, par, h:h + 1],
                                                 accum_out=z[:, par, h:h + 1]).then_inc(probs_ready, 1)

                        def copy(n, h):
                            act.wait_ge(turned, 2 * (n + 1))
                            nc.scalar.activation(PT[:, h % 2, HALF:TILES, :],
                                                 turn_ps[:P, HALF * 128:TILES * 128].rearrange("p (s c) -> p s c", c=128)[:, :, 0:P],
                                                 ACT.Copy).then_inc(copied, 1)

                        def step(r, par, h, after):
                            n = 2 * HEADS * r + HEADS * par + h
                            if after >= 1:
                                act.wait_ge(valued, n + 1)
                                copy(n + 1, h + 1)
                            if after >= 2:
                                ahead = (HEADS * par + h + 2) // HEADS
                                exp(n + 2, ahead % 2, (h + 2) % HEADS)

                        exp(0, 0, 0)
                        exp(1, 0, 1)
                        copy(0, 0)
                        with act.Fori(0, TILES // 2 - 1) as r:
                            pair(r, step, False)
                        pair(TILES // 2 - 1, step, True)

        def node_major_product(srcT, weights, k_chunks, dst, bias=None, add=None):
            with ExitStack() as st:
                sb, pb = tile_in(st), bank_in(st)
                loaded, done, moved = sems_in(st)("w_loaded", "product_done", "product_moved")
                W = sb("Wnm", [128, k_chunks, DIM])
                ps = pb("ps", [128, 4, 512])
                biasB = sb("biasB", [P, DIM]) if bias is not None else None
                with nc.Block() as block:
                    @block.sync
                    def _(sp):
                        sp.dma_start(W[:], weights.rearrange("(k p) n -> p k n", p=128)).then_inc(loaded, 16)
                        if bias is not None:
                            sp.dma_start(biasB[:], row(bias).broadcast_to([P, DIM])).then_inc(loaded, 16)

                    @block.tensor
                    def _(pe):
                        pe.wait_ge(loaded, 16 if bias is None else 32)
                        for t in range(TILES):
                            if t >= 4:
                                pe.wait_ge(moved, (t - 3) * (1 if bias is None else 2))
                            for k in range(k_chunks):
                                last = nc.tensor.matmul(ps[:P, t % 4, :], srcT[:, k, P * t:P * (t + 1)], W[:, k, :],
                                                        start=k == 0, stop=k == k_chunks - 1)
                            last.then_inc(done, 1)

                    @block.vector
                    def _(dve):
                        if bias is not None:
                            dve.wait_ge(loaded, 32)
                        n = 0
                        for t in range(TILES):
                            dve.wait_ge(done, t + 1)
                            nc.vector.tensor_tensor(dst[:, t, :], ps[:P, t % 4, :], add[:, t, :], ALU.add).then_inc(moved, 1)
                            n += 1
                            if bias is not None:
                                dve.wait_ge(moved, n)
                                nc.vector.tensor_tensor(dst[:, t, :], dst[:, t, :], biasB[:], ALU.add).then_inc(moved, 1)
                                n += 1

        def feature_major_layer(srcT, weights, bias, dstT, m_chunks, function):
            with ExitStack() as st:
                sb, pb = tile_in(st), bank_in(st)
                loaded, turned, bias_ready, done, moved = sems_in(st)(
                    "w_loaded", "bias_turned", "bias_ready", "product_done", "product_moved")
                W = sb("Wfm", [128, KC, m_chunks * 128])
                braw, bT = sb("braw", [m_chunks, 128]), sb("bT", [128, m_chunks])
                ps = pb("ps", [128, 4, 512])
                jobs = [(m, c0, cn) for m in range(m_chunks) for c0, cn in CHUNKS]
                with nc.Block() as block:
                    @block.sync
                    def _(sp):
                        sp.dma_start(W[:], weights.rearrange("(k p) n -> p k n", p=128)).then_inc(loaded, 16)
                        sp.dma_start(braw[:], bias.rearrange("(m p) -> m p", p=128)).then_inc(loaded, 16)

                    @block.tensor
                    def _(pe):
                        pe.wait_ge(loaded, 32)
                        nc.tensor.transpose(ps[:, 3, 0:m_chunks], braw[:], ident[:m_chunks, :m_chunks]).then_inc(turned, 1)
                        for n, (m, c0, cn) in enumerate(jobs):
                            if n == 3:
                                pe.wait_ge(bias_ready, 1)
                            if n >= 4:
                                pe.wait_ge(moved, n - 3)
                            for k in range(KC):
                                last = nc.tensor.matmul(ps[:, n % 4, 0:cn], W[:, k, 128 * m:128 * (m + 1)],
                                                        srcT[:, k, c0:c0 + cn], start=k == 0, stop=k == KC - 1)
                            last.then_inc(done, 1)

                    @block.scalar
                    def _(act):
                        act.wait_ge(turned, 1)
                        nc.scalar.activation(bT[:], ps[:, 3, 0:m_chunks], ACT.Copy).then_inc(bias_ready, 1)
                        act.wait_ge(bias_ready, 1)
                        for n, (m, c0, cn) in enumerate(jobs):
                            act.wait_ge(done, n + 1)
                            nc.scalar.activation(dstT[:, m, c0:c0 + cn], ps[:, n % 4, 0:cn], function,
                                                 bias=bT[:, m:m + 1]).then_inc(moved, 1)

        def gate(srcT, weights, weights_are_rows, bias, probs, best, bestI):
            with ExitStack() as st:
                sb, pb = tile_in(st), bank_in(st)
                loaded, turned, w_ready, done, logits_in, exped, steps = sems_in(st)(
                    "w_loaded", "w_turned", "w_ready", "logits_done", "logits_in", "exped", "gate_steps")
                W = sb("Wg", [128, KC, EXPERTS])
                Wraw = sb("Wraw", [EXPERTS, DIM]) if weights_are_rows else None
                biasB = sb("biasB", [P, EXPERTS])
                mx, zs = sb("mx", [P, TILES]), sb("zs", [P, TILES])
                lg = sb("lg", [P, TILES, EXPERTS])
                ps = pb("ps", [128, 2, 512])
                with nc.Block() as block:
                    @block.sync
                    def _(sp):
                        if weights_are_rows:
                            sp.dma_start(Wraw[:], weights).then_inc(loaded, 16)
                        else:
                            sp.dma_start(W[:], weights.rearrange("(k p) n -> p k n", p=128)).then_inc(loaded, 16)
                        sp.dma_start(biasB[:], row(bias).broadcast_to([P, EXPERTS])).then_inc(loaded, 16)

                    @block.tensor
                    def _(pe):
                        pe.wait_ge(loaded, 32)
                        if weights_are_rows:
                            for k in range(KC):
                                last = nc.tensor.transpose(ps[:, 1, EXPERTS * k:EXPERTS * (k + 1)],
                                                           Wraw[:, 128 * k:128 * (k + 1)], ident[:EXPERTS, :EXPERTS])
                            last.then_inc(turned, 1)
                            pe.wait_ge(w_ready, 1)
                        for t in range(TILES):
                            for k in range(KC):
                                last = nc.tensor.matmul(ps[:P, 0, EXPERTS * t:EXPERTS * (t + 1)], srcT[:, k, P * t:P * (t + 1)],
                                                        W[:, k, :], start=k == 0, stop=k == KC - 1)
                        last.then_inc(done, 1)

                    @block.scalar
                    def _(act):
                        if weights_are_rows:
                            act.wait_ge(turned, 1)
                            nc.scalar.activation(W[:], ps[:, 1, 0:KC * EXPERTS].rearrange("p (k e) -> p k e", k=KC),
                                                 ACT.Copy).then_inc(w_ready, 1)
                        act.wait_ge(logits_in, 1)
                        nc.scalar.activation(probs[:], lg[:], ACT.Exp).then_inc(exped, 1)

                    @block.vector
                    def _(dve):
                        step = Chain(dve, steps)
                        dve.wait_ge(loaded, 32)
                        dve.wait_ge(done, 1)
                        step(nc.vector.tensor_tensor(lg[:], ps[:P, 0, 0:TILES * EXPERTS].rearrange("p (t e) -> p t e", t=TILES),
                                                     biasB[:].unsqueeze(1).to_broadcast([P, TILES, EXPERTS]), ALU.add))
                        step(nc.vector.tensor_reduce(mx[:], lg[:], X_AXIS, ALU.max))
                        nc.vector.tensor_tensor(lg[:], lg[:], mx[:].unsqueeze(2).to_broadcast([P, TILES, EXPERTS]),
                                                ALU.subtract).then_inc(logits_in, 1)
                        dve.wait_ge(exped, 1)
                        step(nc.vector.tensor_reduce(zs[:], probs[:], X_AXIS, ALU.add))
                        step(nc.vector.reciprocal(zs[:], zs[:]))
                        step(nc.vector.tensor_tensor(probs[:], probs[:], zs[:].unsqueeze(2).to_broadcast([P, TILES, EXPERTS]), ALU.mult))
                        for t in range(TILES):
                            step(nc.vector.max(best[:, t, :], probs[:, t, :]))
                            step(nc.vector.max_index(bestI[:, t, :], best[:, t, :], probs[:, t, :]))

        def place_choices(best, bestI, weight, slot_in, slot_out):
            SPLIT = 32
            with ExitStack() as st:
                sb, pb = tile_in(st), bank_in(st)
                steps, numbered, w8_ready, turned, first_out, rows_in, compared, ranked = sems_in(st)(
                    "place_steps", "nodes_numbered", "w8_ready", "turned", "first_out", "rows_in", "compared", "ranked")
                zeroed, upper_in, lower_in = sems_in(st)("zeroed", "upper_in", "lower_in")
                idxF = sb("idxF", [P, TILES, 2])
                oh = sb("oh", [P, 2, TILES, EXPERTS])
                w8, tmp, routed = (sb("w8", [P, TILES, EXPERTS]), sb("tmp", [P, TILES, EXPERTS]),
                                   sb("routed", [P, TILES, EXPERTS]))
                w8T = sb("w8T", [SPLIT + EXPERTS, NODES], F32R)
                ohT = sb("ohT", [SPLIT + EXPERTS, 2, NODES], F32R)
                junk, same = sb("junk", [P, NODES]), sb("same", [P, P])
                own = sb("own", [P, TILES, 2])
                parts = sb("parts", [P, TILES, 2, 3])
                rank, keep = sb("rank", [P, TILES, 2]), sb("keep", [P, TILES, 2])
                slotF, node, nodeF = (sb("slotF", [P, TILES, 2]), sb("node", [P, TILES, 2], I32),
                                      sb("nodeF", [P, TILES, 2]))
                ps = pb("ps", [128, 2, 2048])
                wide = [P, TILES, EXPERTS]
                with nc.Block() as block:
                    @block.gpsimd
                    def _(pool):
                        nc.gpsimd.iota(node[:], pattern=[[P, TILES], [NODES, 2]], base=EXPERTS * ROWS0,
                                       channel_multiplier=1).then_inc(numbered, 1)

                    @block.vector
                    def _(dve):
                        step = Chain(dve, steps)
                        step(nc.vector.memset(parts[:], 0.0))
                        nc.vector.tensor_copy(w8T[:], zeros[:SPLIT + EXPERTS, 0:1].to_broadcast([SPLIT + EXPERTS, NODES]))
                        nc.vector.tensor_copy(ohT[:], zeros[:SPLIT + EXPERTS, 0:1].unsqueeze(2).to_broadcast([SPLIT + EXPERTS, 2, NODES])
                                              ).then_inc(zeroed, 1)
                        step(nc.vector.tensor_copy(idxF[:], bestI[:, :, 0:2]))
                        e8 = count[:P, 0:EXPERTS].unsqueeze(1).to_broadcast(wide)
                        for c in range(2):
                            step(nc.vector.tensor_tensor(oh[:, c], e8, idxF[:, :, c:c + 1].to_broadcast(wide), ALU.is_equal))
                        step(nc.vector.tensor_tensor(routed[:], oh[:, 0], oh[:, 1], ALU.add))
                        step(nc.vector.tensor_scalar(routed[:], routed[:], -1.0, None, ALU.add))
                        step(nc.vector.tensor_tensor(w8[:], oh[:, 0], best[:, :, 0:1].to_broadcast(wide), ALU.mult))
                        step(nc.vector.tensor_tensor(tmp[:], oh[:, 1], best[:, :, 1:2].to_broadcast(wide), ALU.mult))
                        step(nc.vector.tensor_tensor(w8[:], w8[:], tmp[:], ALU.add))
                        step(nc.vector.tensor_tensor(w8[:], w8[:], routed[:], ALU.add))
                        dve.sem_inc(w8_ready, 1)
                        dve.wait_ge(numbered, 1)
                        step(nc.vector.tensor_copy(nodeF[:], node[:]))
                        dve.wait_ge(upper_in, 1)
                        nc.vector.tensor_tensor(w8T[SPLIT:SPLIT + EXPERTS, :].rearrange("e (t n) -> e t n", n=P),
                                                ps[:EXPERTS, 0, 0:128 * TILES].rearrange("e (t n) -> e t n", n=128)[:, :, 0:P],
                                                w8T[0:EXPERTS, :].bitcast(F32).rearrange("e (t n) -> e t n", n=P), ALU.subtract
                                                ).then_inc(lower_in, 1)
                        for n in range(2 * TILES):
                            t, c = n // 2, n % 2
                            mine = own[:, t, c:c + 1]
                            dve.wait_ge(ranked, n + 1)
                            full = ps[:P, n % 2, 0:NODES]
                            step(nc.vector.tensor_tensor(same[:], full[:, P * t:P * (t + 1)], ident[:P, :P], ALU.mult))
                            step(nc.vector.tensor_reduce(mine, same[:], X_AXIS, ALU.add))
                            if t > 0:
                                step(nc.vector.tensor_scalar(junk[:, 0:P * t], full[:, 0:P * t], mine, None, ALU.is_ge, ALU.add,
                                                             accum_out=parts[:, t, c, 0:1]))
                            step(nc.vector.tensor_scalar(junk[:, 0:NODES - P * t], full[:, P * t:NODES], mine, None,
                                                         ALU.is_gt, ALU.add, accum_out=parts[:, t, c, 1:2]))
                            step(nc.vector.scalar_tensor_tensor(out=same[:], in0=full[:, P * t:P * (t + 1)], scalar=mine,
                                                                in1=earlier[:P, :P], op0=ALU.is_equal, op1=ALU.mult))
                            dve.sem_inc(compared, 1)
                            step(nc.vector.tensor_reduce(parts[:, t, c, 2:3], same[:], X_AXIS, ALU.add))
                        step(nc.vector.tensor_reduce(rank[:], parts[:], X_AXIS, ALU.add))
                        step(nc.vector.tensor_scalar(keep[:], rank[:], CAP0 - 0.5, None, ALU.is_lt))
                        step(nc.vector.scalar_tensor_tensor(out=slotF[:], in0=idxF[:], scalar=float(ROWS0), in1=rank[:],
                                                            op0=ALU.mult, op1=ALU.add))
                        step(nc.vector.tensor_tensor(slotF[:], slotF[:], keep[:], ALU.mult))
                        step(nc.vector.tensor_copy(slot_out[:], slotF[:]))
                        step(nc.vector.tensor_tensor(weight[:], best[:, :, 0:2], keep[:], ALU.mult))
                        step(nc.vector.tensor_scalar(keep[:], keep[:], -1.0, 1.0, ALU.mult, ALU.add))
                        step(nc.vector.tensor_tensor(keep[:], keep[:], nodeF[:], ALU.mult))
                        step(nc.vector.tensor_tensor(slot_in[:], slotF[:], keep[:], ALU.add))

                    @block.tensor
                    def _(pe):
                        pe.wait_ge(w8_ready, 1)
                        for t in range(TILES):
                            nc.tensor.transpose(ps[:EXPERTS, 0, 128 * t:128 * t + P], w8[:, t, :], ident[:P, :P])
                        for c in range(2):
                            if c == 1:
                                pe.wait_ge(first_out, 1)
                            for t in range(TILES):
                                last = nc.tensor.transpose(ps[:EXPERTS, 1, 128 * t:128 * t + P], oh[:, c, t, :], ident[:P, :P])
                            last.then_inc(turned, 1)
                        pe.wait_ge(rows_in, 1)
                        pe.wait_ge(lower_in, 1)
                        for n in range(2 * TILES):
                            t, c = n // 2, n % 2
                            if n >= 2:
                                pe.wait_ge(compared, n - 1)
                            for c0, cn in CHUNKS:
                                last = nc.tensor.matmul(ps[:P, n % 2, c0:c0 + cn], ohT[:, c, P * t:P * (t + 1)],
                                                        w8T[:, c0:c0 + cn], start=True, stop=True)
                            last.then_inc(ranked, 1)

                    @block.scalar
                    def _(act):
                        act.wait_ge(turned, 1)

                        def row_of_tiles(bank):
                            return ps[:EXPERTS, bank, 0:128 * TILES].rearrange("e (t n) -> e t n", n=128)[:, :, 0:P]

                        def by_tile(rows):
                            return rows.rearrange("e (t n) -> e t n", n=P)

                        act.wait_ge(zeroed, 1)
                        nc.scalar.activation(by_tile(w8T[0:EXPERTS, :]), row_of_tiles(0), ACT.Copy).then_inc(upper_in, 1)
                        nc.scalar.activation(by_tile(ohT[0:EXPERTS, 0, :]), row_of_tiles(1), ACT.Copy)
                        nc.scalar.activation(by_tile(ohT[SPLIT:SPLIT + EXPERTS, 0, :]), row_of_tiles(1), ACT.Copy).then_inc(first_out, 1)
                        act.wait_ge(turned, 2)
                        nc.scalar.activation(by_tile(ohT[0:EXPERTS, 1, :]), row_of_tiles(1), ACT.Copy)
                        nc.scalar.activation(by_tile(ohT[SPLIT:SPLIT + EXPERTS, 1, :]), row_of_tiles(1), ACT.Copy).then_inc(rows_in, 1)

        def fill_zeros(sp, target, zeroed):
            starts = range(0, target.shape[0], 128)
            for r in starts:
                m = min(128, target.shape[0] - r)
                sp.dma_start(target[r:r + m, :], zeros[:m, :]).then_inc(zeroed, 16)
            return 16 * len(starts)

        def scatter_rows(src, slots, choices, target):
            with ExitStack() as st:
                (sent,) = sems_in(st)("rows_sent")
                with nc.Block() as block:
                    @block.gpsimd
                    def _(pool):
                        for t in range(TILES):
                            for c in range(choices):
                                pool.indirect_dma_start(
                                    out=target, out_offset=bass.IndirectOffsetOnAxis(ap=slots[:, t, c:c + 1], axis=0),
                                    in_=src[:, t, :], in_offset=None).then_inc(sent, 16)
                        pool.wait_ge(sent, 16 * TILES * choices)

        def experts0():
            with ExitStack() as st:
                sb, pb = tile_in(st), bank_in(st)
                x_loaded = sems_in(st)("x_loaded0", "x_loaded1")
                w1_loaded = sems_in(st)("w1_loaded0", "w1_loaded1")
                w2_loaded = sems_in(st)("w2_loaded0", "w2_loaded1")
                stored = sems_in(st)("stored0", "stored1")
                (b_loaded, b_turned, b_ready, x_turned, x_moved, hid_done, hid_moved, y_done, y_moved, back_done,
                 back_moved, y_free, tick) = sems_in(st)(
                    "b_loaded", "b_turned", "b_ready", "x_turned", "x_moved", "hid_done", "hid_moved", "y_done",
                    "y_moved", "back_done", "back_moved", "y_free", "tick")
                W1 = [sb(f"W1_{i}", [128, KC, HID0]) for i in range(2)]
                W2 = [sb(f"W2_{i}", [128, MC0, DIM]) for i in range(2)]
                b1raw, b2raw = sb("b1raw", [EXPERTS * MC0, 128]), sb("b2raw", [EXPERTS * KC, 128])
                b1T, b2T = sb("b1T", [128, EXPERTS * MC0]), sb("b2T", [128, EXPERTS * KC])
                xe = [sb(f"xe{i}", [HALF0, 2, DIM]) for i in range(2)]
                ye = [sb(f"ye{i}", [HALF0, 2, DIM]) for i in range(2)]
                xT, yT = sb("xT", [128, KC, ROWS0]), sb("yT", [128, KC, ROWS0])
                hid = sb("hid", [128, MC0, ROWS0])
                hid_ps, y_ps, turn_ps = pb("hid_ps", [128, 4, 512]), pb("y_ps", [128, 2, 512]), pb("turn_ps", [128, 2, 512])
                with nc.Block() as block:
                    def load_first(sp, e, b):
                        rows = xin0[bass.ds(e * ROWS0, ROWS0), :].rearrange("(c p) d -> p c d", p=HALF0)
                        sp.dma_start(xe[b][:], rows).then_inc(x_loaded[b], 16)
                        sp.dma_start(W1[b][:], I["L0_ffn_w1"][bass.ds(e, 1)].rearrange("a (k p) n -> p (a k) n", p=128)
                                     ).then_inc(w1_loaded[b], 16)

                    def load_second(sp, e, b):
                        sp.dma_start(W2[b][:], I["L0_ffn_w2"][bass.ds(e, 1)].rearrange("a (m p) n -> p (a m) n", p=128)
                                     ).then_inc(w2_loaded[b], 16)

                    @block.sync
                    def _(sp):
                        sp.dma_start(b1raw[:], I["L0_ffn_b1"].rearrange("e (m p) -> (e m) p", p=128)).then_inc(b_loaded, 16)
                        sp.dma_start(b2raw[:], I["L0_ffn_b2"].rearrange("e (m p) -> (e m) p", p=128)).then_inc(b_loaded, 16)
                        for b in range(2):
                            load_first(sp, b, b)
                            load_second(sp, b, b)
                        with sp.Fori(0, EXPERTS // 2 - 1) as r:
                            for b in range(2):
                                sp.wait_ge(hid_done, MC0 * (2 * r + b + 1))
                                sp.sem_inc(tick, 1)
                                load_first(sp, 2 * r + 2 + b, b)
                                sp.wait_ge(y_done, KC * (2 * r + b + 1))
                                sp.sem_inc(tick, 1)
                                load_second(sp, 2 * r + 2 + b, b)

                    @block.gpsimd
                    def _(pool):
                        with pool.Fori(0, EXPERTS // 2) as r:
                            for b in range(2):
                                pool.wait_ge(back_moved, 2 * (2 * r + b + 1) + 2)
                                pool.sem_inc(tick, 1)
                                rows = yout0[bass.ds((2 * r + b) * ROWS0, ROWS0), :].rearrange("(c p) d -> p c d", p=HALF0)
                                pool.dma_start(rows, ye[b][:]).then_inc(stored[b], 16)
                                pool.wait_ge(stored[b], 16 * (r + 1))
                                pool.sem_inc(y_free, 1)

                    @block.tensor
                    def _(pe):
                        pe.wait_ge(b_loaded, 32)
                        nc.tensor.transpose(y_ps[:, 0, 0:EXPERTS * MC0], b1raw[:], ident[:])
                        nc.tensor.transpose(y_ps[:, 1, 0:EXPERTS * KC], b2raw[:], ident[:EXPERTS * KC, :EXPERTS * KC]
                                            ).then_inc(b_turned, 1)
                        pe.wait_ge(b_ready, 2)
                        pe.sem_inc(back_moved, 2)
                        with pe.Fori(0, EXPERTS // 2) as r:
                            for b in range(2):
                                e = 2 * r + b
                                pe.wait_ge(x_loaded[b], 16 * (r + 1))
                                for c in range(2):
                                    pe.wait_ge(back_moved, 2 * e + c + 1)
                                    for k in range(KC):
                                        last = nc.tensor.transpose(turn_ps[:, c, HALF0 * k:HALF0 * (k + 1)],
                                                                   xe[b][:, c, 128 * k:128 * (k + 1)], ident[:HALF0, :HALF0])
                                    last.then_inc(x_turned, 1)
                                pe.wait_ge(w1_loaded[b], 16 * (r + 1))
                                pe.wait_ge(x_moved, 2 * (e + 1))
                                for m in range(MC0):
                                    if m >= 4:
                                        pe.wait_ge(hid_moved, MC0 * e + m - 3)
                                    for k in range(KC):
                                        last = nc.tensor.matmul(hid_ps[:, m % 4, 0:ROWS0], W1[b][:, k, 128 * m:128 * (m + 1)],
                                                                xT[:, k, :], start=k == 0, stop=k == KC - 1)
                                    last.then_inc(hid_done, 1)
                                pe.wait_ge(w2_loaded[b], 16 * (r + 1))
                                for d in range(KC):
                                    if d >= 2:
                                        pe.wait_ge(y_moved, KC * e + d - 1)
                                    for m in range(MC0):
                                        if d == 0:
                                            pe.wait_ge(hid_moved, MC0 * e + m + 1)
                                        last = nc.tensor.matmul(y_ps[:, d % 2, 0:ROWS0], W2[b][:, m, 128 * d:128 * (d + 1)],
                                                                hid[:, m, :], start=m == 0, stop=m == MC0 - 1)
                                    last.then_inc(y_done, 1)
                                pe.wait_ge(y_moved, KC * (e + 1))
                                for c in range(2):
                                    for k in range(KC):
                                        last = nc.tensor.transpose(turn_ps[:HALF0, c, 128 * k:128 * (k + 1)],
                                                                   yT[:, k, HALF0 * c:HALF0 * (c + 1)], ident[:])
                                    last.then_inc(back_done, 1)

                    @block.scalar
                    def _(act):
                        act.wait_ge(b_turned, 1)
                        nc.scalar.activation(b1T[:], y_ps[:, 0, 0:EXPERTS * MC0], ACT.Copy).then_inc(b_ready, 1)
                        nc.scalar.activation(b2T[:], y_ps[:, 1, 0:EXPERTS * KC], ACT.Copy).then_inc(b_ready, 1)
                        act.wait_ge(b_ready, 2)
                        with act.Fori(0, EXPERTS) as e:
                            for c in range(2):
                                act.wait_ge(x_turned, 2 * e + c + 1)
                                nc.scalar.activation(xT[:, :, HALF0 * c:HALF0 * (c + 1)],
                                                     turn_ps[:, c, 0:KC * HALF0].rearrange("p (k n) -> p k n", k=KC),
                                                     ACT.Copy).then_inc(x_moved, 1)
                            for m in range(MC0):
                                act.wait_ge(hid_done, MC0 * e + m + 1)
                                nc.scalar.activation(hid[:, m, :], hid_ps[:, m % 4, 0:ROWS0], ACT.Gelu,
                                                     bias=b1T[:, bass.ds(e * MC0 + m, 1)]).then_inc(hid_moved, 1)

                    @block.vector
                    def _(dve):
                        dve.sem_inc(y_free, 2)
                        dve.wait_ge(b_ready, 2)
                        with dve.Fori(0, EXPERTS // 2) as r:
                            for b in range(2):
                                e = 2 * r + b
                                for d in range(KC):
                                    dve.wait_ge(y_done, KC * e + d + 1)
                                    nc.vector.tensor_scalar(yT[:, d, :], y_ps[:, d % 2, 0:ROWS0], b2T[:, bass.ds(e * KC + d, 1)],
                                                            None, ALU.add).then_inc(y_moved, 1)
                                dve.wait_ge(y_free, e + 1)
                                for c in range(2):
                                    dve.wait_ge(back_done, 2 * e + c + 1)
                                    nc.vector.tensor_copy(ye[b][:, c, :], turn_ps[:HALF0, c, :]).then_inc(back_moved, 1)

        def combine(picks):
            with ExitStack() as st:
                sb = tile_in(st)
                RING = 4
                arrived = sems_in(st)(*[f"arrived{i}" for i in range(RING)])
                (added,) = sems_in(st)("added")
                got = sb("got", [P, RING, DIM])
                jobs = [(t, *pick) for t in range(TILES) for pick in picks]
                with nc.Block() as block:
                    @block.gpsimd
                    def _(pool):
                        for n, (t, source, slots, _) in enumerate(jobs):
                            if n >= RING:
                                pool.wait_ge(added, n - RING + 1)
                            pool.indirect_dma_start(
                                out=got[:, n % RING, :], out_offset=None, in_=source,
                                in_offset=bass.IndirectOffsetOnAxis(ap=slots(t), axis=0)).then_inc(arrived[n % RING], 16)

                    @block.vector
                    def _(dve):
                        for n, (t, _, _, weight) in enumerate(jobs):
                            dve.wait_ge(arrived[n % RING], 16 * (n // RING + 1))
                            if n >= 1:
                                dve.wait_ge(added, n)
                            nc.vector.scalar_tensor_tensor(out=X[:, t, :], in0=got[:, n % RING, :], scalar=weight(t),
                                                           in1=X[:, t, :], op0=ALU.mult, op1=ALU.add).then_inc(added, 1)

        def mix_up(xT):
            with ExitStack() as st:
                sb, pb = tile_in(st), bank_in(st)
                loaded, done, moved, stored = sems_in(st)("w_loaded", "mixed", "mixed_moved", "mixed_stored")
                W = sb("Wup", [128, 2, MUL])
                rows = sb("rows", [P, TILES, DIM])
                ps = pb("ps", [128, 4, 512])
                with nc.Block() as block:
                    @block.sync
                    def _(sp):
                        sp.dma_start(W[:, 0, :], I["L1_gnn_W_up0"]).then_inc(loaded, 16)
                        sp.dma_start(W[:, 1, :], I["L1_gnn_W_up1"]).then_inc(loaded, 16)
                        for t in range(TILES):
                            sp.wait_ge(moved, t + 1)
                            sp.dma_start(up_dram[P * t:P * (t + 1), :], rows[:, t, :]).then_inc(stored, 16)
                        sp.wait_ge(stored, 16 * TILES)

                    @block.tensor
                    def _(pe):
                        pe.wait_ge(loaded, 32)
                        for t in range(TILES):
                            if t >= 4:
                                pe.wait_ge(moved, t - 3)
                            for q in range(4):
                                last = nc.tensor.matmul(ps[:P, t % 4, MUL * q:MUL * (q + 1)], xT[:, q, P * t:P * (t + 1)],
                                                        W[:, min(q, 1), :], start=True, stop=True)
                            last.then_inc(done, 1)

                    @block.scalar
                    def _(act):
                        for t in range(TILES):
                            act.wait_ge(done, t + 1)
                            nc.scalar.activation(rows[:, t, :], ps[:P, t % 4, :], ACT.Copy,
                                                 scale=1.0 / math.sqrt(MUL)).then_inc(moved, 1)

        def messages(RECS, MSG):
            HID = 64
            with ExitStack() as st:
                sb, pb = tile_in(st), bank_in(st)
                arrived = sems_in(st)(*[f"rows_arrived{t}" for t in range(EPP)])
                (zeroed, w_loaded, w_scaled, cleared, feats, feats_turned, feats_in, layer_done, layer_out, weighed, products,
                 lanes_ready, one_hots, dots, summed, taken, idx_ready, staged, tick) = sems_in(st)(
                    "zeroed", "mlp_loaded", "mlp_scaled", "sums_cleared", "feats_staged", "feats_turned", "feats_in",
                    "layer_done", "layer_out", "edge_weights_done", "products_ready", "lanes_ready", "one_hots_ready", "dot_steps", "tile_summed",
                    "sums_taken", "indices_ready", "recs_staged", "tick")
                W1b, W2b, W3b = sb("W1b", [16, 128]), sb("W2b", [128, 128]), sb("W3b", [128, 128])
                W4 = sb("W4", [128, DIM])
                srcI = sb("srcI", [128, GROUPS, EPP], I32)
                idx = sb("idx", [128, 2, EPP], I32)
                rows = sb("rows", [128, EPP, DIM])
                lane = sb("lane", [128, P])
                rg = sb("rg", [128, 2, EPP, 8])
                fs = sb("fs", [128, 2, 16])
                fT, h1, h2, h3 = sb("fT", [16, 256]), sb("h1", [128, 256]), sb("h2", [128, 256]), sb("h3", [128, 256])
                prod = sb("prod", [128, 2, 6, MUL])
                dot = sb("dot", [128, 2, 3, MUL])
                oh = sb("oh", [128, 2, 5, P])
                acc, w_ps, mlp_ps = pb("acc", [128, 2, 2, 512]), pb("w_ps", [128, 2, 512]), pb("mlp_ps", [128, 2, 512])

                with nc.Block() as block:
                    @block.sync
                    def _(sp):
                        sp.wait_ge(zeroed, 1)
                        for w, name, k in ((W1b, "L1_gnn_W_mlp1", 8), (W2b, "L1_gnn_W_mlp2", HID), (W3b, "L1_gnn_W_mlp3", HID)):
                            for half in range(2):
                                sp.dma_start(w[k * half:k * (half + 1), HID * half:HID * (half + 1)], I[name]).then_inc(w_loaded, 16)
                        for half in range(2):
                            sp.dma_start(W4[HID * half:HID * (half + 1), :], I["L1_gnn_W_mlp4"]).then_inc(w_loaded, 16)

                    @block.gpsimd
                    def _(pool):
                        nc.gpsimd.memset(W1b[:], 0.0)
                        nc.gpsimd.memset(W2b[:], 0.0)
                        nc.gpsimd.memset(W3b[:], 0.0)
                        nc.gpsimd.iota(lane[:], pattern=[[1, P]], base=0, channel_multiplier=0,
                                       allow_small_or_imprecise_dtypes=True).then_inc(zeroed, 1)
                        pool.sem_inc(products, EPP)
                        pool.wait_ge(idx_ready, 1)
                        with pool.Fori(0, GROUPS // 2) as r:
                            for par in range(2):
                                g = 2 * r + par
                                nc.gpsimd.tensor_copy(idx[:, par, :], srcI[:, bass.ds(g, 1), :].rearrange("p a t -> p (a t)")
                                                      ).then_inc(idx_ready, 1)
                                pool.wait_ge(idx_ready, g + 2)
                                pool.sem_inc(tick, 1)
                                for t in range(EPP):
                                    pool.wait_ge(products, EPP * g + t + 1)
                                    pool.sem_inc(tick, 1)
                                    pool.indirect_dma_start(
                                        out=rows[:, t, :], out_offset=None, in_=up_dram,
                                        in_offset=bass.IndirectOffsetOnAxis(ap=idx[:, par, t:t + 1], axis=0)
                                    ).then_inc(arrived[t], 16)

                    @block.tensor
                    def _(pe):
                        def turn_features(n):
                            pe.wait_ge(feats, n)
                            for tt in range(2):
                                last = nc.tensor.transpose(mlp_ps[:16, 0, 128 * tt:128 * (tt + 1)], fs[:, tt, :], ident[:])
                            last.then_inc(feats_turned, 1)

                        def weigh(t, layers):
                            if layers is not None:
                                pe.wait_ge(layer_out, layers)
                            half, col = t // 2, 128 * (t % 2)
                            nc.tensor.matmul(w_ps[:, t % 2, :], h3[HID * half:HID * (half + 1), col:col + 128],
                                             W4[HID * half:HID * (half + 1), :], start=True, stop=True).then_inc(weighed, 1)

                        def layer1(n):
                            pe.wait_ge(feats_in, n)
                            nc.tensor.matmul(mlp_ps[:, 1, 0:256], W1b[:], fT[:], start=True, stop=True).then_inc(layer_done, 1)

                        def layer2(done):
                            pe.wait_ge(layer_out, done)
                            nc.tensor.matmul(mlp_ps[:, 0, 0:256], W2b[:], h1[:], start=True, stop=True).then_inc(layer_done, 1)

                        def layer3(done):
                            pe.wait_ge(layer_out, done)
                            nc.tensor.matmul(mlp_ps[:, 1, 0:256], W3b[:], h2[:], start=True, stop=True).then_inc(layer_done, 1)

                        pe.wait_ge(w_loaded, 128)
                        pe.wait_ge(w_scaled, 2)
                        turn_features(1)
                        layer1(1)
                        layer2(1)
                        layer3(2)
                        weigh(0, 3)
                        with pe.Fori(0, GROUPS // 2) as r:
                            for par in range(2):
                                g = 2 * r + par
                                for t in range(EPP):
                                    pe.wait_ge(products, EPP * g + t + EPP)
                                    weigh((t + 1) % EPP, 3 * (g + 2) if t == EPP - 1 else None)
                                    if t == 0:
                                        turn_features(g + 2)
                                    pe.wait_ge(one_hots, EPP * g + t + 1)
                                    pe.wait_ge(products, EPP * g + t + 1 + EPP)
                                    if t == 0:
                                        pe.wait_ge(taken, g + 1)
                                    nc.tensor.matmul(acc[:P, par, 0, :], oh[:, t % 2, 0, :], prod[:, t % 2, 0:4, :].rearrange("p b c -> p (b c)"),
                                                     start=t == 0, stop=t == EPP - 1)
                                    if t == 0:
                                        layer1(g + 2)
                                    if t == 1:
                                        layer2(3 * (g + 1) + 1)
                                    if t == 2:
                                        layer3(3 * (g + 1) + 2)
                                    for i in range(4):
                                        last = nc.tensor.matmul(acc[:P, par, 1, MUL * i:MUL * (i + 1)], oh[:, t % 2, 1 + i, :],
                                                                prod[:, t % 2, 4 + i // 3, :], start=t == 0 and i == 0,
                                                                stop=t == EPP - 1 and i == 3, skip_group_check=True)
                                    last.then_inc(summed, 1)

                    @block.scalar
                    def _(act):
                        def features_in(n):
                            act.wait_ge(feats_turned, n)
                            nc.scalar.activation(fT[:], mlp_ps[:16, 0, 0:256], ACT.Copy).then_inc(feats_in, 1)

                        def layer(n, which):
                            act.wait_ge(layer_done, n)
                            nc.scalar.activation((h1, h2, h3)[which][:], mlp_ps[:, (which + 1) % 2, 0:256], ACT.Silu,
                                                 scale=(1 / math.sqrt(8), SILU_2MOM / math.sqrt(HID), SILU_2MOM / math.sqrt(HID))[which]
                                                 ).then_inc(layer_out, 1)

                        features_in(1)
                        for which in range(3):
                            layer(which + 1, which)
                        with act.Fori(0, GROUPS // 2) as r:
                            for par in range(2):
                                g = 2 * r + par
                                for t in range(EPP):
                                    act.wait_ge(lanes_ready, EPP * g + t + 1)
                                    for q in range(4):
                                        last = nc.scalar.activation(oh[:, t % 2, q, :], oh[:, t % 2, 4, :], ACT.Copy,
                                                                    scale=rg[:, par, t, 4 + q:5 + q])
                                    last.then_inc(one_hots, 1)
                                    if t == 0:
                                        features_in(g + 2)
                                    else:
                                        layer(3 * (g + 1) + t, t - 1)

                    @block.vector
                    def _(dve):
                        def stage_features(g):
                            nc.vector.tensor_copy(fs[:].rearrange("p t (b f) -> p b t f", b=2),
                                                  RECS[:, bass.ds(g, 1), :, 8:16].rearrange("p a (b t) f -> p (a b) t f", b=2)
                                                  ).then_inc(feats, 1)

                        def take_sums(block, g, par):
                            dve.wait_ge(summed, EPP * g + 2)
                            dve.wait_ge(taken, g + 1)
                            sums = MSG[:, bass.ds(block, 1), :].rearrange("p a n -> p (a n)")
                            nc.vector.tensor_tensor(sums, sums, acc[:P, par, :, :].rearrange("p a n -> p (a n)"), ALU.add
                                                    ).then_inc(taken, 1)

                        nc.vector.tensor_copy(srcI[:], RECS[:, 0:GROUPS, :, 0]).then_inc(idx_ready, 1)
                        nc.vector.memset(acc[:, 1, :, :], 0.0).then_inc(taken, 1)
                        dve.wait_ge(w_loaded, 128)
                        nc.vector.tensor_scalar(W4[:], W4[:], SILU_2MOM / math.sqrt(HID), None, ALU.mult).then_inc(w_scaled, 1)
                        dve.wait_ge(w_scaled, 1)
                        nc.vector.tensor_scalar(W4[:, 384:512], W4[:, 384:512], 1 / math.sqrt(3), None, ALU.mult).then_inc(w_scaled, 1)
                        stage_features(0)
                        nc.vector.memset(MSG[:], 0.0).then_inc(cleared, 1)
                        dve.wait_ge(cleared, 1)
                        dve.wait_ge(zeroed, 1)
                        dve.sem_inc(summed, 2)
                        with dve.Fori(0, GROUPS // 2) as r:
                            for par in range(2):
                                g = 2 * r + par
                                block_before = dve.value_load(blockI[0:1, bass.ds(g, 1)], min_val=0, max_val=TILES - 1)
                                nc.vector.tensor_copy(rg[:, par], RECS[:, bass.ds(g, 1), :, 0:8].rearrange("p a t w -> p (a t) w")
                                                      ).then_inc(staged, 1)
                                dve.wait_ge(feats_turned, g + 1)
                                stage_features(g + 1)
                                dve.wait_ge(staged, g + 1)
                                for t in range(EPP):
                                    dve.wait_ge(summed, EPP * g + t + 1)
                                    nc.vector.tensor_scalar(oh[:, t % 2, 4, :], lane[:], rg[:, par, t, 1:2], None,
                                                            ALU.is_equal).then_inc(lanes_ready, 1)
                                    dve.wait_ge(arrived[t], 16 * (g + 1))
                                    pr = prod[:, t % 2, :, :]
                                    w = w_ps[:, t % 2, :].rearrange("p (b c) -> p b c", c=MUL)
                                    s = rows[:, t, :].rearrange("p (b c) -> p b c", c=MUL)
                                    y = rg[:, par, t, 4:8]
                                    n = 3 * (EPP * g + t)
                                    nc.vector.tensor_scalar(dot[:, t % 2, 0, :], s[:, 1, :], y[:, 1:2], None, ALU.mult).then_inc(dots, 1)
                                    dve.wait_ge(dots, n + 1)
                                    nc.vector.scalar_tensor_tensor(out=dot[:, t % 2, 1, :], in0=s[:, 2, :], scalar=y[:, 2:3],
                                                                   in1=dot[:, t % 2, 0, :], op0=ALU.mult, op1=ALU.add).then_inc(dots, 1)
                                    dve.wait_ge(weighed, EPP * g + t + 1)
                                    nc.vector.tensor_tensor(pr[:, 0:5:4, :], w[:, 0:2, :], s[:, 0:1, :].to_broadcast([128, 2, MUL]), ALU.mult)
                                    dve.wait_ge(dots, n + 2)
                                    nc.vector.scalar_tensor_tensor(out=dot[:, t % 2, 2, :], in0=s[:, 3, :], scalar=y[:, 3:4],
                                                                   in1=dot[:, t % 2, 1, :], op0=ALU.mult, op1=ALU.add).then_inc(dots, 1)
                                    nc.vector.tensor_tensor(pr[:, 1:4, :], w[:, 2:3, :].to_broadcast([128, 3, MUL]), s[:, 1:4, :], ALU.mult)
                                    dve.wait_ge(dots, n + 3)
                                    nc.vector.tensor_tensor(pr[:, 5, :], w[:, 3, :], dot[:, t % 2, 2, :], ALU.mult).then_inc(products, 1)
                                    if t == 1:
                                        take_sums(block_before, g, 1 - par)
                        take_sums(dve.value_load(blockI[0:1, GROUPS:GROUPS + 1], min_val=0, max_val=TILES - 1), GROUPS, 1)

        def mix_out(MSG):
            with ExitStack() as st:
                sb, pb = tile_in(st), bank_in(st)
                loaded, turned, moved, done, added = sems_in(st)("w_loaded", "turned", "turned_moved", "mixed", "added")
                W = sb("Wout", [128, 4, MUL])
                mT = sb("mT", [128, 2, 8, P])
                turn_ps, ps = pb("turn_ps", [128, 4, 512]), pb("ps", [128, 2, 512])
                with nc.Block() as block:
                    @block.sync
                    def _(sp):
                        sp.dma_start(W[:, 0:2, :], I["L1_gnn_W_out0"].rearrange("(k p) n -> p k n", p=128)).then_inc(loaded, 16)
                        sp.dma_start(W[:, 2:4, :], I["L1_gnn_W_out1"].rearrange("(k p) n -> p k n", p=128)).then_inc(loaded, 16)

                    pairs = [((0, 7), 0)] + [((4 + i, 1 + i), 2) for i in range(3)]

                    @block.tensor
                    def _(pe):
                        pe.wait_ge(loaded, 32)

                        def mix(t):
                            pe.wait_ge(moved, 2 * (t + 1))
                            if t >= 2:
                                pe.wait_ge(added, 2 * (t - 1))
                            for q, (chunks, w) in enumerate(pairs):
                                for n, c in enumerate(chunks):
                                    last = nc.tensor.matmul(ps[:P, t % 2, MUL * q:MUL * (q + 1)], mT[:, t % 2, c, :],
                                                            W[:, w + n, :], start=n == 0, stop=n == 1)
                            last.then_inc(done, 1)

                        for t in range(TILES):
                            if t >= 2:
                                pe.wait_ge(moved, 2 * (t - 1))
                            for half in range(2):
                                for c in range(4):
                                    last = nc.tensor.transpose(turn_ps[:, 2 * (t % 2) + half, P * c:P * (c + 1)],
                                                               MSG[:, t, 128 * (4 * half + c):128 * (4 * half + c + 1)], ident[:P, :P])
                                last.then_inc(turned, 1)
                            if t >= 1:
                                mix(t - 1)
                        mix(TILES - 1)

                    @block.scalar
                    def _(act):
                        for t in range(TILES):
                            if t >= 2:
                                act.wait_ge(done, t - 1)
                            for half in range(2):
                                act.wait_ge(turned, 2 * t + half + 1)
                                nc.scalar.activation(mT[:, t % 2, 4 * half:4 * half + 4, :],
                                                     turn_ps[:, 2 * (t % 2) + half, 0:4 * P].rearrange("p (c n) -> p c n", c=4),
                                                     ACT.Copy).then_inc(moved, 1)

                    @block.vector
                    def _(dve):
                        scale = 1 / (math.sqrt(2 * MUL) * 10.0)
                        for t in range(TILES):
                            dve.wait_ge(done, t + 1)
                            xs, xv = X[:, t, 0:MUL], X[:, t, MUL:DIM].rearrange("p (v m) -> p m v", m=3)
                            nc.vector.scalar_tensor_tensor(out=xs, in0=ps[:P, t % 2, 0:MUL], scalar=scale, in1=xs,
                                                           op0=ALU.mult, op1=ALU.add).then_inc(added, 1)
                            nc.vector.scalar_tensor_tensor(out=xv, in0=ps[:P, t % 2, MUL:DIM].rearrange("p (m v) -> p m v", m=3),
                                                           scalar=scale, in1=xv, op0=ALU.mult, op1=ALU.add).then_inc(added, 1)

        def place_nodes(bestI, slots, expertI):
            with ExitStack() as st:
                sb, pb = tile_in(st), bank_in(st)
                steps, oh_ready, totals = sems_in(st)("place_steps", "one_hots_ready", "totals_ready")
                wide = [P, TILES, EXPERTS]
                idxF = sb("idxF", [P, TILES])
                oh, before_me = sb("oh", wide), sb("before_me", wide)
                n, grp, gI, start = (sb("n", [P, EXPERTS]), sb("grp", [P, EXPERTS]), sb("gI", [P, EXPERTS], I32),
                                     sb("start", [P, EXPERTS]))
                slotF, ef = sb("slotF", [P, TILES]), sb("ef", [P, TT1])
                ps = pb("ps", [128, 2, 512])
                with nc.Block() as block:
                    @block.vector
                    def _(dve):
                        step = Chain(dve, steps)
                        step(nc.vector.tensor_copy(idxF[:], bestI[:, :, 0]))
                        nc.vector.tensor_tensor(oh[:], count[:P, 0:EXPERTS].unsqueeze(1).to_broadcast(wide),
                                                idxF[:].unsqueeze(2).to_broadcast(wide), ALU.is_equal).then_inc(oh_ready, 1)
                        dve.wait_ge(totals, 1)
                        step(nc.vector.tensor_copy(before_me[:], ps[:P, 0, 0:TILES * EXPERTS].rearrange("p (t e) -> p t e", t=TILES)))
                        step(nc.vector.memset(n[:], 0.0))
                        for t in range(TILES):
                            step(nc.vector.tensor_tensor(before_me[:, t, :], before_me[:, t, :], n[:], ALU.add))
                            step(nc.vector.tensor_tensor(n[:], n[:], ps[:P, 1, EXPERTS * t:EXPERTS * (t + 1)], ALU.add))
                        step(nc.vector.tensor_scalar(gI[:], n[:], float(LANES - 1), None, ALU.add))
                        step(nc.vector.tensor_scalar(gI[:], gI[:], int(math.log2(LANES)), None, ALU.arith_shift_right))
                        step(nc.vector.tensor_copy(grp[:], gI[:]))
                        step(nc.vector.tensor_tensor_scan(start[:], ones[:P, 0:EXPERTS], grp[:], 0.0, ALU.mult, ALU.add))
                        step(nc.vector.tensor_tensor(start[:], start[:], grp[:], ALU.subtract))
                        step(nc.vector.tensor_scalar(ef[:], count[:P, 0:TT1], start[:, 1:2], None, ALU.is_ge))
                        for e in range(2, EXPERTS):
                            step(nc.vector.scalar_tensor_tensor(out=ef[:], in0=count[:P, 0:TT1], scalar=start[:, e:e + 1], in1=ef[:],
                                                                op0=ALU.is_ge, op1=ALU.add))
                        step(nc.vector.tensor_copy(expertI[:], ef[:]))
                        step(nc.vector.tensor_scalar(start[:], start[:], float(LANES), None, ALU.mult))
                        step(nc.vector.tensor_tensor(before_me[:], before_me[:], start[:].unsqueeze(1).to_broadcast(wide), ALU.add))
                        step(nc.vector.tensor_tensor(before_me[:], before_me[:], oh[:], ALU.mult))
                        step(nc.vector.tensor_reduce(slotF[:], before_me[:], X_AXIS, ALU.add))
                        step(nc.vector.tensor_copy(slots[:, :, 0], slotF[:]))

                    @block.tensor
                    def _(pe):
                        pe.wait_ge(oh_ready, 1)
                        flat = oh[:].rearrange("p t e -> p (t e)")
                        nc.tensor.matmul(ps[:P, 0, 0:TILES * EXPERTS], before[:P, :P], flat, start=True, stop=True)
                        nc.tensor.matmul(ps[:P, 1, 0:TILES * EXPERTS], ones[:P, :P], flat, start=True, stop=True).then_inc(totals, 1)

        def experts1(expertI):
            UNITS = 4
            ITERS = TT1 // 2
            FC = FF1 // 128
            with ExitStack() as st:
                sb, pb = tile_in(st), bank_in(st)
                loaded = sems_in(st)(*[f"unit_loaded{u}" for u in range(UNITS)])
                stored = sems_in(st)(*[f"unit_stored{u}" for u in range(UNITS)])
                b_loaded, b_turned, b_ready, x_turned, x_moved, hid_done, hid_moved, y_done, y_moved, y_free, tick = sems_in(st)(
                    "b_loaded", "b_turned", "b_ready", "x_turned", "x_moved", "hid_done", "hid_moved", "y_done", "y_moved",
                    "y_free", "tick")
                xe = [sb(f"xe{u}", [128, DIM]) for u in range(UNITS)]
                W1 = [sb(f"W1_{u}", [128, KC, FF1]) for u in range(UNITS)]
                W2 = [sb(f"W2_{u}", [128, FC, DIM]) for u in range(UNITS)]
                b2B = [sb(f"b2B{u}", [128, DIM]) for u in range(UNITS)]
                ye = [sb(f"ye{u}", [128, DIM]) for u in range(UNITS)]
                b1raw, b1T = sb("b1raw", [2 * EXPERTS * FC, 128]), sb("b1T", [128, 2 * EXPERTS, FC])
                xT, hid = sb("xT", [128, 2, KC, 128]), sb("hid", [128, 2, FC, 128])
                turn_ps, hid_ps, y_ps = pb("turn_ps", [128, 2, 512]), pb("hid_ps", [128, 2, 512]), pb("y_ps", [128, 2, 512])
                with nc.Block() as block:
                    def expert_of(engine, r, u):
                        b = u % 2
                        return engine.value_load(expertI[b][0:1, bass.ds(2 * r + u // 2, 1)], min_val=0, max_val=EXPERTS - 1)

                    @block.sync
                    def _(sp):
                        for b, bank in enumerate(BANKS):
                            n = EXPERTS * FC
                            sp.dma_start(b1raw[n * b:n * (b + 1), :], I[f"L1_ffn_b1_{bank}"].rearrange("e (m p) -> (e m) p", p=128)
                                         ).then_inc(b_loaded, 16)
                        sp.sem_inc(y_moved, UNITS)
                        with sp.Fori(0, ITERS) as r:
                            for u in range(UNITS):
                                bank = BANKS[u % 2]
                                e = expert_of(sp, r, u)
                                sp.wait_ge(y_moved, UNITS * r + u + 1)
                                sp.sem_inc(tick, 1)
                                sp.dma_start(xe[u][:], xin1[bank][bass.ds((2 * r + u // 2) * LANES, LANES), :]).then_inc(loaded[u], 16)
                                sp.dma_start(W1[u][:], I[f"L1_ffn_W1_{bank}"][bass.ds(e, 1)].rearrange("a (k p) n -> p (a k) n", p=128)
                                             ).then_inc(loaded[u], 16)
                                sp.dma_start(W2[u][:], I[f"L1_ffn_W2_{bank}"][bass.ds(e, 1)].rearrange("a (k p) n -> p (a k) n", p=128)
                                             ).then_inc(loaded[u], 16)
                                sp.dma_start(b2B[u][:], I[f"L1_ffn_b2_{bank}"][bass.ds(e, 1), :].broadcast_to([128, DIM])
                                             ).then_inc(loaded[u], 16)

                    @block.gpsimd
                    def _(pool):
                        with pool.Fori(0, ITERS) as r:
                            for u in range(UNITS):
                                pool.wait_ge(y_moved, UNITS * (r + 1) + u + 1)
                                pool.sem_inc(tick, 1)
                                pool.dma_start(yout1[BANKS[u % 2]][bass.ds((2 * r + u // 2) * LANES, LANES), :], ye[u][:]
                                               ).then_inc(stored[u], 16)
                                pool.wait_ge(stored[u], 16 * (r + 1))
                                pool.sem_inc(y_free, 1)

                    @block.tensor
                    def _(pe):
                        pe.wait_ge(b_loaded, 32)
                        nb = 2 * EXPERTS * FC
                        nc.tensor.transpose(y_ps[:, 0, 0:nb], b1raw[:], ident[:nb, :nb]).then_inc(b_turned, 1)
                        pe.wait_ge(b_ready, 1)

                        def turn(r, u):
                            n = UNITS * r + u
                            pe.wait_ge(loaded[u], 64 * (r + 1))
                            if u >= 2:
                                pe.wait_ge(x_moved, n - 1)
                            for k in range(KC):
                                last = nc.tensor.transpose(turn_ps[:, u % 2, 128 * k:128 * (k + 1)],
                                                           xe[u][:, 128 * k:128 * (k + 1)], ident[:])
                            last.then_inc(x_turned, 1)

                        def up(r, u):
                            n = UNITS * r + u
                            pe.wait_ge(x_moved, n + 1)
                            for m in range(FC):
                                for k in range(KC):
                                    last = nc.tensor.matmul(hid_ps[:, u % 2, 128 * m:128 * (m + 1)], W1[u][:, k, 128 * m:128 * (m + 1)],
                                                            xT[:, u % 2, k, :], start=k == 0, stop=k == KC - 1)
                            last.then_inc(hid_done, 1)

                        def down(r, u):
                            n = UNITS * r + u
                            pe.wait_ge(hid_moved, FC * (n + 1))
                            pe.wait_ge(y_moved, n - 2 + UNITS + 1)
                            for m in range(FC):
                                last = nc.tensor.matmul(y_ps[:, u % 2, :], hid[:, u % 2, m, :], W2[u][:, m, :],
                                                        start=m == 0, stop=m == FC - 1)
                            last.then_inc(y_done, 1)

                        with pe.Fori(0, ITERS) as r:
                            for s in range(UNITS + 2):
                                if s < UNITS:
                                    turn(r, s)
                                if 1 <= s <= UNITS:
                                    up(r, s - 1)
                                if s >= 2:
                                    down(r, s - 2)

                    @block.scalar
                    def _(act):
                        act.wait_ge(b_turned, 1)
                        nc.scalar.activation(b1T[:], y_ps[:, 0, 0:2 * EXPERTS * FC].rearrange("p (e m) -> p e m", m=FC),
                                             ACT.Copy).then_inc(b_ready, 1)
                        act.wait_ge(b_ready, 1)
                        with act.Fori(0, ITERS) as r:
                            for s in range(UNITS + 1):
                                if s < UNITS:
                                    n = UNITS * r + s
                                    act.wait_ge(x_turned, n + 1)
                                    if s >= 2:
                                        act.wait_ge(hid_done, n - 1)
                                    nc.scalar.activation(xT[:, s % 2, :, :], turn_ps[:, s % 2, :].rearrange("p (k n) -> p k n", k=KC),
                                                         ACT.Copy).then_inc(x_moved, 1)
                                if s >= 1:
                                    u = s - 1
                                    n = UNITS * r + u
                                    e = expert_of(act, r, u)
                                    act.wait_ge(hid_done, n + 1)
                                    if u >= 2:
                                        act.wait_ge(y_done, n - 1)
                                    for m in range(FC):
                                        nc.scalar.activation(hid[:, u % 2, m, :], hid_ps[:, u % 2, 128 * m:128 * (m + 1)], ACT.Gelu,
                                                             bias=b1T[:, bass.ds(e + EXPERTS * (u % 2), 1), m:m + 1].rearrange("p a b -> p (a b)")
                                                             ).then_inc(hid_moved, 1)

                    @block.vector
                    def _(dve):
                        dve.sem_inc(y_free, UNITS)
                        with dve.Fori(0, ITERS) as r:
                            for u in range(UNITS):
                                dve.wait_ge(y_done, UNITS * r + u + 1)
                                dve.wait_ge(y_free, UNITS * r + u + 1)
                                nc.vector.tensor_tensor(ye[u][:], y_ps[:, u % 2, :], b2B[u][:], ALU.add).then_inc(y_moved, 1)

        def move(target, source):
            with ExitStack() as st:
                (moved,) = sems_in(st)("array_moved")
                with nc.Block() as block:
                    @block.sync
                    def _(sp):
                        sp.dma_start(target, source).then_inc(moved, 16)
                        sp.wait_ge(moved, 16)

        RECS = sb("RECS", [128, GROUPS + 1, EPP, REC])
        whole_x = I["x"].rearrange("(t p) d -> p t d", p=P)

        with ExitStack() as outer:
            A = tile_in(outer)("A", [P, TILES, DIM])
            with ExitStack() as attention:
                sb1 = tile_in(attention)
                QT, KT, V = sb1("QT", [128, KC, NODES]), sb1("KT", [128, KC, NODES]), sb1("V", [P, TILES, DIM])
                with ExitStack() as early:
                    sb2 = tile_in(early)
                    pos, recs = sb2("pos", [P, ECOLS], I32), sb2("recs", [P, ECOLS, REC])
                    order_edges(pos, recs)
                    records = record_scatter(early, pos, recs)
                    layer_norm(X, X, pool_work=records(0, 3))
                    HT = sb2("HT", [128, KC, NODES])
                    transpose_all(X, HT, pool_work=records(3, 5))
                    qkv(HT, QT, KT, V, records(5, ECOLS // 8))
                LA, has = sb1("LA", [P, TILES, NODES]), sb1("has", [P, TILES])
                count_edges(LA, has, RECS)
                attend(QT, KT, V, LA, has, A)
            with ExitStack() as post:
                sb1 = tile_in(post)
                T, R, hT = sb1("T", [128, KC, NODES]), sb1("R", [P, TILES, DIM]), sb1("hT", [128, 2, NODES])
                transpose_all(A, T)
                node_major_product(T, I["L0_gnn_Wo"], KC, R, add=X)
                layer_norm(R, R, I["L0_gnn_ln1_g"], I["L0_gnn_ln1_b"])
                transpose_all(R, T)
                feature_major_layer(T, I["L0_gnn_W1"], I["L0_gnn_b1"], hT, 2, ACT.Relu)
                node_major_product(hT, I["L0_gnn_W2"], 2, R, bias=I["L0_gnn_b2"], add=R)
                move(X[:], whole_x)
                layer_norm(R, R, I["L0_gnn_ln2_g"], I["L0_gnn_ln2_b"], add_to=X)
        recycle()
        with ExitStack() as moe:
            sb1 = tile_in(moe)
            best, bestI = sb1("best", [P, TILES, 8]), sb1("bestI", [P, TILES, 8], U32)
            weight = sb1("weight", [P, TILES, 2])
            slot_in, slot_out = sb1("slot_in", [P, TILES, 2], I32), sb1("slot_out", [P, TILES, 2], I32)
            with ExitStack() as routing:
                sb2 = tile_in(routing)
                N, NT, probs = sb2("N", [P, TILES, DIM]), sb2("NT", [128, KC, NODES]), sb2("probs", [P, TILES, EXPERTS])
                layer_norm(X, N)
                transpose_all(N, NT)
                gate(NT, I["L0_ffn_gate_w"], True, I["L0_ffn_gate_b"], probs, best, bestI)
                place_choices(best, bestI, weight, slot_in, slot_out)
                scatter_rows(N, slot_in, 2, xin0)
            experts0()
            combine([(yout0, lambda t, c=c: slot_out[:, t, c:c + 1], lambda t, c=c: weight[:, t, c:c + 1]) for c in range(2)])
        recycle()
        with ExitStack() as graph:
            sb1 = tile_in(graph)
            with ExitStack() as up:
                sb2 = tile_in(up)
                N, NT = sb2("N", [P, TILES, DIM]), sb2("NT", [128, KC, NODES])
                layer_norm(X, N)
                transpose_all(N, NT, [lambda t: N[:, t, 0:MUL]] + [lambda t, m=m: N[:, t, MUL + m:DIM:3] for m in range(3)])
                mix_up(NT)
            MSG = sb1("MSG", [P, TILES, 2 * DIM])
            messages(RECS, MSG)
            mix_out(MSG)
        with ExitStack() as ffn:
            sb1 = tile_in(ffn)
            gates, slots, experts = [], [], []
            for b in range(2):
                gates.append(sb1(f"best{b}", [P, TILES, 8]))
                slots.append(sb1(f"slots{b}", [P, TILES, 1], I32))
                experts.append(sb1(f"expertI{b}", [P, TT1], I32))
            with ExitStack() as routing:
                sb2 = tile_in(routing)
                N, NT, hT = sb2("N", [P, TILES, DIM]), sb2("NT", [128, KC, NODES]), sb2("hT", [128, 2, NODES])
                probs, bestI = sb2("probs", [P, TILES, EXPERTS]), sb2("bestI", [P, TILES, 8], U32)
                layer_norm(X, N)
                transpose_all(N, NT)
                for b, bank in enumerate(BANKS):
                    gate(NT, I[f"L1_ffn_Wr_{bank}"], False, I[f"L1_ffn_br_{bank}"], probs, gates[b], bestI)
                    place_nodes(bestI, slots[b], experts[b])
                    scatter_rows(N, slots[b], 1, xin1[bank])
                feature_major_layer(NT, I["L1_ffn_Ws1"], I["L1_ffn_bs1"], hT, 2, ACT.Gelu)
                node_major_product(hT, I["L1_ffn_Ws2"], 2, X, bias=I["L1_ffn_bs2"], add=X)
            experts1(experts)
            combine([(yout1[bank], lambda t, b=b: slots[b][:, t, 0:1], lambda t, b=b: gates[b][:, t, 0:1])
                     for b, bank in enumerate(BANKS)])
        move(out.rearrange("(t p) d -> p t d", p=P), X[:])


_INS = ['x', 'src', 'dst', 'edge_attr_4', 'edge_attr_8', 'L0_gnn_Wq', 'L0_gnn_Wk', 'L0_gnn_Wv', 'L0_gnn_Wo',
        'L0_gnn_ln1_g', 'L0_gnn_ln1_b', 'L0_gnn_ln2_g', 'L0_gnn_ln2_b', 'L0_gnn_W1', 'L0_gnn_b1', 'L0_gnn_W2',
        'L0_gnn_b2', 'L0_ffn_gate_w', 'L0_ffn_gate_b', 'L0_ffn_w1', 'L0_ffn_b1', 'L0_ffn_w2', 'L0_ffn_b2',
        'L1_gnn_W_up0', 'L1_gnn_W_up1', 'L1_gnn_W_mlp1', 'L1_gnn_W_mlp2', 'L1_gnn_W_mlp3', 'L1_gnn_W_mlp4',
        'L1_gnn_W_out0', 'L1_gnn_W_out1', 'L1_ffn_Wr_sp', 'L1_ffn_br_sp', 'L1_ffn_Wr_fq', 'L1_ffn_br_fq',
        'L1_ffn_Ws1', 'L1_ffn_bs1', 'L1_ffn_Ws2', 'L1_ffn_bs2', 'L1_ffn_W1_sp', 'L1_ffn_b1_sp', 'L1_ffn_W2_sp',
        'L1_ffn_b2_sp', 'L1_ffn_W1_fq', 'L1_ffn_b1_fq', 'L1_ffn_W2_fq', 'L1_ffn_b2_fq']


def kernel(**inputs):
    import numpy as _np
    import concourse.bacc as _bacc
    from concourse import mybir as _mybir
    from concourse.bass_utils import run_bass_kernel_spmd as _run

    nc = _bacc.Bacc("TRN2", target_bir_lowering=False, num_devices=1)
    arrays, args = {}, {}
    for name in _INS:
        a = _np.ascontiguousarray(inputs[name])
        arrays[f"in_{name}"] = a
        args[name] = nc.dram_tensor(f"in_{name}", a.shape, _mybir.dt.from_np(a.dtype), kind="ExternalInput").ap()
    out = nc.dram_tensor("out_0", (NODES, DIM), F32, kind="ExternalOutput").ap()
    gnn_moe_gnn_moe(nc, args, out)
    return _run(nc, [arrays], core_ids=[0]).results[0]["out_0"]
```

```python
import math
from contextlib import ExitStack

import concourse.bass as bass
from concourse import mybir

F32 = mybir.dt.float32
F16 = mybir.dt.float16
F32R = mybir.dt.float32r
I32 = mybir.dt.int32
U32 = mybir.dt.uint32
ALU = mybir.AluOpType
ACT = mybir.ActivationFunctionType
X_AXIS = mybir.AxisListType.X

NODES, DIM, EDGES = 1250, 512, 20000
P = 125
TILES = NODES // P
KC = DIM // 128
HEADS, DK = 8, 64
ECOLS = EDGES // P
LANES, EPP = 128, 4
GROUP = LANES * EPP
GROUPS = (EDGES + TILES * (GROUP - 1)) // GROUP
GROUPS += GROUPS % 2
SLOTS = GROUPS * GROUP
REC = 16
EPS = 1e-5
CHUNKS = [(0, 512), (512, 512), (1024, NODES - 1024)]
EXPERTS = 8
CAP0 = int(1.2 * NODES / EXPERTS)
ROWS0 = CAP0 + 1
HALF0 = ROWS0 // 2
HID0 = 2048
MC0 = HID0 // 128
FF1 = 256
TT1 = (NODES + EXPERTS * (LANES - 1)) // LANES
TT1 += TT1 % 2
ROWS1 = TT1 * LANES
BANKS = ("sp", "fq")
SILU_2MOM = 1.679177
MUL = 128


class Chain:

    def __init__(self, engine, done):
        self.engine, self.done, self.n = engine, done, 0

    def __call__(self, instruction):
        instruction.then_inc(self.done, 1)
        self.n += 1
        self.engine.wait_ge(self.done, self.n)


def gnn_moe_gnn_moe(nc, I, out):
    top = ExitStack()

    used = {}

    def fresh(name):
        used[name] = used.get(name, 0) + 1
        return name if used[name] == 1 else f"{name}_{used[name]}"

    def tile_in(stack):
        return lambda name, shape, dt=F32: stack.enter_context(nc.sbuf_tensor(fresh(name), shape, dt))

    def bank_in(stack):
        return lambda name, shape, dt=F32: stack.enter_context(nc.psum_tensor(fresh(name), shape, dt))

    finished = []

    def sems_in(stack):
        def allocate(*names):
            handles = [nc.alloc_semaphore(name=fresh(n)) for n in names]
            stack.callback(finished.extend, handles)
            return handles
        return allocate

    def recycle():
        nc.clear_and_free_semaphores(finished)
        finished.clear()
        nc.all_engine_barrier()

    def row(ap):
        return ap.rearrange("(a n) -> a n", a=1)

    def dram(name, shape, dt=F32):
        return nc.dram_tensor(name, shape, dt, kind="Internal").ap()

    rec_dram = dram("rec_dram", (SLOTS, REC))
    q_dram = dram("q_dram", (DK, HEADS, NODES))
    up_dram = dram("up_dram", (NODES, DIM))
    xin0 = dram("xin0", (EXPERTS * ROWS0 + 2 * NODES, DIM))
    yout0 = dram("yout0", (EXPERTS * ROWS0, DIM))
    xin1 = {b: dram("xin1_" + b, (ROWS1, DIM)) for b in BANKS}
    yout1 = {b: dram("yout1_" + b, (ROWS1, DIM)) for b in BANKS}

    with top:
        sb = tile_in(top)
        X = sb("X", [P, TILES, DIM])
        ident = sb("ident", [128, 128])
        ones = sb("ones", [128, 128])
        before = sb("before", [128, 128])
        earlier = sb("earlier", [128, 128])
        zeros = sb("zeros", [128, DIM])
        count = sb("count", [128, 64])
        tiny = sb("tiny", [128, 1])
        blockI = sb("blockI", [P, GROUPS + 1], I32)

        def order_edges(pos, recs):
            with ExitStack() as st:
                sb, pb = tile_in(st), bank_in(st)
                loaded, consts, routed, rows_ready, totals, filled, fill_ready = sems_in(st)(
                    "edges_loaded", "consts_ready", "routed", "rows_ready", "totals_ready", "rec_filled", "fill_ready")
                srcI, dstI = sb("srcI", [P, ECOLS], I32), sb("dstI", [P, ECOLS], I32)
                a4, a8 = sb("a4", [P, ECOLS, 4]), sb("a8", [P, ECOLS, 8])
                dstF = sb("dstF", [P, ECOLS])
                ge = sb("ge", [P, TILES + 1, ECOLS])
                oh = sb("oh", [P, TILES, ECOLS])
                cum = sb("cum", [P, TILES, ECOLS])
                blk = sb("blk", [P, ECOLS])
                onesE = sb("onesE", [P, ECOLS])
                base, grp, gI, start = (sb("base", [P, TILES]), sb("grp", [P, TILES]),
                                        sb("gI", [P, TILES], I32), sb("start", [P, TILES]))
                rows = sb("rows", [P, TILES])
                posF = sb("posF", [P, ECOLS])
                bf = sb("bf", [P, GROUPS])
                fill = sb("fill", [128, SLOTS // 128, REC])
                ps = pb("ps", [128, 2, 512])
                with nc.Block() as block:
                    @block.sync
                    def _(sp):
                        sp.dma_start(srcI[:], I["src"].rearrange("(p c) -> p c", p=P)).then_inc(loaded, 16)
                        sp.dma_start(dstI[:], I["dst"].rearrange("(p c) -> p c", p=P)).then_inc(loaded, 16)
                        sp.dma_start(a4[:], I["edge_attr_4"].rearrange("(p c) f -> p c f", p=P)).then_inc(loaded, 16)
                        sp.dma_start(a8[:], I["edge_attr_8"].rearrange("(p c) f -> p c f", p=P)).then_inc(loaded, 16)
                        sp.dma_start(X[:], I["x"].rearrange("(t p) d -> p t d", p=P)).then_inc(loaded, 16)
                        sp.wait_ge(fill_ready, 1)
                        sp.dma_start(rec_dram.rearrange("(p c) w -> p c w", p=128), fill[:]).then_inc(filled, 16)
                        sp.wait_ge(loaded, 80)
                        sp.wait_ge(filled, 16)

                    @block.gpsimd
                    def _(pool):
                        nc.gpsimd.memset(ident[:], 0.0)
                        nc.gpsimd.memset(before[:], 0.0)
                        nc.gpsimd.memset(earlier[:], 0.0)
                        nc.gpsimd.memset(ones[:], 1.0)
                        nc.gpsimd.memset(zeros[:], 0.0)
                        nc.gpsimd.memset(tiny[:], EPS)
                        nc.gpsimd.memset(onesE[:], 1.0)
                        nc.gpsimd.iota(count[:], pattern=[[1, 64]], base=0, channel_multiplier=0,
                                       allow_small_or_imprecise_dtypes=True).then_inc(consts, 1)
                        pool.wait_ge(consts, 1)
                        nc.gpsimd.affine_select(out=ident[:], in_=ident[:], compare_op=ALU.not_equal, fill=1.0,
                                                base=0, pattern=[[-1, 128]], channel_multiplier=1)
                        nc.gpsimd.affine_select(out=before[:], in_=before[:], compare_op=ALU.is_ge, fill=1.0,
                                                base=0, pattern=[[-1, 128]], channel_multiplier=1)
                        nc.gpsimd.affine_select(out=earlier[:], in_=earlier[:], compare_op=ALU.is_ge, fill=1.0,
                                                base=0, pattern=[[1, 128]], channel_multiplier=-1).then_inc(consts, 1)

                    @block.vector
                    def _(dve):
                        step = Chain(dve, routed)
                        step(nc.vector.memset(fill[:], 0.0))
                        nc.vector.memset(fill[:, :, 1:2], -1.0).then_inc(fill_ready, 1)
                        dve.wait_ge(loaded, 80)
                        step(nc.vector.tensor_copy(dstF[:], dstI[:]))
                        step(nc.vector.tensor_copy(recs[:, :, 0], srcI[:]))
                        for b in range(TILES):
                            nc.vector.tensor_scalar(ge[:, b, :], dstF[:], float(P * b), None, ALU.is_ge)
                        nc.vector.tensor_copy(recs[:, :, 4:8], a4[:])
                        nc.vector.tensor_copy(recs[:, :, 8:16], a8[:])
                        nc.vector.memset(recs[:, :, 2:4], 0.0)
                        step(nc.vector.memset(ge[:, TILES, :], 0.0))
                        step(nc.vector.tensor_tensor(oh[:], ge[:, 0:TILES, :], ge[:, 1:TILES + 1, :], ALU.subtract))
                        step(nc.vector.tensor_reduce(blk[:], ge[:, 1:TILES, :].rearrange("p b c -> p c b"), X_AXIS, ALU.add))
                        step(nc.vector.scalar_tensor_tensor(out=recs[:, :, 1], in0=blk[:], scalar=-float(P), in1=dstF[:],
                                                            op0=ALU.mult, op1=ALU.add))
                        dve.wait_ge(consts, 2)
                        for b in range(TILES):
                            scan = nc.vector.tensor_tensor_scan(cum[:, b, :], onesE[:], oh[:, b, :], 0.0, ALU.mult, ALU.add)
                        step(scan)
                        nc.vector.tensor_copy(rows[:], cum[:, :, ECOLS - 1]).then_inc(rows_ready, 1)
                        dve.wait_ge(totals, 1)
                        step(nc.vector.tensor_scalar(gI[:], ps[:P, 1, 0:TILES], float(GROUP - 1), None, ALU.add))
                        step(nc.vector.tensor_scalar(gI[:], gI[:], int(math.log2(GROUP)), None, ALU.arith_shift_right))
                        step(nc.vector.tensor_copy(grp[:], gI[:]))
                        step(nc.vector.tensor_tensor_scan(start[:], onesE[:, 0:TILES], grp[:], 0.0, ALU.mult, ALU.add))
                        step(nc.vector.tensor_tensor(start[:], start[:], grp[:], ALU.subtract))
                        step(nc.vector.scalar_tensor_tensor(out=base[:], in0=start[:], scalar=float(GROUP),
                                                            in1=ps[:P, 0, 0:TILES], op0=ALU.mult, op1=ALU.add))
                        for b in range(TILES):
                            nc.vector.scalar_tensor_tensor(out=ge[:, b, :], in0=cum[:, b, :], scalar=base[:, b:b + 1],
                                                           in1=oh[:, b, :], op0=ALU.add, op1=ALU.mult)
                        step(nc.vector.tensor_scalar(bf[:], count[:P, 0:GROUPS], start[:, 1:2], None, ALU.is_ge))
                        step(nc.vector.tensor_reduce(posF[:], ge[:, 0:TILES, :].rearrange("p b c -> p c b"), X_AXIS, ALU.add))
                        step(nc.vector.tensor_scalar(pos[:], posF[:], -1.0, None, ALU.add))
                        for b in range(2, TILES):
                            step(nc.vector.scalar_tensor_tensor(out=bf[:], in0=count[:P, 0:GROUPS], scalar=start[:, b:b + 1],
                                                                in1=bf[:], op0=ALU.is_ge, op1=ALU.add))
                        nc.vector.memset(blockI[:, 0:1], 0)
                        step(nc.vector.tensor_copy(blockI[:, 1:GROUPS + 1], bf[:]))

                    @block.tensor
                    def _(pe):
                        pe.wait_ge(consts, 2)
                        pe.wait_ge(rows_ready, 1)
                        nc.tensor.matmul(ps[:P, 0, 0:TILES], before[:P, :P], rows[:], start=True, stop=True)
                        nc.tensor.matmul(ps[:P, 1, 0:TILES], ones[:P, :P], rows[:], start=True, stop=True).then_inc(totals, 1)

        def layer_norm(src, dst, gain=None, shift=None, add_to=None, turned_to=None, chunks=None, pool_work=None):
            with ExitStack() as st:
                sb = tile_in(st)
                stats_done, root_done, steps, params, applied = sems_in(st)(
                    "ln_stats", "ln_root", "ln_steps", "ln_params", "ln_applied")
                stats = sb("stats", [P, TILES, 6])
                mv = sb("mv", [P, TILES, 2])
                root, rstd = sb("root", [P, TILES]), sb("rstd", [P, TILES])
                if gain is not None:
                    gainB, shiftB = sb("gainB", [P, DIM]), sb("shiftB", [P, DIM])
                pe_part, act_part = turning(st, dst, turned_to, chunks, applied) if turned_to is not None else (None, None)
                with nc.Block() as block:
                    if pool_work is not None:
                        block.gpsimd(pool_work)

                    if pe_part is not None:
                        block.tensor(pe_part)

                    if gain is not None:
                        @block.sync
                        def _(sp):
                            sp.dma_start(gainB[:], row(gain).broadcast_to([P, DIM])).then_inc(params, 16)
                            sp.dma_start(shiftB[:], row(shift).broadcast_to([P, DIM])).then_inc(params, 16)

                    @block.vector
                    def _(dve):
                        step = Chain(dve, steps)
                        for t in range(TILES):
                            stat = nc.vector.bn_stats(stats[:, t, :], src[:, t, :])
                        step(stat)
                        for t in range(TILES):
                            aggr = nc.vector.bn_aggr(mv[:, t, :], stats[:, t, :])
                        aggr.then_inc(stats_done, 1)
                        dve.wait_ge(root_done, 1)
                        step(nc.vector.reciprocal(rstd[:], root[:]))
                        if gain is None:
                            for t in range(TILES):
                                nc.vector.tensor_scalar(dst[:, t, :], src[:, t, :], mv[:, t, 0:1], rstd[:, t:t + 1],
                                                        ALU.subtract, ALU.mult).then_inc(applied, 1)
                        else:
                            dve.wait_ge(params, 32)
                            for t in range(TILES):
                                step(nc.vector.scalar_tensor_tensor(out=dst[:, t, :], in0=src[:, t, :], scalar=mv[:, t, 0:1],
                                                                    in1=gainB[:], op0=ALU.subtract, op1=ALU.mult))
                                nc.vector.scalar_tensor_tensor(out=dst[:, t, :], in0=dst[:, t, :], scalar=rstd[:, t:t + 1],
                                                               in1=shiftB[:], op0=ALU.mult, op1=ALU.add).then_inc(applied, 1)
                        if add_to is not None:
                            for t in range(TILES):
                                dve.wait_ge(applied, t + 1)
                                nc.vector.tensor_tensor(add_to[:, t, :], dst[:, t, :], add_to[:, t, :], ALU.add)

                    @block.scalar
                    def _(act):
                        act.wait_ge(stats_done, 1)
                        nc.scalar.activation(root[:], mv[:, :, 1], ACT.Sqrt, bias=tiny[:P, :]).then_inc(root_done, 1)
                        if act_part is not None:
                            act_part(act)

        def turning(stack, src, dst, chunks, ready=None):
            chunks = chunks or [lambda t, k=k: src[:, t, 128 * k:128 * (k + 1)] for k in range(KC)]
            ps = bank_in(stack)("ps", [128, 4, 512])
            turned, moved = sems_in(stack)("turned", "moved")
            n = len(chunks)

            def pe_part(pe):
                for t in range(TILES):
                    if ready is not None:
                        pe.wait_ge(ready, t + 1)
                    if t >= 4:
                        pe.wait_ge(moved, t - 3)
                    for k in range(n):
                        last = nc.tensor.transpose(ps[:, t % 4, P * k:P * (k + 1)], chunks[k](t), ident[:P, :P])
                    last.then_inc(turned, 1)

            def act_part(act):
                for t in range(TILES):
                    act.wait_ge(turned, t + 1)
                    nc.scalar.activation(dst[:, :, P * t:P * (t + 1)],
                                         ps[:, t % 4, 0:n * P].rearrange("p (k c) -> p k c", k=n),
                                         ACT.Copy).then_inc(moved, 1)

            return pe_part, act_part

        def transpose_all(src, dst):
            with ExitStack() as st:
                pe_part, act_part = turning(st, src, dst, None)
                with nc.Block() as block:
                    block.tensor(pe_part)
                    block.scalar(act_part)

        def record_scatter(stack, pos, recs):
            COLS = 4
            staged, tick = sems_in(stack)("rec_staged", "tick")
            scattered = sems_in(stack)("rec_scattered0", "rec_scattered1")
            pos_st = [tile_in(stack)(f"pos_st{b}", [P, COLS], I32) for b in range(2)]
            rec_st = [tile_in(stack)(f"rec_st{b}", [P, COLS, REC]) for b in range(2)]

            def columns(pool, c, b, first):
                m = 2 * c + b
                if not first:
                    pool.wait_ge(scattered[b], 16 * COLS * c)
                    pool.sem_inc(tick, 1)
                nc.gpsimd.tensor_copy(pos_st[b][:], pos[:, bass.ds(m * COLS, COLS)]).then_inc(staged, 1)
                nc.gpsimd.tensor_copy(rec_st[b][:], recs[:, bass.ds(m * COLS, COLS), :]).then_inc(staged, 1)
                pool.wait_ge(staged, 2 * (m + 1))
                pool.sem_inc(tick, 1)
                for k in range(COLS):
                    pool.indirect_dma_start(
                        out=rec_dram, out_offset=bass.IndirectOffsetOnAxis(ap=pos_st[b][:, k:k + 1], axis=0),
                        in_=rec_st[b][:, k, :], in_offset=None).then_inc(scattered[b], 16)

            def part(first, end):
                def program(pool):
                    start = first
                    if start == 0:
                        for b in range(2):
                            columns(pool, 0, b, True)
                        start = 1
                    with pool.Fori(start, end) as c:
                        for b in range(2):
                            columns(pool, c, b, False)
                    if end * 2 * COLS == ECOLS:
                        for b in range(2):
                            pool.wait_ge(scattered[b], 8 * ECOLS)
                return program

            return part

        def qkv(HT, KT, V, pool_work):
            with ExitStack() as st:
                sb, pb = tile_in(st), bank_in(st)
                wload, done, moved, upper_moved, v_moved, q_stored = sems_in(st)(
                    "w_loaded", "product_done", "product_moved", "upper_moved", "values_moved", "queries_stored")
                QT = sb("QT", [128, KC, NODES])
                W = [sb(f"Wqkv{i}", [128, KC, DIM]) for i in range(3)]
                ps = pb("ps", [128, 8, 512])
                jobs = []
                for which in range(2):
                    for j in range(KC):
                        for c0, cn in CHUNKS:
                            jobs.append((which, j, c0, cn))
                for t in range(TILES):
                    jobs.append((2, t, 0, DIM))

                with nc.Block() as block:
                    @block.sync
                    def _(sp):
                        for i, name in enumerate(("L0_gnn_Wq", "L0_gnn_Wk", "L0_gnn_Wv")):
                            sp.dma_start(W[i][:], I[name].rearrange("(k p) n -> p k n", p=128)).then_inc(wload, 16)
                        for j in range(KC):
                            sp.wait_ge(moved, (j + 1) * len(CHUNKS))
                            for half in range(2):
                                sp.dma_start(q_dram[:, 2 * j + half, :], QT[DK * half:DK * (half + 1), j, :]).then_inc(q_stored, 16)
                        sp.wait_ge(q_stored, 32 * KC)

                    block.gpsimd(pool_work)

                    @block.tensor
                    def _(pe):
                        pe.wait_ge(wload, 48)
                        for n, (which, j, c0, cn) in enumerate(jobs):
                            if n >= 8:
                                pe.wait_ge(moved, min(n - 7, 2 * KC * len(CHUNKS)))
                            if n >= 2 * KC * len(CHUNKS) + 8:
                                pe.wait_ge(v_moved, n - 7 - 2 * KC * len(CHUNKS))
                            for k in range(KC):
                                if which < 2:
                                    last = nc.tensor.matmul(ps[:, n % 8, 0:cn], W[which][:, k, 128 * j:128 * (j + 1)],
                                                            HT[:, k, c0:c0 + cn], start=k == 0, stop=k == KC - 1)
                                else:
                                    last = nc.tensor.matmul(ps[:P, n % 8, :], HT[:, k, P * j:P * (j + 1)],
                                                            W[2][:, k, :], start=k == 0, stop=k == KC - 1)
                            last.then_inc(done, 1)

                    @block.scalar
                    def _(act):
                        for n, job in enumerate(jobs):
                            act.wait_ge(done, n + 1)
                            which, j, c0, cn = job
                            if which == 0:
                                nc.scalar.activation(QT[:, j, c0:c0 + cn], ps[:, n % 8, 0:cn], ACT.Copy,
                                                     scale=1.0 / math.sqrt(DK)).then_inc(moved, 1)
                            elif which == 1:
                                for half in range(2):
                                    rows = slice(DK * half, DK * (half + 1))
                                    nc.scalar.activation(KT[rows, 2 * j + half, c0:c0 + cn], ps[rows, n % 8, 0:cn], ACT.Copy
                                                         ).then_inc(upper_moved, 1)
                            else:
                                nc.scalar.activation(V[:, j, :], ps[:P, n % 8, :], ACT.Copy).then_inc(v_moved, 1)

                    @block.vector
                    def _(dve):
                        for m in range(KC * len(CHUNKS)):
                            n = KC * len(CHUNKS) + m
                            _, j, c0, cn = jobs[n]
                            dve.wait_ge(upper_moved, 2 * (m + 1))
                            for half in range(2):
                                rows, others = slice(DK * half, DK * (half + 1)), slice(DK * (1 - half), DK * (2 - half))
                                last = nc.vector.tensor_tensor(KT[others, 2 * j + half, c0:c0 + cn], ps[rows, n % 8, 0:cn],
                                                               KT[rows, 2 * j + half, c0:c0 + cn].bitcast(F32), ALU.subtract)
                            last.then_inc(moved, 1)

        def count_edges(LA, has):
            with ExitStack() as st:
                sb, pb = tile_in(st), bank_in(st)
                RECS = sb("recs_in", [128, GROUPS, EPP, REC])
                loaded, cols, hot, counted, added, cleared, zeroed = sems_in(st)(
                    "recs_loaded", "cols_ready", "one_hots_ready", "counted", "counts_added", "cleared", "zeroed")
                RING = 4
                nodes16 = sb("nodes16", [128, NODES], F16)
                ohS, ohD = sb("ohS", [128, RING, NODES], F16), sb("ohD", [128, RING, P], F16)
                ps = pb("ps", [128, 2, 2048])
                with nc.Block() as block:
                    @block.sync
                    def _(sp):
                        sp.dma_start(RECS[:], rec_dram.rearrange("(g p t) w -> p g t w", p=128, t=EPP)).then_inc(loaded, 16)
                        zeros_in = fill_zeros(sp, xin0, zeroed)
                        for bank in BANKS:
                            zeros_in += fill_zeros(sp, xin1[bank], zeroed)
                        sp.wait_ge(zeroed, zeros_in)

                    @block.gpsimd
                    def _(pool):
                        nc.gpsimd.iota(nodes16[:], pattern=[[1, NODES]], base=0, channel_multiplier=0,
                                       allow_small_or_imprecise_dtypes=True).then_inc(cols, 1)

                    @block.vector
                    def _(dve):
                        def add_counts(block, g, par):
                            dve.wait_ge(counted, EPP * g + RING)
                            dve.wait_ge(added, g + 1)
                            acc = LA[:, bass.ds(block, 1), :].rearrange("p a n -> p (a n)")
                            nc.vector.tensor_tensor(acc, acc, ps[:P, par, 0:NODES], ALU.add).then_inc(added, 1)

                        nc.vector.memset(ps[:, 1, 0:NODES], 0.0).then_inc(added, 1)
                        nc.vector.memset(LA[:], 0.0).then_inc(cleared, 1)
                        dve.wait_ge(cols, 1)
                        dve.wait_ge(loaded, 16)
                        dve.wait_ge(cleared, 1)
                        with dve.Fori(0, GROUPS // 2) as r:
                            for par in range(2):
                                g = 2 * r + par
                                block_before = dve.value_load(blockI[0:1, bass.ds(g, 1)], min_val=0, max_val=TILES - 1)
                                for t in range(EPP):
                                    dve.wait_ge(counted, EPP * g + t + 1)
                                    nc.vector.tensor_scalar(ohS[:, t, :], nodes16[:], RECS[:, bass.ds(g, 1), t, 0:1].rearrange("p a b -> p (a b)"),
                                                            None, ALU.is_equal)
                                    nc.vector.tensor_scalar(ohD[:, t, :], nodes16[:, 0:P], RECS[:, bass.ds(g, 1), t, 1:2].rearrange("p a b -> p (a b)"),
                                                            None, ALU.is_equal).then_inc(hot, 1)
                                    if t == 1:
                                        add_counts(block_before, g, 1 - par)
                        add_counts(dve.value_load(blockI[0:1, GROUPS:GROUPS + 1], min_val=0, max_val=TILES - 1), GROUPS, 1)

                    @block.tensor
                    def _(pe):
                        pe.sem_inc(counted, RING)
                        with pe.Fori(0, GROUPS // 2) as r:
                            for par in range(2):
                                g = 2 * r + par
                                for t in range(EPP):
                                    pe.wait_ge(hot, EPP * g + t + 1)
                                    if t == 0:
                                        pe.wait_ge(added, g + 1)
                                    for c0, cn in CHUNKS:
                                        last = nc.tensor.matmul(ps[:P, par, c0:c0 + cn], ohD[:, t, :], ohS[:, t, c0:c0 + cn],
                                                                start=t == 0, stop=t == EPP - 1)
                                    last.then_inc(counted, 1)

            with ExitStack() as st:
                sb = tile_in(st)
                least, logs, done = sems_in(st)("counts_floored", "logs_ready", "log_steps")
                low, lg = sb("low", [P, 2, NODES]), sb("lg", [P, 2, NODES])
                with nc.Block() as block:
                    @block.vector
                    def _(dve):
                        step = Chain(dve, done)
                        for t in range(TILES):
                            step(nc.vector.tensor_reduce(has[:, t:t + 1], LA[:, t, :], X_AXIS, ALU.max))
                        step(nc.vector.tensor_scalar(has[:], has[:], 0.5, None, ALU.is_ge))
                        nc.vector.tensor_scalar(low[:, 0, :], LA[:, 0, :], 2.0 ** -60, None, ALU.max).then_inc(least, 1)
                        for t in range(TILES):
                            if t + 1 < TILES:
                                nc.vector.tensor_scalar(low[:, (t + 1) % 2, :], LA[:, t + 1, :], 2.0 ** -60, None,
                                                        ALU.max).then_inc(least, 1)
                            dve.wait_ge(logs, t + 1)
                            step(nc.vector.tensor_scalar(LA[:, t, :], lg[:, t % 2, :], 1.0, 2.5e28, ALU.add, ALU.mult))
                            step(nc.vector.tensor_tensor(LA[:, t, :], LA[:, t, :], lg[:, t % 2, :], ALU.min))

                    @block.scalar
                    def _(act):
                        for t in range(TILES):
                            act.wait_ge(least, t + 1)
                            if t >= 2:
                                act.wait_ge(done, TILES + 1 + 2 * (t - 1))
                            nc.scalar.activation(lg[:, t % 2, :], low[:, t % 2, :], ACT.Ln).then_inc(logs, 1)

        def attend(KT, V, LA, has, A):
            with ExitStack() as st:
                sb, pb = tile_in(st), bank_in(st)
                staged = sems_in(st)("tile_staged0", "tile_staged1")
                scored, masked, shifted, probs_ready, turned, copied, valued, inverse, normed, tick = sems_in(st)(
                    "scored", "masked", "shifted", "probs_ready", "probs_turned", "turned_copied",
                    "head_valued", "inverse_steps", "tile_normed", "tick")
                QF = sb("QF", [128, HEADS, P])
                QS = [sb(f"QS{par}", [128, 2, HEADS, 128], F32R) for par in range(2)]
                q_loaded, upper_ready, tiles_scored = sems_in(st)("q_loaded", "q_upper_ready", "tiles_scored")
                q_split = sems_in(st)("q_split0", "q_split1")
                logs = [sb(f"logs{par}", [P, NODES]) for par in range(2)]
                S = sb("S", [P, 2, NODES])
                PT = sb("PT", [P, 2, TILES, P])
                mx, z, rz = sb("mx", [P, 2, HEADS]), sb("z", [P, 2, HEADS]), sb("rz", [P, HEADS])
                score_ps, turn_ps, out_ps = pb("score_ps", [128, 1536]), pb("turn_ps", [128, 1536]), pb("out_ps", [128, 2, 512])
                HALF = 4

                def pair(r, step, last):
                    for par in range(2):
                        for h in range(HEADS):
                            after = 2 * HEADS - 1 - (HEADS * par + h) if last else 2
                            step(r, par, h, after)

                with nc.Block() as block:
                    @block.sync
                    def _(sp):
                        def stage(i, par):
                            sp.wait_ge(upper_ready, 2 * i + 1)
                            sp.sem_inc(tick, 1)
                            for half in range(2):
                                sp.dma_start(QF[DK * half:DK * (half + 1)], q_dram[:, :, bass.ds(i * P, P)]).then_inc(q_loaded, 16)
                            sp.dma_start(logs[par][:], LA[:, bass.ds(i, 1), :].rearrange("p a n -> p (a n)")
                                         ).then_inc(staged[par], 16)

                        sp.sem_inc(upper_ready, 1)
                        for par in range(2):
                            stage(par, par)
                        with sp.Fori(0, TILES // 2 - 1) as r:
                            for par in range(2):
                                sp.wait_ge(masked, HEADS * (2 * r + par + 1))
                                sp.sem_inc(tick, 1)
                                stage(2 * r + 2 + par, par)

                    @block.gpsimd
                    def _(pool):
                        pool.sem_inc(tiles_scored, 2)
                        with pool.Fori(0, TILES // 2) as r:
                            for par in range(2):
                                i = 2 * r + par
                                pool.wait_ge(q_loaded, 32 * (i + 1))
                                pool.wait_ge(tiles_scored, i + 1)
                                pool.sem_inc(tick, 1)
                                nc.gpsimd.tensor_copy(QS[par][:, 0, :, 0:P], QF[:]).then_inc(upper_ready, 1)
                                pool.wait_ge(upper_ready, 2 * (i + 1))
                                nc.gpsimd.tensor_tensor(QS[par][:, 1, :, 0:P], QF[:], QS[par][:, 0, :, 0:P].bitcast(F32),
                                                        ALU.subtract).then_inc(upper_ready, 1)
                                pool.wait_ge(upper_ready, 2 * (i + 1) + 1)
                                pool.sem_inc(q_split[par], 1)

                    @block.tensor
                    def _(pe):
                        def scores(par, h, pairs):
                            if h == 0:
                                pe.wait_ge(q_split[par], pairs)
                            for c0, cn in CHUNKS:
                                for part in range(2):
                                    last = nc.tensor.matmul(score_ps[:P, c0:c0 + cn], QS[par][:, part, h, 0:P],
                                                            KT[:, h, c0:c0 + cn], start=part == 0, stop=part == 1)
                            last.then_inc(scored, 1)
                            if h == HEADS - 1:
                                pe.wait_ge(scored, HEADS * (2 * pairs - 1 + par))
                                pe.sem_inc(tiles_scored, 1)

                        def turn(h):
                            for s in range(TILES):
                                last = nc.tensor.transpose(turn_ps[:P, 128 * s:128 * s + P],
                                                           S[:, h % 2, P * s:P * (s + 1)], ident[:P, :P])
                                if s in (HALF - 1, TILES - 1):
                                    last.then_inc(turned, 1)

                        def step(r, par, h, after):
                            n = 2 * HEADS * r + HEADS * par + h
                            if after >= 2:
                                pe.wait_ge(masked, n + 2)
                                ahead = (HEADS * par + h + 2) // HEADS
                                scores(ahead % 2, (h + 2) % HEADS, r + 1 + ahead // 2)
                            pe.wait_ge(copied, 2 * (n + 1))
                            if after >= 1:
                                pe.wait_ge(probs_ready, n + 2)
                                turn((h + 1) % HEADS)
                            if h == 0:
                                pe.wait_ge(normed, 2 * r + par + 1)
                            for s in range(TILES):
                                last = nc.tensor.matmul(out_ps[:P, par, DK * h:DK * (h + 1)], PT[:, h % 2, s, :],
                                                        V[:, s, DK * h:DK * (h + 1)], start=s == 0, stop=s == TILES - 1)
                            last.then_inc(valued, 1)

                        pe.sem_inc(normed, 2)
                        pe.sem_inc(valued, 1)
                        scores(0, 0, 1)
                        pe.wait_ge(masked, 1)
                        scores(0, 1, 1)
                        pe.wait_ge(probs_ready, 1)
                        turn(0)
                        with pe.Fori(0, TILES // 2 - 1) as r:
                            pair(r, step, False)
                        pair(TILES // 2 - 1, step, True)

                    @block.vector
                    def _(dve):
                        def mask(n, par, h, pairs):
                            if h == 0:
                                dve.wait_ge(staged[par], 16 * pairs)
                            dve.wait_ge(scored, n + 1)
                            dve.sem_inc(tick, 1)
                            nc.vector.tensor_tensor_reduce(
                                out=S[:, h % 2, :], in0=score_ps[:P, 0:NODES], in1=logs[par][:],
                                scale=1.0, scalar=-3e38, op0=ALU.add, op1=ALU.max,
                                accum_out=mx[:, par, h:h + 1]).then_inc(masked, 1)
                            dve.wait_ge(masked, n + 1)
                            nc.vector.tensor_scalar(mx[:, par, h:h + 1], mx[:, par, h:h + 1], -1.0, None,
                                                    ALU.mult).then_inc(shifted, 1)

                        def copy(n, h):
                            dve.wait_ge(turned, 2 * n + 1)
                            nc.vector.tensor_copy(PT[:, h % 2, 0:HALF, :],
                                                  turn_ps[:P, 0:HALF * 128].rearrange("p (s c) -> p s c", c=128)[:, :, 0:P]
                                                  ).then_inc(copied, 1)

                        def step(r, par, h, after):
                            i = 2 * r + par
                            n = HEADS * i + h
                            if after >= 2:
                                dve.wait_ge(turned, 2 * (n + 1))
                                ahead = (HEADS * par + h + 2) // HEADS
                                mask(n + 2, ahead % 2, (h + 2) % HEADS, r + 1 + ahead // 2)
                            if after >= 1:
                                dve.wait_ge(valued, n + 1)
                                copy(n + 1, h + 1)
                            if h == HEADS - 1:
                                dve.wait_ge(probs_ready, n + 1)
                                nc.vector.reciprocal(rz[:], z[:, par, :]).then_inc(inverse, 1)
                                dve.wait_ge(inverse, 2 * i + 1)
                                nc.vector.tensor_scalar(rz[:], rz[:], has[:, bass.ds(i, 1)], None, ALU.mult).then_inc(inverse, 1)
                                dve.wait_ge(inverse, 2 * i + 2)
                                dve.wait_ge(valued, n + 2)
                                nc.vector.tensor_tensor(
                                    A[:, bass.ds(i, 1), :].rearrange("p a (h c) -> p (a h) c", c=DK),
                                    out_ps[:P, par, :].rearrange("p (h c) -> p h c", c=DK),
                                    rz[:].unsqueeze(2).to_broadcast([P, HEADS, DK]), ALU.mult).then_inc(normed, 1)

                        mask(0, 0, 0, 1)
                        mask(1, 0, 1, 1)
                        copy(0, 0)
                        with dve.Fori(0, TILES // 2 - 1) as r:
                            pair(r, step, False)
                        pair(TILES // 2 - 1, step, True)

                    @block.scalar
                    def _(act):
                        def exp(n, par, h):
                            act.wait_ge(shifted, n + 1)
                            nc.scalar.activation(S[:, h % 2, :], S[:, h % 2, :], ACT.Exp, bias=mx[:, par, h:h + 1],
                                                 accum_out=z[:, par, h:h + 1]).then_inc(probs_ready, 1)

                        def copy(n, h):
                            act.wait_ge(turned, 2 * (n + 1))
                            nc.scalar.activation(PT[:, h % 2, HALF:TILES, :],
                                                 turn_ps[:P, HALF * 128:TILES * 128].rearrange("p (s c) -> p s c", c=128)[:, :, 0:P],
                                                 ACT.Copy).then_inc(copied, 1)

                        def step(r, par, h, after):
                            n = 2 * HEADS * r + HEADS * par + h
                            if after >= 1:
                                act.wait_ge(valued, n + 1)
                                copy(n + 1, h + 1)
                            if after >= 2:
                                ahead = (HEADS * par + h + 2) // HEADS
                                exp(n + 2, ahead % 2, (h + 2) % HEADS)

                        exp(0, 0, 0)
                        exp(1, 0, 1)
                        copy(0, 0)
                        with act.Fori(0, TILES // 2 - 1) as r:
                            pair(r, step, False)
                        pair(TILES // 2 - 1, step, True)

        def node_major_product(srcT, weights, k_chunks, dst, bias=None, add=None, pool_work=None):
            with ExitStack() as st:
                sb, pb = tile_in(st), bank_in(st)
                loaded, done, moved = sems_in(st)("w_loaded", "product_done", "product_moved")
                W = sb("Wnm", [128, k_chunks, DIM])
                ps = pb("ps", [128, 4, 512])
                biasB = sb("biasB", [P, DIM]) if bias is not None else None
                with nc.Block() as block:
                    if pool_work is not None:
                        block.gpsimd(pool_work)

                    @block.sync
                    def _(sp):
                        sp.dma_start(W[:], weights.rearrange("(k p) n -> p k n", p=128)).then_inc(loaded, 16)
                        if bias is not None:
                            sp.dma_start(biasB[:], row(bias).broadcast_to([P, DIM])).then_inc(loaded, 16)

                    @block.tensor
                    def _(pe):
                        pe.wait_ge(loaded, 16 if bias is None else 32)
                        for t in range(TILES):
                            if t >= 4:
                                pe.wait_ge(moved, (t - 3) * (1 if bias is None else 2))
                            for k in range(k_chunks):
                                last = nc.tensor.matmul(ps[:P, t % 4, :], srcT[:, k, P * t:P * (t + 1)], W[:, k, :],
                                                        start=k == 0, stop=k == k_chunks - 1)
                            last.then_inc(done, 1)

                    @block.vector
                    def _(dve):
                        if bias is not None:
                            dve.wait_ge(loaded, 32)
                        n = 0
                        for t in range(TILES):
                            dve.wait_ge(done, t + 1)
                            nc.vector.tensor_tensor(dst[:, t, :], ps[:P, t % 4, :], add[:, t, :], ALU.add).then_inc(moved, 1)
                            n += 1
                            if bias is not None:
                                dve.wait_ge(moved, n)
                                nc.vector.tensor_tensor(dst[:, t, :], dst[:, t, :], biasB[:], ALU.add).then_inc(moved, 1)
                                n += 1

        def feature_major_layer(srcT, weights, bias, dstT, m_chunks, function, sync_work=None, pool_work=None):
            with ExitStack() as st:
                sb, pb = tile_in(st), bank_in(st)
                loaded, turned, bias_ready, done, moved = sems_in(st)(
                    "w_loaded", "bias_turned", "bias_ready", "product_done", "product_moved")
                W = sb("Wfm", [128, KC, m_chunks * 128])
                braw, bT = sb("braw", [m_chunks, 128]), sb("bT", [128, m_chunks])
                ps = pb("ps", [128, 4, 512])
                jobs = [(m, c0, cn) for m in range(m_chunks) for c0, cn in CHUNKS]
                with nc.Block() as block:
                    @block.sync
                    def _(sp):
                        sp.dma_start(W[:], weights.rearrange("(k p) n -> p k n", p=128)).then_inc(loaded, 16)
                        sp.dma_start(braw[:], bias.rearrange("(m p) -> m p", p=128)).then_inc(loaded, 16)
                        if sync_work is not None:
                            sync_work(sp)

                    if pool_work is not None:
                        block.gpsimd(pool_work)

                    @block.tensor
                    def _(pe):
                        pe.wait_ge(loaded, 32)
                        nc.tensor.transpose(ps[:, 3, 0:m_chunks], braw[:], ident[:m_chunks, :m_chunks]).then_inc(turned, 1)
                        for n, (m, c0, cn) in enumerate(jobs):
                            if n == 3:
                                pe.wait_ge(bias_ready, 1)
                            if n >= 4:
                                pe.wait_ge(moved, n - 3)
                            for k in range(KC):
                                last = nc.tensor.matmul(ps[:, n % 4, 0:cn], W[:, k, 128 * m:128 * (m + 1)],
                                                        srcT[:, k, c0:c0 + cn], start=k == 0, stop=k == KC - 1)
                            last.then_inc(done, 1)

                    @block.scalar
                    def _(act):
                        act.wait_ge(turned, 1)
                        nc.scalar.activation(bT[:], ps[:, 3, 0:m_chunks], ACT.Copy).then_inc(bias_ready, 1)
                        act.wait_ge(bias_ready, 1)
                        for n, (m, c0, cn) in enumerate(jobs):
                            act.wait_ge(done, n + 1)
                            nc.scalar.activation(dstT[:, m, c0:c0 + cn], ps[:, n % 4, 0:cn], function,
                                                 bias=bT[:, m:m + 1]).then_inc(moved, 1)

        def gate(srcT, weights, weights_are_rows, bias, probs, best, bestI):
            sets = len(weights)
            per_tile, n_rows = sets * EXPERTS, TILES * sets
            wide = [P, n_rows, EXPERTS]
            with ExitStack() as st:
                sb, pb = tile_in(st), bank_in(st)
                loaded, turned, w_ready, done, logits_in, exped, steps = sems_in(st)(
                    "w_loaded", "w_turned", "w_ready", "logits_done", "logits_in", "exped", "gate_steps")
                W = sb("Wg", [128, KC, per_tile])
                Wraw = sb("Wraw", [EXPERTS, DIM]) if weights_are_rows else None
                biasB = sb("biasB", [P, per_tile])
                mx, zs = sb("mx", [P, n_rows]), sb("zs", [P, n_rows])
                lg = sb("lg", wide)
                ps = pb("ps", [128, 2, 512])
                with nc.Block() as block:
                    @block.sync
                    def _(sp):
                        for s in range(sets):
                            own = slice(EXPERTS * s, EXPERTS * (s + 1))
                            if weights_are_rows:
                                sp.dma_start(Wraw[:], weights[s]).then_inc(loaded, 16)
                            else:
                                sp.dma_start(W[:, :, own], weights[s].rearrange("(k p) n -> p k n", p=128)).then_inc(loaded, 16)
                            sp.dma_start(biasB[:, own], row(bias[s]).broadcast_to([P, EXPERTS])).then_inc(loaded, 16)

                    @block.tensor
                    def _(pe):
                        pe.wait_ge(loaded, 32 * sets)
                        if weights_are_rows:
                            for k in range(KC):
                                last = nc.tensor.transpose(ps[:, 1, EXPERTS * k:EXPERTS * (k + 1)],
                                                           Wraw[:, 128 * k:128 * (k + 1)], ident[:EXPERTS, :EXPERTS])
                            last.then_inc(turned, 1)
                            pe.wait_ge(w_ready, 1)
                        for t in range(TILES):
                            for k in range(KC):
                                last = nc.tensor.matmul(ps[:P, 0, per_tile * t:per_tile * (t + 1)], srcT[:, k, P * t:P * (t + 1)],
                                                        W[:, k, :], start=k == 0, stop=k == KC - 1)
                        last.then_inc(done, 1)

                    @block.scalar
                    def _(act):
                        if weights_are_rows:
                            act.wait_ge(turned, 1)
                            nc.scalar.activation(W[:], ps[:, 1, 0:KC * EXPERTS].rearrange("p (k e) -> p k e", k=KC),
                                                 ACT.Copy).then_inc(w_ready, 1)
                        act.wait_ge(logits_in, 1)
                        nc.scalar.activation(probs[:], lg[:], ACT.Exp).then_inc(exped, 1)

                    @block.vector
                    def _(dve):
                        step = Chain(dve, steps)
                        dve.wait_ge(loaded, 32 * sets)
                        dve.wait_ge(done, 1)
                        step(nc.vector.tensor_tensor(lg[:].rearrange("p (t s) e -> p t (s e)", s=sets),
                                                     ps[:P, 0, 0:TILES * per_tile].rearrange("p (t e) -> p t e", t=TILES),
                                                     biasB[:].unsqueeze(1).to_broadcast([P, TILES, per_tile]), ALU.add))
                        step(nc.vector.tensor_reduce(mx[:], lg[:], X_AXIS, ALU.max))
                        nc.vector.tensor_tensor(lg[:], lg[:], mx[:].unsqueeze(2).to_broadcast(wide),
                                                ALU.subtract).then_inc(logits_in, 1)
                        dve.wait_ge(exped, 1)
                        step(nc.vector.tensor_reduce(zs[:], probs[:], X_AXIS, ALU.add))
                        step(nc.vector.reciprocal(zs[:], zs[:]))
                        step(nc.vector.tensor_tensor(probs[:], probs[:], zs[:].unsqueeze(2).to_broadcast(wide), ALU.mult))
                        for n in range(n_rows):
                            best_of = nc.vector.max(best[:, n, :], probs[:, n, :])
                        step(best_of)
                        for n in range(n_rows):
                            index_of = nc.vector.max_index(bestI[:, n, :], best[:, n, :], probs[:, n, :])
                        step(index_of)

        def place_choices(best, bestI, weight, slot_in, slot_out, sync_work):
            SPLIT = 32
            with ExitStack() as st:
                sb, pb = tile_in(st), bank_in(st)
                steps, numbered, w8_ready, turned, first_out, rows_in, compared, ranked = sems_in(st)(
                    "place_steps", "nodes_numbered", "w8_ready", "turned", "first_out", "rows_in", "compared", "ranked")
                zeroed, upper_in, lower_in = sems_in(st)("zeroed", "upper_in", "lower_in")
                idxF = sb("idxF", [P, TILES, 2])
                oh = sb("oh", [P, 2, TILES, EXPERTS])
                w8, tmp, routed = (sb("w8", [P, TILES, EXPERTS]), sb("tmp", [P, TILES, EXPERTS]),
                                   sb("routed", [P, TILES, EXPERTS]))
                w8T = sb("w8T", [SPLIT + EXPERTS, NODES], F32R)
                ohT = sb("ohT", [SPLIT + EXPERTS, 2, NODES], F32R)
                junk, same = sb("junk", [P, NODES]), sb("same", [P, P])
                own = sb("own", [P, TILES, 2])
                parts = sb("parts", [P, TILES, 2, 3])
                rank, keep = sb("rank", [P, TILES, 2]), sb("keep", [P, TILES, 2])
                slotF, node, nodeF = (sb("slotF", [P, TILES, 2]), sb("node", [P, TILES, 2], I32),
                                      sb("nodeF", [P, TILES, 2]))
                ps = pb("ps", [128, 2, 2048])
                wide = [P, TILES, EXPERTS]
                with nc.Block() as block:
                    block.sync(sync_work)

                    @block.gpsimd
                    def _(pool):
                        nc.gpsimd.iota(node[:], pattern=[[P, TILES], [NODES, 2]], base=EXPERTS * ROWS0,
                                       channel_multiplier=1).then_inc(numbered, 1)

                    @block.vector
                    def _(dve):
                        step = Chain(dve, steps)
                        step(nc.vector.memset(parts[:], 0.0))
                        nc.vector.tensor_copy(w8T[:], zeros[:SPLIT + EXPERTS, 0:1].to_broadcast([SPLIT + EXPERTS, NODES]))
                        nc.vector.tensor_copy(ohT[:], zeros[:SPLIT + EXPERTS, 0:1].unsqueeze(2).to_broadcast([SPLIT + EXPERTS, 2, NODES])
                                              ).then_inc(zeroed, 1)
                        step(nc.vector.tensor_copy(idxF[:], bestI[:, :, 0:2]))
                        e8 = count[:P, 0:EXPERTS].unsqueeze(1).to_broadcast(wide)
                        for c in range(2):
                            step(nc.vector.tensor_tensor(oh[:, c], e8, idxF[:, :, c:c + 1].to_broadcast(wide), ALU.is_equal))
                        step(nc.vector.tensor_tensor(routed[:], oh[:, 0], oh[:, 1], ALU.add))
                        step(nc.vector.tensor_scalar(routed[:], routed[:], -1.0, None, ALU.add))
                        step(nc.vector.tensor_tensor(w8[:], oh[:, 0], best[:, :, 0:1].to_broadcast(wide), ALU.mult))
                        step(nc.vector.tensor_tensor(tmp[:], oh[:, 1], best[:, :, 1:2].to_broadcast(wide), ALU.mult))
                        step(nc.vector.tensor_tensor(w8[:], w8[:], tmp[:], ALU.add))
                        step(nc.vector.tensor_tensor(w8[:], w8[:], routed[:], ALU.add))
                        dve.sem_inc(w8_ready, 1)
                        dve.wait_ge(numbered, 1)
                        step(nc.vector.tensor_copy(nodeF[:], node[:]))
                        dve.wait_ge(upper_in, 1)
                        nc.vector.tensor_tensor(w8T[SPLIT:SPLIT + EXPERTS, :].rearrange("e (t n) -> e t n", n=P),
                                                ps[:EXPERTS, 0, 0:128 * TILES].rearrange("e (t n) -> e t n", n=128)[:, :, 0:P],
                                                w8T[0:EXPERTS, :].bitcast(F32).rearrange("e (t n) -> e t n", n=P), ALU.subtract
                                                ).then_inc(lower_in, 1)
                        for n in range(2 * TILES):
                            t, c = n // 2, n % 2
                            mine = own[:, t, c:c + 1]
                            dve.wait_ge(ranked, n + 1)
                            full = ps[:P, n % 2, 0:NODES]
                            step(nc.vector.tensor_tensor(same[:], full[:, P * t:P * (t + 1)], ident[:P, :P], ALU.mult))
                            step(nc.vector.tensor_reduce(mine, same[:], X_AXIS, ALU.add))
                            if t > 0:
                                step(nc.vector.tensor_scalar(junk[:, 0:P * t], full[:, 0:P * t], mine, None, ALU.is_ge, ALU.add,
                                                             accum_out=parts[:, t, c, 0:1]))
                            step(nc.vector.tensor_scalar(junk[:, 0:NODES - P * t], full[:, P * t:NODES], mine, None,
                                                         ALU.is_gt, ALU.add, accum_out=parts[:, t, c, 1:2]))
                            step(nc.vector.scalar_tensor_tensor(out=same[:], in0=full[:, P * t:P * (t + 1)], scalar=mine,
                                                                in1=earlier[:P, :P], op0=ALU.is_equal, op1=ALU.mult))
                            dve.sem_inc(compared, 1)
                            step(nc.vector.tensor_reduce(parts[:, t, c, 2:3], same[:], X_AXIS, ALU.add))
                        step(nc.vector.tensor_reduce(rank[:], parts[:], X_AXIS, ALU.add))
                        step(nc.vector.tensor_scalar(keep[:], rank[:], CAP0 - 0.5, None, ALU.is_lt))
                        step(nc.vector.scalar_tensor_tensor(out=slotF[:], in0=idxF[:], scalar=float(ROWS0), in1=rank[:],
                                                            op0=ALU.mult, op1=ALU.add))
                        step(nc.vector.tensor_tensor(slotF[:], slotF[:], keep[:], ALU.mult))
                        step(nc.vector.tensor_copy(slot_out[:], slotF[:]))
                        step(nc.vector.tensor_tensor(weight[:], best[:, :, 0:2], keep[:], ALU.mult))
                        step(nc.vector.tensor_scalar(keep[:], keep[:], -1.0, 1.0, ALU.mult, ALU.add))
                        step(nc.vector.tensor_tensor(keep[:], keep[:], nodeF[:], ALU.mult))
                        step(nc.vector.tensor_tensor(slot_in[:], slotF[:], keep[:], ALU.add))

                    @block.tensor
                    def _(pe):
                        pe.wait_ge(w8_ready, 1)
                        for t in range(TILES):
                            nc.tensor.transpose(ps[:EXPERTS, 0, 128 * t:128 * t + P], w8[:, t, :], ident[:P, :P])
                        for c in range(2):
                            if c == 1:
                                pe.wait_ge(first_out, 1)
                            for t in range(TILES):
                                last = nc.tensor.transpose(ps[:EXPERTS, 1, 128 * t:128 * t + P], oh[:, c, t, :], ident[:P, :P])
                            last.then_inc(turned, 1)
                        pe.wait_ge(rows_in, 1)
                        pe.wait_ge(lower_in, 1)
                        for n in range(2 * TILES):
                            t, c = n // 2, n % 2
                            if n >= 2:
                                pe.wait_ge(compared, n - 1)
                            for c0, cn in CHUNKS:
                                last = nc.tensor.matmul(ps[:P, n % 2, c0:c0 + cn], ohT[:, c, P * t:P * (t + 1)],
                                                        w8T[:, c0:c0 + cn], start=True, stop=True)
                            last.then_inc(ranked, 1)

                    @block.scalar
                    def _(act):
                        act.wait_ge(turned, 1)

                        def row_of_tiles(bank):
                            return ps[:EXPERTS, bank, 0:128 * TILES].rearrange("e (t n) -> e t n", n=128)[:, :, 0:P]

                        def by_tile(rows):
                            return rows.rearrange("e (t n) -> e t n", n=P)

                        act.wait_ge(zeroed, 1)
                        nc.scalar.activation(by_tile(w8T[0:EXPERTS, :]), row_of_tiles(0), ACT.Copy).then_inc(upper_in, 1)
                        nc.scalar.activation(by_tile(ohT[0:EXPERTS, 0, :]), row_of_tiles(1), ACT.Copy)
                        nc.scalar.activation(by_tile(ohT[SPLIT:SPLIT + EXPERTS, 0, :]), row_of_tiles(1), ACT.Copy).then_inc(first_out, 1)
                        act.wait_ge(turned, 2)
                        nc.scalar.activation(by_tile(ohT[0:EXPERTS, 1, :]), row_of_tiles(1), ACT.Copy)
                        nc.scalar.activation(by_tile(ohT[SPLIT:SPLIT + EXPERTS, 1, :]), row_of_tiles(1), ACT.Copy).then_inc(rows_in, 1)

        def fill_zeros(sp, target, zeroed):
            starts = range(0, target.shape[0], 128)
            for r in starts:
                m = min(128, target.shape[0] - r)
                sp.dma_start(target[r:r + m, :], zeros[:m, :]).then_inc(zeroed, 16)
            return 16 * len(starts)

        def row_scatter(stack, src, slots, choices, target):
            (sent,) = sems_in(stack)("rows_sent")

            def program(pool):
                for t in range(TILES):
                    for c in range(choices):
                        pool.indirect_dma_start(
                            out=target, out_offset=bass.IndirectOffsetOnAxis(ap=slots[:, t, c:c + 1], axis=0),
                            in_=src[:, t, :], in_offset=None).then_inc(sent, 16)
                pool.wait_ge(sent, 16 * TILES * choices)

            return program

        def scatter_rows(src, slots, choices, target):
            with ExitStack() as st:
                with nc.Block() as block:
                    block.gpsimd(row_scatter(st, src, slots, choices, target))

        def first_weights(stack):
            sb = tile_in(stack)
            W1, W2 = sb("W1_0", [128, KC, HID0]), sb("W2_0", [128, MC0, DIM])
            w1_loaded, w2_loaded = sems_in(stack)("w1_loaded0", "w2_loaded0")

            def load(sp):
                sp.dma_start(W1[:], I["L0_ffn_w1"][0].rearrange("(k p) n -> p k n", p=128)).then_inc(w1_loaded, 16)
                sp.dma_start(W2[:], I["L0_ffn_w2"][0].rearrange("(m p) n -> p m n", p=128)).then_inc(w2_loaded, 16)

            return (W1, W2, w1_loaded, w2_loaded), load

        def experts0(first):
            with ExitStack() as st:
                sb, pb = tile_in(st), bank_in(st)
                x_loaded = sems_in(st)("x_loaded0", "x_loaded1")
                w1_loaded = [first[2], *sems_in(st)("w1_loaded1")]
                w2_loaded = [first[3], *sems_in(st)("w2_loaded1")]
                stored = sems_in(st)("stored0", "stored1")
                (b_loaded, b_turned, b_ready, x_turned, x_moved, hid_done, hid_moved, y_done, y_moved, back_done,
                 back_moved, y_free, tick) = sems_in(st)(
                    "b_loaded", "b_turned", "b_ready", "x_turned", "x_moved", "hid_done", "hid_moved", "y_done",
                    "y_moved", "back_done", "back_moved", "y_free", "tick")
                W1 = [first[0], sb("W1_1", [128, KC, HID0])]
                W2 = [first[1], sb("W2_1", [128, MC0, DIM])]
                b1raw, b2raw = sb("b1raw", [EXPERTS * MC0, 128]), sb("b2raw", [EXPERTS * KC, 128])
                b1T, b2T = sb("b1T", [128, EXPERTS * MC0]), sb("b2T", [128, EXPERTS * KC])
                xe = [sb(f"xe{i}", [HALF0, 2, DIM]) for i in range(2)]
                ye = [sb(f"ye{i}", [HALF0, 2, DIM]) for i in range(2)]
                xT, yT = sb("xT", [128, KC, ROWS0]), sb("yT", [128, KC, ROWS0])
                hid = sb("hid", [128, MC0, ROWS0])
                hid_ps, y_ps, turn_ps = pb("hid_ps", [128, 4, 512]), pb("y_ps", [128, 2, 512]), pb("turn_ps", [128, 2, 512])
                with nc.Block() as block:
                    def load_rows(sp, e, b):
                        rows = xin0[bass.ds(e * ROWS0, ROWS0), :].rearrange("(c p) d -> p c d", p=HALF0)
                        sp.dma_start(xe[b][:], rows).then_inc(x_loaded[b], 16)

                    def load_first(sp, e, b):
                        sp.dma_start(W1[b][:], I["L0_ffn_w1"][bass.ds(e, 1)].rearrange("a (k p) n -> p (a k) n", p=128)
                                     ).then_inc(w1_loaded[b], 16)

                    def load_second(sp, e, b):
                        sp.dma_start(W2[b][:], I["L0_ffn_w2"][bass.ds(e, 1)].rearrange("a (m p) n -> p (a m) n", p=128)
                                     ).then_inc(w2_loaded[b], 16)

                    @block.sync
                    def _(sp):
                        sp.dma_start(b1raw[:], I["L0_ffn_b1"].rearrange("e (m p) -> (e m) p", p=128)).then_inc(b_loaded, 16)
                        sp.dma_start(b2raw[:], I["L0_ffn_b2"].rearrange("e (m p) -> (e m) p", p=128)).then_inc(b_loaded, 16)
                        for b in range(2):
                            load_rows(sp, b, b)
                        load_first(sp, 1, 1)
                        load_second(sp, 1, 1)
                        with sp.Fori(0, EXPERTS // 2 - 1) as r:
                            for b in range(2):
                                sp.wait_ge(hid_done, MC0 * (2 * r + b + 1))
                                sp.sem_inc(tick, 1)
                                load_rows(sp, 2 * r + 2 + b, b)
                                load_first(sp, 2 * r + 2 + b, b)
                                sp.wait_ge(y_done, KC * (2 * r + b + 1))
                                sp.sem_inc(tick, 1)
                                load_second(sp, 2 * r + 2 + b, b)

                    @block.gpsimd
                    def _(pool):
                        with pool.Fori(0, EXPERTS // 2) as r:
                            for b in range(2):
                                pool.wait_ge(back_moved, 2 * (2 * r + b + 1) + 2)
                                pool.sem_inc(tick, 1)
                                rows = yout0[bass.ds((2 * r + b) * ROWS0, ROWS0), :].rearrange("(c p) d -> p c d", p=HALF0)
                                pool.dma_start(rows, ye[b][:]).then_inc(stored[b], 16)
                                pool.wait_ge(stored[b], 16 * (r + 1))
                                pool.sem_inc(y_free, 1)

                    @block.tensor
                    def _(pe):
                        pe.wait_ge(b_loaded, 32)
                        nc.tensor.transpose(y_ps[:, 0, 0:EXPERTS * MC0], b1raw[:], ident[:])
                        nc.tensor.transpose(y_ps[:, 1, 0:EXPERTS * KC], b2raw[:], ident[:EXPERTS * KC, :EXPERTS * KC]
                                            ).then_inc(b_turned, 1)
                        pe.wait_ge(b_ready, 2)
                        pe.sem_inc(back_moved, 2)

                        def turn(r, b):
                            e = 2 * r + b
                            pe.wait_ge(x_loaded[b], 16 * (r + 1))
                            for c in range(2):
                                if not (isinstance(r, int) and e == 0):
                                    pe.wait_ge(back_moved, 2 * (e - 1) + c + 1)
                                for k in range(KC):
                                    last = nc.tensor.transpose(turn_ps[:, c, HALF0 * k:HALF0 * (k + 1)],
                                                               xe[b][:, c, 128 * k:128 * (k + 1)], ident[:HALF0, :HALF0])
                                last.then_inc(x_turned, 1)

                        def back(e, x_tiles):
                            pe.wait_ge(y_moved, KC * (e + 1))
                            pe.wait_ge(x_moved, x_tiles)
                            for c in range(2):
                                for k in range(KC):
                                    last = nc.tensor.transpose(turn_ps[:HALF0, c, 128 * k:128 * (k + 1)],
                                                               yT[:, k, HALF0 * c:HALF0 * (c + 1)], ident[:])
                                last.then_inc(back_done, 1)

                        def expert(r, b, is_first, is_last):
                            e = 2 * r + b
                            pe.wait_ge(w1_loaded[b], 16 * (r + 1))
                            pe.wait_ge(x_moved, 2 * (e + 1))
                            for m in range(MC0):
                                if m == 2 and not is_first:
                                    back(e - 1, 2 * (e + 1))
                                if m >= 4:
                                    pe.wait_ge(hid_moved, MC0 * e + m - 3)
                                for k in range(KC):
                                    last = nc.tensor.matmul(hid_ps[:, m % 4, 0:ROWS0], W1[b][:, k, 128 * m:128 * (m + 1)],
                                                            xT[:, k, :], start=k == 0, stop=k == KC - 1)
                                last.then_inc(hid_done, 1)
                            if not is_last:
                                turn(r + b, 1 - b)
                            pe.wait_ge(w2_loaded[b], 16 * (r + 1))
                            for d in range(KC):
                                if d >= 2:
                                    pe.wait_ge(y_moved, KC * e + d - 1)
                                for m in range(MC0):
                                    if d == 0:
                                        pe.wait_ge(hid_moved, MC0 * e + m + 1)
                                    last = nc.tensor.matmul(y_ps[:, d % 2, 0:ROWS0], W2[b][:, m, 128 * d:128 * (d + 1)],
                                                            hid[:, m, :], start=m == 0, stop=m == MC0 - 1)
                                last.then_inc(y_done, 1)

                        PAIRS = EXPERTS // 2
                        turn(0, 0)
                        for b in range(2):
                            expert(0, b, b == 0, False)
                        with pe.Fori(1, PAIRS - 1) as r:
                            for b in range(2):
                                expert(r, b, False, False)
                        for b in range(2):
                            expert(PAIRS - 1, b, False, b == 1)
                        back(EXPERTS - 1, 2 * EXPERTS)

                    @block.scalar
                    def _(act):
                        act.wait_ge(b_turned, 1)
                        nc.scalar.activation(b1T[:], y_ps[:, 0, 0:EXPERTS * MC0], ACT.Copy).then_inc(b_ready, 1)
                        nc.scalar.activation(b2T[:], y_ps[:, 1, 0:EXPERTS * KC], ACT.Copy).then_inc(b_ready, 1)
                        act.wait_ge(b_ready, 2)

                        def rows_in(e):
                            for c in range(2):
                                act.wait_ge(x_turned, 2 * e + c + 1)
                                nc.scalar.activation(xT[:, :, HALF0 * c:HALF0 * (c + 1)],
                                                     turn_ps[:, c, 0:KC * HALF0].rearrange("p (k n) -> p k n", k=KC),
                                                     ACT.Copy).then_inc(x_moved, 1)

                        def hidden(e):
                            for m in range(MC0):
                                act.wait_ge(hid_done, MC0 * e + m + 1)
                                nc.scalar.activation(hid[:, m, :], hid_ps[:, m % 4, 0:ROWS0], ACT.Gelu,
                                                     bias=b1T[:, bass.ds(e * MC0 + m, 1)]).then_inc(hid_moved, 1)

                        rows_in(0)
                        with act.Fori(0, EXPERTS - 1) as e:
                            hidden(e)
                            rows_in(e + 1)
                        hidden(EXPERTS - 1)

                    @block.vector
                    def _(dve):
                        dve.sem_inc(y_free, 2)
                        dve.wait_ge(b_ready, 2)
                        with dve.Fori(0, EXPERTS // 2) as r:
                            for b in range(2):
                                e = 2 * r + b
                                for d in range(KC):
                                    dve.wait_ge(y_done, KC * e + d + 1)
                                    nc.vector.tensor_scalar(yT[:, d, :], y_ps[:, d % 2, 0:ROWS0], b2T[:, bass.ds(e * KC + d, 1)],
                                                            None, ALU.add).then_inc(y_moved, 1)
                                dve.wait_ge(y_free, e + 1)
                                for c in range(2):
                                    dve.wait_ge(back_done, 2 * e + c + 1)
                                    nc.vector.tensor_copy(ye[b][:, c, :], turn_ps[:HALF0, c, :]).then_inc(back_moved, 1)

        def combine(picks, result=None):
            with ExitStack() as st:
                sb = tile_in(st)
                RING = 4
                arrived = sems_in(st)(*[f"arrived{i}" for i in range(RING)])
                added, stored = sems_in(st)("added", "result_stored")
                got = sb("got", [P, RING, DIM])
                jobs = [(t, *pick) for t in range(TILES) for pick in picks]
                with nc.Block() as block:
                    if result is not None:
                        @block.sync
                        def _(sp):
                            for t in range(TILES):
                                sp.wait_ge(added, len(picks) * (t + 1))
                                sp.dma_start(result[P * t:P * (t + 1), :], X[:, t, :]).then_inc(stored, 16)
                            sp.wait_ge(stored, 16 * TILES)

                    @block.gpsimd
                    def _(pool):
                        for n, (t, source, slots, _) in enumerate(jobs):
                            if n >= RING:
                                pool.wait_ge(added, n - RING + 1)
                            pool.indirect_dma_start(
                                out=got[:, n % RING, :], out_offset=None, in_=source,
                                in_offset=bass.IndirectOffsetOnAxis(ap=slots(t), axis=0)).then_inc(arrived[n % RING], 16)

                    @block.vector
                    def _(dve):
                        for n, (t, _, _, weight) in enumerate(jobs):
                            dve.wait_ge(arrived[n % RING], 16 * (n // RING + 1))
                            if n >= 1:
                                dve.wait_ge(added, n)
                            nc.vector.scalar_tensor_tensor(out=X[:, t, :], in0=got[:, n % RING, :], scalar=weight(t),
                                                           in1=X[:, t, :], op0=ALU.mult, op1=ALU.add).then_inc(added, 1)

        def mix_up(xT):
            with ExitStack() as st:
                sb, pb = tile_in(st), bank_in(st)
                loaded, done, moved, stored = sems_in(st)("w_loaded", "mixed", "mixed_moved", "mixed_stored")
                W = sb("Wup", [128, 2, MUL])
                rows = sb("rows", [P, TILES, DIM])
                ps = pb("ps", [128, 4, 512])
                with nc.Block() as block:
                    @block.sync
                    def _(sp):
                        sp.dma_start(W[:, 0, :], I["L1_gnn_W_up0"]).then_inc(loaded, 16)
                        sp.dma_start(W[:, 1, :], I["L1_gnn_W_up1"]).then_inc(loaded, 16)
                        for t in range(TILES):
                            sp.wait_ge(moved, t + 1)
                            sp.dma_start(up_dram[P * t:P * (t + 1), :], rows[:, t, :]).then_inc(stored, 16)
                        sp.wait_ge(stored, 16 * TILES)

                    @block.tensor
                    def _(pe):
                        pe.wait_ge(loaded, 32)
                        for t in range(TILES):
                            if t >= 4:
                                pe.wait_ge(moved, t - 3)
                            for q in range(4):
                                last = nc.tensor.matmul(ps[:P, t % 4, MUL * q:MUL * (q + 1)], xT[:, q, P * t:P * (t + 1)],
                                                        W[:, min(q, 1), :], start=True, stop=True)
                            last.then_inc(done, 1)

                    @block.scalar
                    def _(act):
                        for t in range(TILES):
                            act.wait_ge(done, t + 1)
                            nc.scalar.activation(rows[:, t, :], ps[:P, t % 4, :], ACT.Copy,
                                                 scale=1.0 / math.sqrt(MUL)).then_inc(moved, 1)

        def messages(MSG):
            HID = 64
            with ExitStack() as st:
                sb, pb = tile_in(st), bank_in(st)
                RECS = sb("RECS", [128, GROUPS + 2, EPP, REC])
                recs_loaded, upper_ready, h3_split = sems_in(st)("recs_loaded", "upper_ready", "hidden_split")
                arrived = sems_in(st)(*[f"rows_arrived{t}" for t in range(EPP)])
                (zeroed, w_loaded, w_scaled, cleared, feats, feats_turned, feats_in, layer_done, layer_out, weighed, products,
                 lanes_ready, one_hots, dots, summed, taken, idx_ready, staged, tick) = sems_in(st)(
                    "zeroed", "mlp_loaded", "mlp_scaled", "sums_cleared", "feats_staged", "feats_turned", "feats_in",
                    "layer_done", "layer_out", "edge_weights_done", "products_ready", "lanes_ready", "one_hots_ready", "dot_steps", "tile_summed",
                    "sums_taken", "indices_ready", "recs_staged", "tick")
                W1b, W2b, W3b = sb("W1b", [16, 128]), sb("W2b", [128, 128]), sb("W3b", [128, 128])
                W4 = sb("W4", [128, DIM])
                W4_parts = sb("W4_parts", [128, 2, DIM], F32R)
                h3_parts = sb("h3_parts", [128, DIM], F32R)
                srcI = sb("srcI", [128, GROUPS, EPP], I32)
                idx = sb("idx", [128, 2, EPP], I32)
                rows = sb("rows", [128, EPP, DIM])
                lane = sb("lane", [128, P])
                rg = sb("rg", [128, 2, EPP, 8])
                fs = sb("fs", [128, 2, 16])
                fT, h1, h2, h3 = sb("fT", [16, 256]), sb("h1", [128, 256]), sb("h2", [128, 256]), sb("h3", [128, 512])
                prod = sb("prod", [128, 2, 6, MUL])
                dot = sb("dot", [128, 2, 3, MUL])
                oh = sb("oh", [128, 2, 5, P])
                acc, w_ps, mlp_ps = pb("acc", [128, 2, 2, 512]), pb("w_ps", [128, 2, 512]), pb("mlp_ps", [128, 2, 512])

                with nc.Block() as block:
                    @block.sync
                    def _(sp):
                        sp.dma_start(RECS[:, 0:GROUPS], rec_dram.rearrange("(g p t) w -> p g t w", p=128, t=EPP)).then_inc(recs_loaded, 16)
                        sp.wait_ge(zeroed, 1)
                        for w, name, k in ((W1b, "L1_gnn_W_mlp1", 8), (W2b, "L1_gnn_W_mlp2", HID)):
                            for half in range(2):
                                sp.dma_start(w[k * half:k * (half + 1), HID * half:HID * (half + 1)], I[name]).then_inc(w_loaded, 16)
                        for half in range(4):
                            rows, cols = HID * (half // 2), HID * (half % 2)
                            sp.dma_start(W3b[rows:rows + HID, cols:cols + HID], I["L1_gnn_W_mlp3"]).then_inc(w_loaded, 16)
                        for half in range(2):
                            sp.dma_start(W4[HID * half:HID * (half + 1), :], I["L1_gnn_W_mlp4"]).then_inc(w_loaded, 16)

                    @block.gpsimd
                    def _(pool):
                        nc.gpsimd.memset(W1b[:], 0.0)
                        nc.gpsimd.memset(W2b[:], 0.0)
                        nc.gpsimd.iota(lane[:], pattern=[[1, P]], base=0, channel_multiplier=0,
                                       allow_small_or_imprecise_dtypes=True).then_inc(zeroed, 1)
                        pool.sem_inc(products, EPP)
                        pool.wait_ge(idx_ready, 1)

                        with pool.Fori(0, GROUPS // 2) as r:
                            for par in range(2):
                                g = 2 * r + par
                                nc.gpsimd.tensor_copy(idx[:, par, :], srcI[:, bass.ds(g, 1), :].rearrange("p a t -> p (a t)")
                                                      ).then_inc(idx_ready, 1)
                                pool.wait_ge(idx_ready, g + 2)
                                pool.sem_inc(tick, 1)
                                for t in range(EPP):
                                    pool.wait_ge(products, EPP * g + t + 1)
                                    pool.sem_inc(tick, 1)
                                    pool.indirect_dma_start(
                                        out=rows[:, t, :], out_offset=None, in_=up_dram,
                                        in_offset=bass.IndirectOffsetOnAxis(ap=idx[:, par, t:t + 1], axis=0)
                                    ).then_inc(arrived[t], 16)

                    @block.tensor
                    def _(pe):
                        def turn_features(n):
                            pe.wait_ge(feats, n)
                            for tt in range(2):
                                last = nc.tensor.transpose(mlp_ps[:16, 0, 128 * tt:128 * (tt + 1)], fs[:, tt, :], ident[:])
                            last.then_inc(feats_turned, 1)

                        def weigh(t, group):
                            if t == 0:
                                pe.wait_ge(h3_split, group)
                            for part in range(2):
                                last = nc.tensor.matmul(w_ps[:, t % 2, :], h3_parts[:, 128 * t:128 * (t + 1)], W4_parts[:, part, :],
                                                        start=part == 0, stop=part == 1)
                            last.then_inc(weighed, 1)

                        def layer1(n):
                            pe.wait_ge(feats_in, n)
                            nc.tensor.matmul(mlp_ps[:, 1, 0:256], W1b[:], fT[:], start=True, stop=True).then_inc(layer_done, 1)

                        def layer2(done):
                            pe.wait_ge(layer_out, done)
                            nc.tensor.matmul(mlp_ps[:, 0, 0:256], W2b[:], h1[:], start=True, stop=True).then_inc(layer_done, 1)

                        def layer3(done):
                            pe.wait_ge(layer_out, done)
                            for half in range(2):
                                rows = slice(HID * half, HID * (half + 1))
                                last = nc.tensor.matmul(mlp_ps[:, half, 0:256], W3b[rows, :], h2[rows, :],
                                                        start=True, stop=True)
                            last.then_inc(layer_done, 1)

                        pe.wait_ge(w_loaded, 160)
                        pe.wait_ge(w_scaled, 4)
                        turn_features(1)
                        layer1(1)
                        layer2(1)
                        layer3(2)
                        weigh(0, 1)
                        turn_features(2)
                        with pe.Fori(0, GROUPS // 2) as r:
                            for par in range(2):
                                g = 2 * r + par
                                for t in range(EPP):
                                    if t == 0:
                                        layer1(g + 2)
                                    if t == 1:
                                        layer2(3 * (g + 1) + 1)
                                    pe.wait_ge(products, EPP * g + t + EPP)
                                    weigh((t + 1) % EPP, g + 2)
                                    if t == 2:
                                        layer3(3 * (g + 1) + 2)
                                    if t == EPP - 1:
                                        turn_features(g + 3)
                                    pe.wait_ge(one_hots, EPP * g + t + 1)
                                    pe.wait_ge(products, EPP * g + t + 1 + EPP)
                                    if t == 0:
                                        pe.wait_ge(taken, g + 1)
                                    nc.tensor.matmul(acc[:P, par, 0, :], oh[:, t % 2, 0, :], prod[:, t % 2, 0:4, :].rearrange("p b c -> p (b c)"),
                                                     start=t == 0, stop=t == EPP - 1)
                                    for i in range(4):
                                        last = nc.tensor.matmul(acc[:P, par, 1, MUL * i:MUL * (i + 1)], oh[:, t % 2, 1 + i, :],
                                                                prod[:, t % 2, 4 + i // 3, :], start=t == 0 and i == 0,
                                                                stop=t == EPP - 1 and i == 3, skip_group_check=True)
                                    last.then_inc(summed, 1)

                    @block.scalar
                    def _(act):
                        def features_in(n):
                            act.wait_ge(feats_turned, n)
                            nc.scalar.activation(fT[:], mlp_ps[:16, 0, 0:256], ACT.Copy).then_inc(feats_in, 1)

                        def layer(n, which):
                            act.wait_ge(layer_done, n)
                            target, source = ((h1[:], mlp_ps[:, 1, 0:256]), (h2[:], mlp_ps[:, 0, 0:256]),
                                              (h3[:].rearrange("p (a n) -> p a n", a=2), mlp_ps[:, :, 0:256]))[which]
                            nc.scalar.activation(target, source, ACT.Silu,
                                                 scale=(1 / math.sqrt(8), SILU_2MOM / math.sqrt(HID), SILU_2MOM / math.sqrt(HID))[which]
                                                 ).then_inc(layer_out, 1)

                        def upper_hidden(g):
                            act.wait_ge(layer_out, 3 * (g + 1))
                            nc.scalar.activation(h3_parts[:], h3[:], ACT.Copy).then_inc(upper_ready, 1)

                        features_in(1)
                        for which in range(3):
                            layer(which + 1, which)
                        upper_hidden(0)
                        features_in(2)
                        with act.Fori(0, GROUPS // 2) as r:
                            for par in range(2):
                                g = 2 * r + par
                                for t in range(EPP):
                                    act.wait_ge(lanes_ready, EPP * g + t + 1)
                                    for q in range(4):
                                        last = nc.scalar.activation(oh[:, t % 2, q, :], oh[:, t % 2, 4, :], ACT.Copy,
                                                                    scale=rg[:, par, t, 4 + q:5 + q])
                                    last.then_inc(one_hots, 1)
                                    if t < 3:
                                        layer(3 * (g + 1) + t + 1, t)
                                    if t == 2:
                                        upper_hidden(g + 1)
                                    if t == EPP - 1:
                                        features_in(g + 3)

                    @block.vector
                    def _(dve):
                        def stage_features(g):
                            nc.vector.tensor_copy(fs[:].rearrange("p t (b f) -> p b t f", b=2),
                                                  RECS[:, bass.ds(g, 1), :, 8:16].rearrange("p a (b t) f -> p (a b) t f", b=2)
                                                  ).then_inc(feats, 1)

                        def take_sums(block, g, par):
                            dve.wait_ge(summed, EPP * g + 2)
                            dve.wait_ge(taken, g + 1)
                            sums = MSG[:, bass.ds(block, 1), :].rearrange("p a n -> p (a n)")
                            nc.vector.tensor_tensor(sums, sums, acc[:P, par, :, :].rearrange("p a n -> p (a n)"), ALU.add
                                                    ).then_inc(taken, 1)

                        nc.vector.memset(RECS[:, GROUPS:GROUPS + 2, :, :], 0.0).then_inc(cleared, 1)
                        nc.vector.memset(MSG[:], 0.0).then_inc(cleared, 1)
                        dve.wait_ge(recs_loaded, 16)
                        nc.vector.tensor_copy(srcI[:], RECS[:, 0:GROUPS, :, 0]).then_inc(idx_ready, 1)
                        nc.vector.memset(acc[:, 1, :, :], 0.0).then_inc(taken, 1)
                        dve.wait_ge(w_loaded, 160)
                        nc.vector.tensor_scalar(W4[:], W4[:], SILU_2MOM / math.sqrt(HID), None, ALU.mult).then_inc(w_scaled, 1)
                        dve.wait_ge(w_scaled, 1)
                        nc.vector.tensor_scalar(W4[:, 384:512], W4[:, 384:512], 1 / math.sqrt(3), None, ALU.mult).then_inc(w_scaled, 1)
                        dve.wait_ge(w_scaled, 2)
                        nc.vector.tensor_copy(W4_parts[:, 0, :], W4[:]).then_inc(w_scaled, 1)
                        dve.wait_ge(w_scaled, 3)
                        nc.vector.tensor_tensor(W4_parts[:, 1, :], W4[:], W4_parts[:, 0, :].bitcast(F32), ALU.subtract
                                                ).then_inc(w_scaled, 1)
                        def split_hidden(g):
                            dve.wait_ge(upper_ready, g + 1)
                            nc.vector.tensor_tensor(h3_parts[HID:128, :], h3[HID:128, :], h3_parts[HID:128, :].bitcast(F32),
                                                    ALU.subtract).then_inc(h3_split, 1)

                        stage_features(0)
                        dve.wait_ge(feats_turned, 1)
                        stage_features(1)
                        split_hidden(0)
                        dve.wait_ge(cleared, 2)
                        dve.wait_ge(zeroed, 1)
                        dve.sem_inc(summed, 2)
                        with dve.Fori(0, GROUPS // 2) as r:
                            for par in range(2):
                                g = 2 * r + par
                                block_before = dve.value_load(blockI[0:1, bass.ds(g, 1)], min_val=0, max_val=TILES - 1)
                                nc.vector.tensor_copy(rg[:, par], RECS[:, bass.ds(g, 1), :, 0:8].rearrange("p a t w -> p (a t) w")
                                                      ).then_inc(staged, 1)
                                dve.wait_ge(feats_turned, g + 2)
                                stage_features(g + 2)
                                dve.wait_ge(staged, g + 1)
                                for t in range(EPP):
                                    dve.wait_ge(summed, EPP * g + t + 1)
                                    nc.vector.tensor_scalar(oh[:, t % 2, 4, :], lane[:], rg[:, par, t, 1:2], None,
                                                            ALU.is_equal).then_inc(lanes_ready, 1)
                                    dve.wait_ge(arrived[t], 16 * (g + 1))
                                    pr = prod[:, t % 2, :, :]
                                    w = w_ps[:, t % 2, :].rearrange("p (b c) -> p b c", c=MUL)
                                    s = rows[:, t, :].rearrange("p (b c) -> p b c", c=MUL)
                                    y = rg[:, par, t, 4:8]
                                    n = 3 * (EPP * g + t)
                                    nc.vector.tensor_scalar(dot[:, t % 2, 0, :], s[:, 1, :], y[:, 1:2], None, ALU.mult).then_inc(dots, 1)
                                    dve.wait_ge(dots, n + 1)
                                    nc.vector.scalar_tensor_tensor(out=dot[:, t % 2, 1, :], in0=s[:, 2, :], scalar=y[:, 2:3],
                                                                   in1=dot[:, t % 2, 0, :], op0=ALU.mult, op1=ALU.add).then_inc(dots, 1)
                                    dve.wait_ge(weighed, EPP * g + t + 1)
                                    nc.vector.tensor_tensor(pr[:, 0:5:4, :], w[:, 0:2, :], s[:, 0:1, :].to_broadcast([128, 2, MUL]), ALU.mult)
                                    dve.wait_ge(dots, n + 2)
                                    nc.vector.scalar_tensor_tensor(out=dot[:, t % 2, 2, :], in0=s[:, 3, :], scalar=y[:, 3:4],
                                                                   in1=dot[:, t % 2, 1, :], op0=ALU.mult, op1=ALU.add).then_inc(dots, 1)
                                    nc.vector.tensor_tensor(pr[:, 1:4, :], w[:, 2:3, :].to_broadcast([128, 3, MUL]), s[:, 1:4, :], ALU.mult)
                                    dve.wait_ge(dots, n + 3)
                                    nc.vector.tensor_tensor(pr[:, 5, :], w[:, 3, :], dot[:, t % 2, 2, :], ALU.mult).then_inc(products, 1)
                                    if t == EPP - 1:
                                        split_hidden(g + 1)
                                    if t == 1:
                                        take_sums(block_before, g, 1 - par)
                        take_sums(dve.value_load(blockI[0:1, GROUPS:GROUPS + 1], min_val=0, max_val=TILES - 1), GROUPS, 1)

        def mix_out(MSG):
            with ExitStack() as st:
                sb, pb = tile_in(st), bank_in(st)
                loaded, turned, moved, done, added = sems_in(st)("w_loaded", "turned", "turned_moved", "mixed", "added")
                W = sb("Wout", [128, 4, MUL])
                mT = sb("mT", [128, 2, 8, P])
                turn_ps, ps = pb("turn_ps", [128, 4, 512]), pb("ps", [128, 2, 512])
                with nc.Block() as block:
                    @block.sync
                    def _(sp):
                        sp.dma_start(W[:, 0:2, :], I["L1_gnn_W_out0"].rearrange("(k p) n -> p k n", p=128)).then_inc(loaded, 16)
                        sp.dma_start(W[:, 2:4, :], I["L1_gnn_W_out1"].rearrange("(k p) n -> p k n", p=128)).then_inc(loaded, 16)

                    pairs = [((0, 7), 0)] + [((4 + i, 1 + i), 2) for i in range(3)]

                    @block.tensor
                    def _(pe):
                        pe.wait_ge(loaded, 32)

                        def mix(t):
                            pe.wait_ge(moved, 2 * (t + 1))
                            if t >= 2:
                                pe.wait_ge(added, 2 * (t - 1))
                            for q, (chunks, w) in enumerate(pairs):
                                for n, c in enumerate(chunks):
                                    last = nc.tensor.matmul(ps[:P, t % 2, MUL * q:MUL * (q + 1)], mT[:, t % 2, c, :],
                                                            W[:, w + n, :], start=n == 0, stop=n == 1)
                            last.then_inc(done, 1)

                        for t in range(TILES):
                            if t >= 2:
                                pe.wait_ge(moved, 2 * (t - 1))
                            for half in range(2):
                                for c in range(4):
                                    last = nc.tensor.transpose(turn_ps[:, 2 * (t % 2) + half, P * c:P * (c + 1)],
                                                               MSG[:, t, 128 * (4 * half + c):128 * (4 * half + c + 1)], ident[:P, :P])
                                last.then_inc(turned, 1)
                            if t >= 1:
                                mix(t - 1)
                        mix(TILES - 1)

                    @block.scalar
                    def _(act):
                        for t in range(TILES):
                            if t >= 2:
                                act.wait_ge(done, t - 1)
                            for half in range(2):
                                act.wait_ge(turned, 2 * t + half + 1)
                                nc.scalar.activation(mT[:, t % 2, 4 * half:4 * half + 4, :],
                                                     turn_ps[:, 2 * (t % 2) + half, 0:4 * P].rearrange("p (c n) -> p c n", c=4),
                                                     ACT.Copy).then_inc(moved, 1)

                    @block.vector
                    def _(dve):
                        scale = 1 / (math.sqrt(2 * MUL) * 10.0)
                        for t in range(TILES):
                            dve.wait_ge(done, t + 1)
                            xs, xv = X[:, t, 0:MUL], X[:, t, MUL:DIM].rearrange("p (v m) -> p m v", m=3)
                            nc.vector.scalar_tensor_tensor(out=xs, in0=ps[:P, t % 2, 0:MUL], scalar=scale, in1=xs,
                                                           op0=ALU.mult, op1=ALU.add).then_inc(added, 1)
                            nc.vector.scalar_tensor_tensor(out=xv, in0=ps[:P, t % 2, MUL:DIM].rearrange("p (m v) -> p m v", m=3),
                                                           scalar=scale, in1=xv, op0=ALU.mult, op1=ALU.add).then_inc(added, 1)

        def place_nodes(chosen, slots, expertI):
            with ExitStack() as st:
                sb, pb = tile_in(st), bank_in(st)
                steps, oh_ready, totals = sems_in(st)("place_steps", "one_hots_ready", "totals_ready")
                wide = [P, TILES, EXPERTS]
                idxF = sb("idxF", [P, TILES])
                oh, before_me = sb("oh", wide), sb("before_me", wide)
                n, grp, gI, start = (sb("n", [P, EXPERTS]), sb("grp", [P, EXPERTS]), sb("gI", [P, EXPERTS], I32),
                                     sb("start", [P, EXPERTS]))
                slotF, ef = sb("slotF", [P, TILES]), sb("ef", [P, TT1])
                ps = pb("ps", [128, 2, 512])
                with nc.Block() as block:
                    @block.vector
                    def _(dve):
                        step = Chain(dve, steps)
                        step(nc.vector.tensor_copy(idxF[:], chosen))
                        nc.vector.tensor_tensor(oh[:], count[:P, 0:EXPERTS].unsqueeze(1).to_broadcast(wide),
                                                idxF[:].unsqueeze(2).to_broadcast(wide), ALU.is_equal).then_inc(oh_ready, 1)
                        dve.wait_ge(totals, 1)
                        step(nc.vector.tensor_copy(before_me[:], ps[:P, 0, 0:TILES * EXPERTS].rearrange("p (t e) -> p t e", t=TILES)))
                        step(nc.vector.memset(n[:], 0.0))
                        for t in range(TILES):
                            step(nc.vector.tensor_tensor(before_me[:, t, :], before_me[:, t, :], n[:], ALU.add))
                            step(nc.vector.tensor_tensor(n[:], n[:], ps[:P, 1, EXPERTS * t:EXPERTS * (t + 1)], ALU.add))
                        step(nc.vector.tensor_scalar(gI[:], n[:], float(LANES - 1), None, ALU.add))
                        step(nc.vector.tensor_scalar(gI[:], gI[:], int(math.log2(LANES)), None, ALU.arith_shift_right))
                        step(nc.vector.tensor_copy(grp[:], gI[:]))
                        step(nc.vector.tensor_tensor_scan(start[:], ones[:P, 0:EXPERTS], grp[:], 0.0, ALU.mult, ALU.add))
                        step(nc.vector.tensor_tensor(start[:], start[:], grp[:], ALU.subtract))
                        step(nc.vector.tensor_scalar(ef[:], count[:P, 0:TT1], start[:, 1:2], None, ALU.is_ge))
                        for e in range(2, EXPERTS):
                            step(nc.vector.scalar_tensor_tensor(out=ef[:], in0=count[:P, 0:TT1], scalar=start[:, e:e + 1], in1=ef[:],
                                                                op0=ALU.is_ge, op1=ALU.add))
                        step(nc.vector.tensor_copy(expertI[:], ef[:]))
                        step(nc.vector.tensor_scalar(start[:], start[:], float(LANES), None, ALU.mult))
                        step(nc.vector.tensor_tensor(before_me[:], before_me[:], start[:].unsqueeze(1).to_broadcast(wide), ALU.add))
                        step(nc.vector.tensor_tensor(before_me[:], before_me[:], oh[:], ALU.mult))
                        step(nc.vector.tensor_reduce(slotF[:], before_me[:], X_AXIS, ALU.add))
                        step(nc.vector.tensor_copy(slots[:, :, 0], slotF[:]))

                    @block.tensor
                    def _(pe):
                        pe.wait_ge(oh_ready, 1)
                        flat = oh[:].rearrange("p t e -> p (t e)")
                        nc.tensor.matmul(ps[:P, 0, 0:TILES * EXPERTS], before[:P, :P], flat, start=True, stop=True)
                        nc.tensor.matmul(ps[:P, 1, 0:TILES * EXPERTS], ones[:P, :P], flat, start=True, stop=True).then_inc(totals, 1)

        def experts1(expertI):
            UNITS = 4
            ITERS = TT1 // 2
            FC = FF1 // 128
            with ExitStack() as st:
                sb, pb = tile_in(st), bank_in(st)
                loaded = sems_in(st)(*[f"unit_loaded{u}" for u in range(UNITS)])
                stored = sems_in(st)(*[f"unit_stored{u}" for u in range(UNITS)])
                b_loaded, b_turned, b_ready, x_turned, x_moved, hid_done, hid_moved, y_done, y_moved, y_free, tick = sems_in(st)(
                    "b_loaded", "b_turned", "b_ready", "x_turned", "x_moved", "hid_done", "hid_moved", "y_done", "y_moved",
                    "y_free", "tick")
                xe = [sb(f"xe{u}", [128, DIM]) for u in range(UNITS)]
                W1 = [sb(f"W1_{u}", [128, KC, FF1]) for u in range(UNITS)]
                W2 = [sb(f"W2_{u}", [128, FC, DIM]) for u in range(UNITS)]
                b2B = [sb(f"b2B{u}", [128, DIM]) for u in range(UNITS)]
                ye = [sb(f"ye{u}", [128, DIM]) for u in range(UNITS)]
                b1raw, b1T = sb("b1raw", [2 * EXPERTS * FC, 128]), sb("b1T", [128, 2 * EXPERTS, FC])
                xT, hid = sb("xT", [128, 2, KC, 128]), sb("hid", [128, 2, FC, 128])
                turn_ps, hid_ps, y_ps = pb("turn_ps", [128, 2, 512]), pb("hid_ps", [128, 2, 512]), pb("y_ps", [128, 2, 512])
                with nc.Block() as block:
                    def expert_of(engine, r, u):
                        b = u % 2
                        return engine.value_load(expertI[b][0:1, bass.ds(2 * r + u // 2, 1)], min_val=0, max_val=EXPERTS - 1)

                    @block.sync
                    def _(sp):
                        for b, bank in enumerate(BANKS):
                            n = EXPERTS * FC
                            sp.dma_start(b1raw[n * b:n * (b + 1), :], I[f"L1_ffn_b1_{bank}"].rearrange("e (m p) -> (e m) p", p=128)
                                         ).then_inc(b_loaded, 16)
                        sp.sem_inc(y_moved, UNITS)
                        with sp.Fori(0, ITERS) as r:
                            for u in range(UNITS):
                                bank = BANKS[u % 2]
                                e = expert_of(sp, r, u)
                                sp.wait_ge(y_moved, UNITS * r + u + 1)
                                sp.sem_inc(tick, 1)
                                sp.dma_start(xe[u][:], xin1[bank][bass.ds((2 * r + u // 2) * LANES, LANES), :]).then_inc(loaded[u], 16)
                                sp.dma_start(W1[u][:], I[f"L1_ffn_W1_{bank}"][bass.ds(e, 1)].rearrange("a (k p) n -> p (a k) n", p=128)
                                             ).then_inc(loaded[u], 16)
                                sp.dma_start(W2[u][:], I[f"L1_ffn_W2_{bank}"][bass.ds(e, 1)].rearrange("a (k p) n -> p (a k) n", p=128)
                                             ).then_inc(loaded[u], 16)
                                sp.dma_start(b2B[u][:], I[f"L1_ffn_b2_{bank}"][bass.ds(e, 1), :].broadcast_to([128, DIM])
                                             ).then_inc(loaded[u], 16)

                    @block.gpsimd
                    def _(pool):
                        with pool.Fori(0, ITERS) as r:
                            for u in range(UNITS):
                                pool.wait_ge(y_moved, UNITS * (r + 1) + u + 1)
                                pool.sem_inc(tick, 1)
                                pool.dma_start(yout1[BANKS[u % 2]][bass.ds((2 * r + u // 2) * LANES, LANES), :], ye[u][:]
                                               ).then_inc(stored[u], 16)
                                pool.wait_ge(stored[u], 16 * (r + 1))
                                pool.sem_inc(y_free, 1)

                    @block.tensor
                    def _(pe):
                        pe.wait_ge(b_loaded, 32)
                        nb = 2 * EXPERTS * FC
                        nc.tensor.transpose(y_ps[:, 0, 0:nb], b1raw[:], ident[:nb, :nb]).then_inc(b_turned, 1)
                        pe.wait_ge(b_ready, 1)

                        def turn(r, u):
                            n = UNITS * r + u
                            pe.wait_ge(loaded[u], 64 * (r + 1))
                            if u >= 2:
                                pe.wait_ge(x_moved, n - 1)
                            for k in range(KC):
                                last = nc.tensor.transpose(turn_ps[:, u % 2, 128 * k:128 * (k + 1)],
                                                           xe[u][:, 128 * k:128 * (k + 1)], ident[:])
                            last.then_inc(x_turned, 1)

                        def up(r, u):
                            n = UNITS * r + u
                            pe.wait_ge(x_moved, n + 1)
                            for m in range(FC):
                                for k in range(KC):
                                    last = nc.tensor.matmul(hid_ps[:, u % 2, 128 * m:128 * (m + 1)], W1[u][:, k, 128 * m:128 * (m + 1)],
                                                            xT[:, u % 2, k, :], start=k == 0, stop=k == KC - 1)
                            last.then_inc(hid_done, 1)

                        def down(r, u):
                            n = UNITS * r + u
                            pe.wait_ge(hid_moved, FC * (n + 1))
                            pe.wait_ge(y_moved, n - 2 + UNITS + 1)
                            for m in range(FC):
                                last = nc.tensor.matmul(y_ps[:, u % 2, :], hid[:, u % 2, m, :], W2[u][:, m, :],
                                                        start=m == 0, stop=m == FC - 1)
                            last.then_inc(y_done, 1)

                        with pe.Fori(0, ITERS) as r:
                            for s in range(UNITS + 2):
                                if s < UNITS:
                                    turn(r, s)
                                if 1 <= s <= UNITS:
                                    up(r, s - 1)
                                if s >= 2:
                                    down(r, s - 2)

                    @block.scalar
                    def _(act):
                        act.wait_ge(b_turned, 1)
                        nc.scalar.activation(b1T[:], y_ps[:, 0, 0:2 * EXPERTS * FC].rearrange("p (e m) -> p e m", m=FC),
                                             ACT.Copy).then_inc(b_ready, 1)
                        act.wait_ge(b_ready, 1)
                        with act.Fori(0, ITERS) as r:
                            for s in range(UNITS + 1):
                                if s < UNITS:
                                    n = UNITS * r + s
                                    act.wait_ge(x_turned, n + 1)
                                    if s >= 2:
                                        act.wait_ge(hid_done, n - 1)
                                    nc.scalar.activation(xT[:, s % 2, :, :], turn_ps[:, s % 2, :].rearrange("p (k n) -> p k n", k=KC),
                                                         ACT.Copy).then_inc(x_moved, 1)
                                if s >= 1:
                                    u = s - 1
                                    n = UNITS * r + u
                                    e = expert_of(act, r, u)
                                    act.wait_ge(hid_done, n + 1)
                                    if u >= 2:
                                        act.wait_ge(y_done, n - 1)
                                    for m in range(FC):
                                        nc.scalar.activation(hid[:, u % 2, m, :], hid_ps[:, u % 2, 128 * m:128 * (m + 1)], ACT.Gelu,
                                                             bias=b1T[:, bass.ds(e + EXPERTS * (u % 2), 1), m:m + 1].rearrange("p a b -> p (a b)")
                                                             ).then_inc(hid_moved, 1)

                    @block.vector
                    def _(dve):
                        dve.sem_inc(y_free, UNITS)
                        with dve.Fori(0, ITERS) as r:
                            for u in range(UNITS):
                                dve.wait_ge(y_done, UNITS * r + u + 1)
                                dve.wait_ge(y_free, UNITS * r + u + 1)
                                nc.vector.tensor_tensor(ye[u][:], y_ps[:, u % 2, :], b2B[u][:], ALU.add).then_inc(y_moved, 1)

        whole_x = I["x"].rearrange("(t p) d -> p t d", p=P)

        with ExitStack() as outer:
            A = tile_in(outer)("A", [P, TILES, DIM])
            with ExitStack() as attention:
                sb1 = tile_in(attention)
                KT, V = sb1("KT", [128, HEADS, NODES], F32R), sb1("V", [P, TILES, DIM])
                with ExitStack() as early:
                    sb2 = tile_in(early)
                    pos, recs = sb2("pos", [P, ECOLS], I32), sb2("recs", [P, ECOLS, REC])
                    order_edges(pos, recs)
                    records = record_scatter(early, pos, recs)
                    HT = sb2("HT", [128, KC, NODES])
                    layer_norm(X, X, turned_to=HT, pool_work=records(0, 3))
                    qkv(HT, KT, V, records(3, ECOLS // 8))
                LA, has = sb1("LA", [P, TILES, NODES]), sb1("has", [P, TILES])
                count_edges(LA, has)
                attend(KT, V, LA, has, A)
            with ExitStack() as post:
                sb1 = tile_in(post)
                (x_loaded,) = sems_in(post)("x_loaded")

                def reload_x(sp):
                    sp.dma_start(X[:], whole_x).then_inc(x_loaded, 16)
                    sp.wait_ge(x_loaded, 16)

                T, R, hT = sb1("T", [128, KC, NODES]), sb1("R", [P, TILES, DIM]), sb1("hT", [128, 2, NODES])
                transpose_all(A, T)
                node_major_product(T, I["L0_gnn_Wo"], KC, R, add=X)
                layer_norm(R, R, I["L0_gnn_ln1_g"], I["L0_gnn_ln1_b"], turned_to=T)
                feature_major_layer(T, I["L0_gnn_W1"], I["L0_gnn_b1"], hT, 2, ACT.Relu, sync_work=reload_x)
                node_major_product(hT, I["L0_gnn_W2"], 2, R, bias=I["L0_gnn_b2"], add=R)
                layer_norm(R, R, I["L0_gnn_ln2_g"], I["L0_gnn_ln2_b"], add_to=X)
        recycle()
        with ExitStack() as moe:
            sb1 = tile_in(moe)
            best, bestI = sb1("best", [P, TILES, 8]), sb1("bestI", [P, TILES, 8], U32)
            weight = sb1("weight", [P, TILES, 2])
            slot_in, slot_out = sb1("slot_in", [P, TILES, 2], I32), sb1("slot_out", [P, TILES, 2], I32)
            weights_of_first, load_first_weights = first_weights(moe)
            with ExitStack() as routing:
                sb2 = tile_in(routing)
                N, NT, probs = sb2("N", [P, TILES, DIM]), sb2("NT", [128, KC, NODES]), sb2("probs", [P, TILES, EXPERTS])
                layer_norm(X, N, turned_to=NT)
                gate(NT, [I["L0_ffn_gate_w"]], True, [I["L0_ffn_gate_b"]], probs, best, bestI)
                place_choices(best, bestI, weight, slot_in, slot_out, load_first_weights)
                scatter_rows(N, slot_in, 2, xin0)
            experts0(weights_of_first)
            combine([(yout0, lambda t, c=c: slot_out[:, t, c:c + 1], lambda t, c=c: weight[:, t, c:c + 1]) for c in range(2)])
        recycle()
        with ExitStack() as graph:
            sb1 = tile_in(graph)
            with ExitStack() as up:
                sb2 = tile_in(up)
                N, NT = sb2("N", [P, TILES, DIM]), sb2("NT", [128, KC, NODES])
                layer_norm(X, N, turned_to=NT, chunks=[lambda t: N[:, t, 0:MUL]] + [lambda t, m=m: N[:, t, MUL + m:DIM:3] for m in range(3)])
                mix_up(NT)
            MSG = sb1("MSG", [P, TILES, 2 * DIM])
            messages(MSG)
            mix_out(MSG)
        with ExitStack() as ffn:
            sb1 = tile_in(ffn)
            best = sb1("best", [P, 2 * TILES, 8])
            slots, experts = [], []
            for b in range(2):
                slots.append(sb1(f"slots{b}", [P, TILES, 1], I32))
                experts.append(sb1(f"expertI{b}", [P, TT1], I32))
            with ExitStack() as routing:
                sb2 = tile_in(routing)
                N, NT, hT = sb2("N", [P, TILES, DIM]), sb2("NT", [128, KC, NODES]), sb2("hT", [128, 2, NODES])
                probs, bestI = sb2("probs", [P, 2 * TILES, EXPERTS]), sb2("bestI", [P, 2 * TILES, 8], U32)
                layer_norm(X, N, turned_to=NT)
                gate(NT, [I["L1_ffn_Wr_" + bank] for bank in BANKS], False, [I["L1_ffn_br_" + bank] for bank in BANKS],
                     probs, best, bestI)
                for b in range(2):
                    place_nodes(bestI[:, b:2 * TILES:2, 0], slots[b], experts[b])
                to_bank = [row_scatter(routing, N, slots[b], 1, xin1[bank]) for b, bank in enumerate(BANKS)]
                feature_major_layer(NT, I["L1_ffn_Ws1"], I["L1_ffn_bs1"], hT, 2, ACT.Gelu, pool_work=to_bank[0])
                node_major_product(hT, I["L1_ffn_Ws2"], 2, X, bias=I["L1_ffn_bs2"], add=X, pool_work=to_bank[1])
            experts1(experts)
            combine([(yout1[bank], lambda t, b=b: slots[b][:, t, 0:1], lambda t, b=b: best[:, 2 * t + b, 0:1])
                     for b, bank in enumerate(BANKS)], result=out)


_INS = ['x', 'src', 'dst', 'edge_attr_4', 'edge_attr_8', 'L0_gnn_Wq', 'L0_gnn_Wk', 'L0_gnn_Wv', 'L0_gnn_Wo',
        'L0_gnn_ln1_g', 'L0_gnn_ln1_b', 'L0_gnn_ln2_g', 'L0_gnn_ln2_b', 'L0_gnn_W1', 'L0_gnn_b1', 'L0_gnn_W2',
        'L0_gnn_b2', 'L0_ffn_gate_w', 'L0_ffn_gate_b', 'L0_ffn_w1', 'L0_ffn_b1', 'L0_ffn_w2', 'L0_ffn_b2',
        'L1_gnn_W_up0', 'L1_gnn_W_up1', 'L1_gnn_W_mlp1', 'L1_gnn_W_mlp2', 'L1_gnn_W_mlp3', 'L1_gnn_W_mlp4',
        'L1_gnn_W_out0', 'L1_gnn_W_out1', 'L1_ffn_Wr_sp', 'L1_ffn_br_sp', 'L1_ffn_Wr_fq', 'L1_ffn_br_fq',
        'L1_ffn_Ws1', 'L1_ffn_bs1', 'L1_ffn_Ws2', 'L1_ffn_bs2', 'L1_ffn_W1_sp', 'L1_ffn_b1_sp', 'L1_ffn_W2_sp',
        'L1_ffn_b2_sp', 'L1_ffn_W1_fq', 'L1_ffn_b1_fq', 'L1_ffn_W2_fq', 'L1_ffn_b2_fq']


def kernel(**inputs):
    import numpy as _np
    import concourse.bacc as _bacc
    from concourse import mybir as _mybir
    from concourse.bass_utils import run_bass_kernel_spmd as _run

    nc = _bacc.Bacc("TRN2", target_bir_lowering=False, num_devices=1)
    arrays, args = {}, {}
    for name in _INS:
        a = _np.ascontiguousarray(inputs[name])
        arrays[f"in_{name}"] = a
        args[name] = nc.dram_tensor(f"in_{name}", a.shape, _mybir.dt.from_np(a.dtype), kind="ExternalInput").ap()
    out = nc.dram_tensor("out_0", (NODES, DIM), F32, kind="ExternalOutput").ap()
    gnn_moe_gnn_moe(nc, args, out)
    return _run(nc, [arrays], core_ids=[0]).results[0]["out_0"]
```
